# Optimizing a Trainium2 kernel written in Bass

```python
import numpy as np
import jax
import jax.numpy as jnp

def _softmax(x, axis=-1):
    return jax.nn.softmax(x, axis=axis)

def _gelu(x):
    return jax.nn.gelu(x, approximate=True)

def _silu(x):
    return jax.nn.silu(x)

def _sigmoid(x):
    return jax.nn.sigmoid(x)

def _layernorm(x, axis=-1, eps=1e-05):
    m = jnp.mean(x, axis=axis, keepdims=True)
    v = jnp.var(x, axis=axis, keepdims=True)
    return (x - m) / jnp.sqrt(v + eps)

def _scatter_add(tgt, idx, src, axis=0):
    return tgt.at[idx].add(src)

def _segment_sum(src, seg, n):
    return jax.ops.segment_sum(src, seg, n)
kernel_name = 'mk_perceiver_d2_seqx_r4_7c45f2'

def setup_inputs(seed: int=0):
    np.random.seed(seed)
    _w = jnp.asarray

    def _rec_inputs():
        import jax
        import jax.numpy as jnp
        _rk = jax.random.key(seed)
        x = -0.000125 + 0.9999 * jax.random.normal(jax.random.fold_in(_rk, 1), (32, 32, 256), jnp.float32)
        _lenS = 32 - jax.random.randint(jax.random.fold_in(_rk, 7), (32,), 0, max(1, 32 // 4) + 1, jnp.int32)
        _lenS2 = 257 - jax.random.randint(jax.random.fold_in(_rk, 8), (32,), 0, max(1, 257 // 4) + 1, jnp.int32)
        _ctx_768P = jax.random.normal(jax.random.fold_in(_rk, 11), (32, 16, 192), jnp.float32)
        _ctx_768c = jax.random.dirichlet(jax.random.fold_in(_rk, 511), 0.3 * jnp.ones((16,), jnp.float32), (32, 257))
        _ctx_768t = jnp.einsum('bsk,bkd->bsd', _ctx_768c, _ctx_768P)
        _ctx_768t = _ctx_768t * jax.lax.rsqrt(jnp.mean(jnp.square(_ctx_768t)) + 1e-12) * 0.953939
        ctx_768 = -5.15168e-05 + 0.999825 * (_ctx_768t + 0.3 * jax.random.normal(jax.random.fold_in(_rk, 611), (32, 257, 192), jnp.float32))
        _validS = jnp.arange(32)[None, :] < _lenS[:, None]
        _validS2 = jnp.arange(257)[None, :] < _lenS2[:, None]
        _causal = jnp.tril(jnp.ones((32, 32), dtype=bool))
        mask_BxS2_bk0 = jnp.logical_not(jnp.broadcast_to(_validS2[:, :], (32, 257)))
        return (x, ctx_768, mask_BxS2_bk0)
    x, ctx_768, mask_BxS2_bk0 = _rec_inputs()

    def _L0_xattn_setup():
        import jax, jax.numpy as jnp
        import numpy as np
        Q_DIM, K_DIM, V_DIM, OUT_DIM = (256, 192, 192, 256)
        key = jax.random.key(seed)
        ks = jax.random.split(key, 9)
        s = lambda d: 1.0 / np.sqrt(d)
        return {'query': jax.random.normal(ks[0], (16, 512, Q_DIM), jnp.float32), 'key': jax.random.normal(ks[1], (16, 512, K_DIM), jnp.float32), 'value': jax.random.normal(ks[2], (16, 512, V_DIM), jnp.float32), 'Wq': jax.random.uniform(ks[3], (OUT_DIM, Q_DIM), jnp.float32, -s(Q_DIM), s(Q_DIM)), 'bq': jax.random.uniform(ks[4], (OUT_DIM,), jnp.float32, -s(Q_DIM), s(Q_DIM)), 'Wk': jax.random.uniform(ks[5], (OUT_DIM, K_DIM), jnp.float32, -s(K_DIM), s(K_DIM)), 'bk': jax.random.uniform(ks[6], (OUT_DIM,), jnp.float32, -s(K_DIM), s(K_DIM)), 'Wv': jax.random.uniform(ks[7], (OUT_DIM, V_DIM), jnp.float32, -s(V_DIM), s(V_DIM)), 'bv': jax.random.uniform(ks[8], (OUT_DIM,), jnp.float32, -s(V_DIM), s(V_DIM))}
    _L0_xattn_all = _L0_xattn_setup()
    _L0_xattn_in = {k: v for k, v in _L0_xattn_all.items() if k in ('Wq', 'bq', 'Wk', 'bk', 'Wv', 'bv')}
    del _L0_xattn_all

    def _L0_attn_setup():
        import jax, jax.numpy as jnp
        import numpy as np
        NUM_HEADS = 16
        EPS = 1e-06
        L2_EPS = 1e-12

        def _l2_normalize(x):
            n = jnp.linalg.norm(x, axis=-1, keepdims=True)
            return x / jnp.maximum(n, L2_EPS)
        key = jax.random.key(seed)
        k1, k2 = jax.random.split(key)
        x = jax.random.normal(k1, (2, 2048, 256), dtype=jnp.float32)
        W_qkv = jax.random.normal(k2, (768, 256), dtype=jnp.float32) * 0.02
        return {'x': x, 'W_qkv': W_qkv}
    _L0_attn_all = _L0_attn_setup()
    _L0_attn_in = {k: v for k, v in _L0_attn_all.items() if k in ('W_qkv',)}
    del _L0_attn_all

    def _L0_ffn_setup():
        import jax, jax.numpy as jnp
        import numpy as np
        E = 16
        H = 256
        F = 512
        TOP_K = 1
        B, S = (2, 256)
        key = jax.random.key(seed)
        ks = jax.random.split(key, 7)
        s = 0.02
        return {'hidden_states': jax.random.normal(ks[0], (B, S, H), jnp.float32), 'w_router': jax.random.normal(ks[1], (E, H), jnp.float32) * s, 'gate_up_proj': jax.random.normal(ks[2], (E, H, 2 * F), jnp.float32) * s, 'down_proj': jax.random.normal(ks[3], (E, F, H), jnp.float32) * s, 'w_gate': jax.random.normal(ks[4], (F, H), jnp.float32) * s, 'w_up': jax.random.normal(ks[5], (F, H), jnp.float32) * s, 'w_down': jax.random.normal(ks[6], (H, F), jnp.float32) * s}
    _L0_ffn_all = _L0_ffn_setup()
    _L0_ffn_in = {k: v for k, v in _L0_ffn_all.items() if k in ('w_router', 'gate_up_proj', 'down_proj', 'w_gate', 'w_up', 'w_down')}
    del _L0_ffn_all

    def _L1_xattn_setup():
        import jax, jax.numpy as jnp
        import numpy as np
        HEADS = 8
        DIM_HEAD = 64
        QUERY_DIM = 256
        CONTEXT_DIM = 192
        INNER = HEADS * DIM_HEAD
        key = jax.random.key(seed)
        ks = jax.random.split(key, 8)
        b, n, j = (4, 512, 512)
        x = jax.random.normal(ks[0], (b, n, QUERY_DIM), dtype=jnp.float32)
        context = jax.random.normal(ks[1], (b, j, CONTEXT_DIM), dtype=jnp.float32)
        mask = jax.random.randint(ks[2], (b, j), 0, 2).astype(jnp.bool_)
        W_q = jax.random.normal(ks[3], (QUERY_DIM, INNER), dtype=jnp.float32) / np.sqrt(QUERY_DIM)
        W_k = jax.random.normal(ks[4], (CONTEXT_DIM, INNER), dtype=jnp.float32) / np.sqrt(CONTEXT_DIM)
        W_v = jax.random.normal(ks[5], (CONTEXT_DIM, INNER), dtype=jnp.float32) / np.sqrt(CONTEXT_DIM)
        W_o = jax.random.normal(ks[6], (INNER, QUERY_DIM), dtype=jnp.float32) / np.sqrt(INNER)
        b_o = jax.random.normal(ks[7], (QUERY_DIM,), dtype=jnp.float32) * 0.01
        return {'x': x, 'context': context, 'mask': mask, 'W_q': W_q, 'W_k': W_k, 'W_v': W_v, 'W_o': W_o, 'b_o': b_o}
    _L1_xattn_all = _L1_xattn_setup()
    _L1_xattn_in = {k: v for k, v in _L1_xattn_all.items() if k in ('W_q', 'W_k', 'W_v', 'W_o', 'b_o')}
    del _L1_xattn_all

    def _L1_attn_setup():
        import jax, jax.numpy as jnp
        import numpy as np
        D_MODEL, D_STATE, EXPAND, D_CONV, HEADDIM = (256, 128, 2, 4, 64)
        D_INNER = EXPAND * D_MODEL
        NHEADS = D_INNER // HEADDIM
        NGROUPS = 1
        CONV_DIM = D_INNER + 2 * NGROUPS * D_STATE
        D_IN_PROJ = 2 * D_INNER + 2 * NGROUPS * D_STATE + NHEADS
        BATCH, SEQ = (2, 1024)
        EPS = 1e-05

        def _mamba2(u, in_proj_w, conv_w, conv_b, dt_bias, A_log, Dp, norm_w, out_proj_w):
            b, l, _ = u.shape
            zxbcdt = u @ in_proj_w.T
            z, xBC, dt = jnp.split(zxbcdt, [D_INNER, D_INNER + CONV_DIM], axis=-1)
            xBC = jnp.transpose(xBC, (0, 2, 1))
            xBC = jax.lax.conv_general_dilated(xBC, conv_w[:, None, :], window_strides=(1,), padding=[(D_CONV - 1, 0)], feature_group_count=CONV_DIM, dimension_numbers=('NCH', 'OIH', 'NCH'))
            xBC = jax.nn.silu(jnp.transpose(xBC, (0, 2, 1)) + conv_b)
            x, Bm, Cm = jnp.split(xBC, [D_INNER, D_INNER + NGROUPS * D_STATE], axis=-1)
            dt = jax.nn.softplus(dt + dt_bias)
            A = -jnp.exp(A_log)
            xh = x.reshape(b, l, NHEADS, HEADDIM)
            dt_t, x_t = (jnp.moveaxis(dt, 1, 0), jnp.moveaxis(xh, 1, 0))
            B_t, C_t = (jnp.moveaxis(Bm, 1, 0), jnp.moveaxis(Cm, 1, 0))

            def step(h, inputs):
                dtk, xk, Bk, Ck = inputs
                decay = jnp.exp(dtk * A)
                h = h * decay[:, :, None, None] + dtk[:, :, None, None] * xk[..., None] * Bk[:, None, None, :]
                y = jnp.einsum('bhpn,bn->bhp', h, Ck)
                return (h, y)
            h0 = jnp.zeros((b, NHEADS, HEADDIM, D_STATE), u.dtype)
            _, ys = jax.lax.scan(step, h0, (dt_t, x_t, B_t, C_t))
            y = jnp.moveaxis(ys, 0, 1) + Dp[None, None, :, None] * xh
            y = y.reshape(b, l, D_INNER)
            y = y * jax.nn.silu(z)
            y = y * jax.lax.rsqrt(jnp.mean(y * y, axis=-1, keepdims=True) + EPS) * norm_w
            return y @ out_proj_w.T
        key = jax.random.key(seed)
        ks = jax.random.split(key, 6)
        sn = lambda k, shape, sc: jax.random.normal(k, shape, jnp.float32) * sc
        dt = jnp.linspace(0.001, 0.1, NHEADS)
        return {'x': sn(ks[0], (BATCH, SEQ, D_MODEL), 1.0), 'ln_w': jnp.ones((D_MODEL,), jnp.float32), 'ln_b': jnp.zeros((D_MODEL,), jnp.float32), 'in_proj_w': sn(ks[1], (D_IN_PROJ, D_MODEL), D_MODEL ** (-0.5)), 'conv_w': sn(ks[2], (CONV_DIM, D_CONV), D_CONV ** (-0.5)), 'conv_b': jnp.zeros((CONV_DIM,), jnp.float32), 'dt_bias': jnp.log(jnp.expm1(dt)).astype(jnp.float32), 'A_log': jnp.log(jnp.arange(1, NHEADS + 1, dtype=jnp.float32)), 'D': jnp.ones((NHEADS,), jnp.float32), 'norm_w': jnp.ones((D_INNER,), jnp.float32), 'out_proj_w': sn(ks[3], (D_MODEL, D_INNER), D_INNER ** (-0.5))}
    _L1_attn_all = _L1_attn_setup()
    _L1_attn_in = {k: v for k, v in _L1_attn_all.items() if k in ('ln_w', 'ln_b', 'in_proj_w', 'conv_w', 'conv_b', 'dt_bias', 'A_log', 'D', 'norm_w', 'out_proj_w')}
    del _L1_attn_all

    def _L1_ffn_setup():
        import jax, jax.numpy as jnp
        import numpy as np
        DIM = 256
        HIDDEN = 768
        SCALE = 1.0 / 127.0

        def _dequant(w_int, dtype):
            return w_int.astype(dtype) * jnp.asarray(SCALE, dtype)
        key = jax.random.key(seed)
        k_x, k_g, k_u, k_d = jax.random.split(key, 4)
        x = jax.random.normal(k_x, (4, 512, DIM), dtype=jnp.float32)
        w_gate = jax.random.randint(k_g, (HIDDEN, DIM), -127, 128, dtype=jnp.int32)
        w_up = jax.random.randint(k_u, (HIDDEN, DIM), -127, 128, dtype=jnp.int32)
        w_down = jax.random.randint(k_d, (DIM, HIDDEN), -127, 128, dtype=jnp.int32)
        return {'x': x, 'w_gate': w_gate, 'w_up': w_up, 'w_down': w_down}
    _L1_ffn_all = _L1_ffn_setup()
    _L1_ffn_in = {k: v for k, v in _L1_ffn_all.items() if k in ('w_gate', 'w_up', 'w_down')}
    del _L1_ffn_all
    return {'x': x, 'ctx_768': ctx_768, 'mask_BxS2_bk0': mask_BxS2_bk0, 'L0_xattn_Wq': _L0_xattn_in['Wq'], 'L0_xattn_bq': _L0_xattn_in['bq'], 'L0_xattn_Wk': _L0_xattn_in['Wk'], 'L0_xattn_bk': _L0_xattn_in['bk'], 'L0_xattn_Wv': _L0_xattn_in['Wv'], 'L0_xattn_bv': _L0_xattn_in['bv'], 'L0_attn_W_qkv': _L0_attn_in['W_qkv'], 'L0_ffn_w_router': _L0_ffn_in['w_router'], 'L0_ffn_gate_up_proj': _L0_ffn_in['gate_up_proj'], 'L0_ffn_down_proj': _L0_ffn_in['down_proj'], 'L0_ffn_w_gate': _L0_ffn_in['w_gate'], 'L0_ffn_w_up': _L0_ffn_in['w_up'], 'L0_ffn_w_down': _L0_ffn_in['w_down'], 'L1_xattn_W_q': _L1_xattn_in['W_q'], 'L1_xattn_W_k': _L1_xattn_in['W_k'], 'L1_xattn_W_v': _L1_xattn_in['W_v'], 'L1_xattn_W_o': _L1_xattn_in['W_o'], 'L1_xattn_b_o': _L1_xattn_in['b_o'], 'L1_attn_ln_w': _L1_attn_in['ln_w'], 'L1_attn_ln_b': _L1_attn_in['ln_b'], 'L1_attn_in_proj_w': _L1_attn_in['in_proj_w'], 'L1_attn_conv_w': _L1_attn_in['conv_w'], 'L1_attn_conv_b': _L1_attn_in['conv_b'], 'L1_attn_dt_bias': _L1_attn_in['dt_bias'], 'L1_attn_A_log': _L1_attn_in['A_log'], 'L1_attn_D': _L1_attn_in['D'], 'L1_attn_norm_w': _L1_attn_in['norm_w'], 'L1_attn_out_proj_w': _L1_attn_in['out_proj_w'], 'L1_ffn_w_gate': _L1_ffn_in['w_gate'], 'L1_ffn_w_up': _L1_ffn_in['w_up'], 'L1_ffn_w_down': _L1_ffn_in['w_down']}

def reference(x, ctx_768, mask_BxS2_bk0, L0_xattn_Wq, L0_xattn_bq, L0_xattn_Wk, L0_xattn_bk, L0_xattn_Wv, L0_xattn_bv, L0_attn_W_qkv, L0_ffn_w_router, L0_ffn_gate_up_proj, L0_ffn_down_proj, L0_ffn_w_gate, L0_ffn_w_up, L0_ffn_w_down, L1_xattn_W_q, L1_xattn_W_k, L1_xattn_W_v, L1_xattn_W_o, L1_xattn_b_o, L1_attn_ln_w, L1_attn_ln_b, L1_attn_in_proj_w, L1_attn_conv_w, L1_attn_conv_b, L1_attn_dt_bias, L1_attn_A_log, L1_attn_D, L1_attn_norm_w, L1_attn_out_proj_w, L1_ffn_w_gate, L1_ffn_w_up, L1_ffn_w_down):
    import jax
    import jax.numpy as jnp

    def _L0_xattn_ref(query, key, value, Wq, bq, Wk, bk, Wv, bv):
        import jax, jax.numpy as jnp
        import numpy as np
        Q_DIM, K_DIM, V_DIM, OUT_DIM = (256, 192, 192, 256)
        scale = OUT_DIM ** (-0.5)
        q = jnp.einsum('bsd,od->bso', query, Wq) + bq
        k = jnp.einsum('bsd,od->bso', key, Wk) + bk
        v = jnp.einsum('bsd,od->bso', value, Wv) + bv
        scores = jnp.einsum('bqo,bko->bqk', q, k) * scale
        probs = jax.nn.softmax(scores, axis=-1)
        return jnp.einsum('bqk,bko->bqo', probs, v)

    def _L0_attn_ref(x, W_qkv):
        import jax, jax.numpy as jnp
        import numpy as np
        NUM_HEADS = 16
        EPS = 1e-06
        L2_EPS = 1e-12

        def _l2_normalize(x):
            n = jnp.linalg.norm(x, axis=-1, keepdims=True)
            return x / jnp.maximum(n, L2_EPS)
        b, n, dim = x.shape
        h = NUM_HEADS
        d = dim // h
        scale = d ** (-0.5)
        qkv = x @ W_qkv.T
        q, k, v = jnp.split(qkv, 3, axis=-1)
        to_heads = lambda t: t.reshape(b, n, h, d).transpose(0, 2, 1, 3)
        q, k, v = (to_heads(q), to_heads(k), to_heads(v))
        q = jax.nn.softplus(_l2_normalize(q))
        k = jax.nn.softplus(_l2_normalize(k))
        kv = jnp.einsum('bhnd,bhnc->bhdc', k, v) * scale
        ksum = jnp.sum(k, axis=2) + EPS
        norm = 1.0 / jnp.einsum('bhnd,bhd->bhn', q, ksum)
        out = jnp.einsum('bhnd,bhdc,bhn->bhnc', q, kv, norm)
        return out.transpose(0, 2, 1, 3).reshape(b, n, dim)

    def _L0_ffn_ref(hidden_states, w_router, gate_up_proj, down_proj, w_gate, w_up, w_down):
        import jax, jax.numpy as jnp
        import numpy as np
        E = 16
        H = 256
        F = 512
        TOP_K = 1
        B, S = (2, 256)
        b, s, h = hidden_states.shape
        x = hidden_states.reshape(-1, h)
        logits = x @ w_router.T
        _, top_idx = jax.lax.top_k(logits, TOP_K)
        mask = jax.nn.one_hot(top_idx, E, dtype=logits.dtype).sum(axis=1)
        scores = jax.nn.sigmoid(logits) * mask
        masked_inputs = scores.T[:, :, None] * x[None, :, :]
        gate_up = jnp.einsum('eth,ehf->etf', masked_inputs, gate_up_proj)
        gate, up = jnp.split(gate_up, 2, axis=-1)
        expert_out = jnp.einsum('etf,efh->eth', up * jax.nn.silu(gate), down_proj)
        shared = jax.nn.silu(x @ w_gate.T) * (x @ w_up.T) @ w_down.T
        out = shared + expert_out.sum(axis=0)
        return out.reshape(b, s, h)

    def _L1_xattn_ref(x, context, mask, W_q, W_k, W_v, W_o, b_o):
        import jax, jax.numpy as jnp
        import numpy as np
        HEADS = 8
        DIM_HEAD = 64
        QUERY_DIM = 256
        CONTEXT_DIM = 192
        INNER = HEADS * DIM_HEAD
        b, n, _ = x.shape
        j = context.shape[1]
        scale = DIM_HEAD ** (-0.5)
        q = (x @ W_q).reshape(b, n, HEADS, DIM_HEAD)
        k = (context @ W_k).reshape(b, j, HEADS, DIM_HEAD)
        v = (context @ W_v).reshape(b, j, HEADS, DIM_HEAD)
        sim = jnp.einsum('bihd,bjhd->bhij', q, k) * scale
        max_neg = -jnp.finfo(sim.dtype).max
        sim = jnp.where(mask[:, None, None, :], sim, max_neg)
        attn = jax.nn.softmax(sim, axis=-1)
        out = jnp.einsum('bhij,bjhd->bihd', attn, v).reshape(b, n, INNER)
        return out @ W_o + b_o

    def _L1_attn_ref(x, ln_w, ln_b, in_proj_w, conv_w, conv_b, dt_bias, A_log, D, norm_w, out_proj_w):
        import jax, jax.numpy as jnp
        import numpy as np
        D_MODEL, D_STATE, EXPAND, D_CONV, HEADDIM = (256, 128, 2, 4, 64)
        D_INNER = EXPAND * D_MODEL
        NHEADS = D_INNER // HEADDIM
        NGROUPS = 1
        CONV_DIM = D_INNER + 2 * NGROUPS * D_STATE
        D_IN_PROJ = 2 * D_INNER + 2 * NGROUPS * D_STATE + NHEADS
        BATCH, SEQ = (2, 1024)
        EPS = 1e-05

        def _mamba2(u, in_proj_w, conv_w, conv_b, dt_bias, A_log, Dp, norm_w, out_proj_w):
            b, l, _ = u.shape
            zxbcdt = u @ in_proj_w.T
            z, xBC, dt = jnp.split(zxbcdt, [D_INNER, D_INNER + CONV_DIM], axis=-1)
            xBC = jnp.transpose(xBC, (0, 2, 1))
            xBC = jax.lax.conv_general_dilated(xBC, conv_w[:, None, :], window_strides=(1,), padding=[(D_CONV - 1, 0)], feature_group_count=CONV_DIM, dimension_numbers=('NCH', 'OIH', 'NCH'))
            xBC = jax.nn.silu(jnp.transpose(xBC, (0, 2, 1)) + conv_b)
            x, Bm, Cm = jnp.split(xBC, [D_INNER, D_INNER + NGROUPS * D_STATE], axis=-1)
            dt = jax.nn.softplus(dt + dt_bias)
            A = -jnp.exp(A_log)
            xh = x.reshape(b, l, NHEADS, HEADDIM)
            dt_t, x_t = (jnp.moveaxis(dt, 1, 0), jnp.moveaxis(xh, 1, 0))
            B_t, C_t = (jnp.moveaxis(Bm, 1, 0), jnp.moveaxis(Cm, 1, 0))

            def step(h, inputs):
                dtk, xk, Bk, Ck = inputs
                decay = jnp.exp(dtk * A)
                h = h * decay[:, :, None, None] + dtk[:, :, None, None] * xk[..., None] * Bk[:, None, None, :]
                y = jnp.einsum('bhpn,bn->bhp', h, Ck)
                return (h, y)
            h0 = jnp.zeros((b, NHEADS, HEADDIM, D_STATE), u.dtype)
            _, ys = jax.lax.scan(step, h0, (dt_t, x_t, B_t, C_t))
            y = jnp.moveaxis(ys, 0, 1) + Dp[None, None, :, None] * xh
            y = y.reshape(b, l, D_INNER)
            y = y * jax.nn.silu(z)
            y = y * jax.lax.rsqrt(jnp.mean(y * y, axis=-1, keepdims=True) + EPS) * norm_w
            return y @ out_proj_w.T
        mu = jnp.mean(x, -1, keepdims=True)
        var = jnp.mean((x - mu) ** 2, -1, keepdims=True)
        xn = (x - mu) * jax.lax.rsqrt(var + EPS) * ln_w + ln_b
        return x + _mamba2(xn, in_proj_w, conv_w, conv_b, dt_bias, A_log, D, norm_w, out_proj_w)

    def _L1_ffn_ref(x, w_gate, w_up, w_down):
        import jax, jax.numpy as jnp
        import numpy as np
        DIM = 256
        HIDDEN = 768
        SCALE = 1.0 / 127.0

        def _dequant(w_int, dtype):
            return w_int.astype(dtype) * jnp.asarray(SCALE, dtype)
        wg = _dequant(w_gate, x.dtype)
        wu = _dequant(w_up, x.dtype)
        wd = _dequant(w_down, x.dtype)
        gate = jnp.einsum('bsd,hd->bsh', x, wg)
        up = jnp.einsum('bsd,hd->bsh', x, wu)
        h = jax.nn.silu(gate) * up
        return jnp.einsum('bsh,dh->bsd', h, wd)
    x = x + _L0_xattn_ref(_layernorm(x, axis=-1), ctx_768, ctx_768, L0_xattn_Wq, L0_xattn_bq, L0_xattn_Wk, L0_xattn_bk, L0_xattn_Wv, L0_xattn_bv)
    x = x + _L0_attn_ref(_layernorm(x, axis=-1), L0_attn_W_qkv)
    x = x + _L0_ffn_ref(_layernorm(x, axis=-1), L0_ffn_w_router, L0_ffn_gate_up_proj, L0_ffn_down_proj, L0_ffn_w_gate, L0_ffn_w_up, L0_ffn_w_down)
    x = x + _L1_xattn_ref(_layernorm(x, axis=-1), ctx_768, mask_BxS2_bk0, L1_xattn_W_q, L1_xattn_W_k, L1_xattn_W_v, L1_xattn_W_o, L1_xattn_b_o)
    x = x + _L1_attn_ref(_layernorm(x, axis=-1), L1_attn_ln_w, L1_attn_ln_b, L1_attn_in_proj_w, L1_attn_conv_w, L1_attn_conv_b, L1_attn_dt_bias, L1_attn_A_log, L1_attn_D, L1_attn_norm_w, L1_attn_out_proj_w)
    x = x + _L1_ffn_ref(_layernorm(x, axis=-1), L1_ffn_w_gate, L1_ffn_w_up, L1_ffn_w_down)
    return x

_drawn_inputs = setup_inputs


def setup_inputs(seed=0):
    import zlib

    import numpy as np

    out = dict(_drawn_inputs(seed))
    spreads = {'L1_attn_ln_w': (1.0, 0.2),
     'L1_attn_ln_b': (0.0, 0.1),
     'L1_attn_conv_b': (0.0, 0.1),
     'L1_attn_D': (1.0, 0.2),
     'L1_attn_norm_w': (1.0, 0.2)}
    factors = {'L0_xattn_bq': 8.0,
     'L0_xattn_bk': 64.0,
     'L0_ffn_w_router': 4.39,
     'L0_ffn_gate_up_proj': 4.142,
     'L0_ffn_down_proj': 4.147,
     'L1_xattn_b_o': 4.233,
     'L0_ffn_w_gate': 3.191,
     'L0_ffn_w_up': 3.158,
     'L0_ffn_w_down': 3.142}
    for name, (base, spread) in spreads.items():
        noise = np.random.default_rng([zlib.crc32(name.encode()), seed]).standard_normal(out[name].shape)
        drawn = base * np.exp(spread * noise) if base else spread * noise
        out[name] = jnp.asarray(drawn.astype(out[name].dtype))
    for name, factor in factors.items():
        out[name] = (out[name] * factor).astype(out[name].dtype)
    return out
```

```python
import concourse.bass as bass
from concourse import mybir
from contextlib import ExitStack
import numpy as np

ORDER = {
    "setup_vector": """
        ones0 ones1 ones_n0 ones_l0 ones_n1 ones_l1 zero negmask""",
    "attn0_tensor": """
        trA q qk sc_0 sc_1 pt_0 pt_1 ov_0 ov_1 ot_0 ot_1 wv_0 wv_1 trB qkv_0 qkv_1 ks_0 kv_0_0 kv_0_1 qt_0 ks_1
        kv_1_0 kv_1_1 qt_1 at_0 at_1 trC lg""",
    "attn0_scalar": """
        xnT_A q_bias0 q_bias1 qk_evac0 qk_evac1 exp0 exp1 oT_evac0_0 oT_evac1_0 oT_evac0_1 oT_evac1_1 xnT_B square0
        vblk0_0 vblk0_1 vblk0_2 vblk0_3 square1 vblk1_0 vblk1_1 vblk1_2 vblk1_3 sp_exp0 sp_exp1 softplus0 softplus1
        qt_evac0 qt_evac1 xnT_C gate_exp""",
    "attn0_vector": """
        lnA_stats0 lnA_stats1 lnA_mean0 lnA_mean1 lnA_var lnA_norm0 lnA_norm1 row_max0 row_max1 pT_evac0 pT_evac1
        rsum ov_evac0 ov_evac1 x_attn0 x_attn1 lnB_stats0 lnB_stats1 lnB_mean0 lnB_mean1 lnB_var lnB_norm0 lnB_norm1
        ss0 ss1 ss_max unit0 unit1 den_mul0 kv_evac0_0 kv_evac0_1 den0 den_mul1 kv_evac1_0 kv_evac1_1 den1 rden
        at_norm0 at_norm1 x_lin0 x_lin1 lnC_stats0 lnC_stats1 lnC_mean0 lnC_mean1 lnC_var lnC_norm0 lnC_norm1 logits
        top0 top1 argmax0 argmax1 arg_f gate_1p gate eidx onehot0 onehot1 xm0 xm1""",
    "attn0_gpsimd": """
        lnA_rstd lnB_rstd rnorm lnC_rstd xnT_all""",
    "routing_vector": """
        rank_oh over7 rank novf q7 oend q obase e7 base_oh etab_sum base etab_min etab_n t1 etab past t2 t3 tile
        slot1 slot2 slot""",
    "shared_tensor": """
        rank count gu0 gu1 gu2 gu3 gu4 gu5 gu6 gu7 down0 down1 down2 down3 down4 down5 down6 down7""",
    "shared_scalar": """
        silu0 silu1 silu2 silu3 silu4 silu5 silu6 silu7""",
    "shared_vector": """
        h0 h1 h2 h3 h4 h5 h6 h7 x0 x1 x2 x3 x4 x5 x6 x7""",
    "experts_tensor": """
        xt0 gu0 xt1 gu1 dn0 xt2 gu2 dn1 xt3 gu3 dn2 dn3""",
    "experts_scalar": """
        xT0 silu0 xT1 silu1 xT2 silu2 xT3 silu3""",
    "experts_vector": """
        h0 y0 h1 y1 h2 y2 h3 y3""",
    "overflow_tensor": """
        xt gu dn""",
    "overflow_scalar": """
        xT silu""",
    "overflow_vector": """
        h y""",
    "x_experts_vector": """
        x0 x1 x2 x3 x4 x5 x6 x7""",
    "attn1_tensor": """
        tr q0 q1 qk0 qk1 qk2 qk3 qk4 qk5 qk6 qk7 sc0 sc1 sc2 pt0 sc3 pt1 ov0 sc4 pt2 ov1 opT0 sc5 pt3 ov2 opT1 sc6
        pt4 ov3 opT2 sc7 pt5 ov4 opT3 sc8 pt6 ov5 opT4 sc9 pt7 ov6 opT5 sc10 pt8 ov7 opT6 sc11 pt9 ov8 opT7 sc12
        pt10 ov9 opT8 sc13 pt11 ov10 opT9 sc14 pt12 ov11 opT10 sc15 pt13 ov12 opT11 pt14 ov13 opT12 pt15 ov14 opT13
        ov15 opT14 opT15 o0 o1 ot0 ot1 wo0 wo1""",
    "attn1_scalar": """
        xnT q_evac0 q_evac1 qk_evac0 qk_evac1 qk_evac2 qk_evac3 qk_evac4 qk_evac5 qk_evac6 qk_evac7 exp0 exp1 exp2
        pT_evac0 exp3 pT_evac1 exp4 pT_evac2 exp5 pT_evac3 exp6 pT_evac4 exp7 pT_evac5 exp8 pT_evac6 exp9 pT_evac7
        exp10 pT_evac8 exp11 pT_evac9 exp12 pT_evac10 exp13 pT_evac11 exp14 pT_evac12 exp15 pT_evac13 pT_evac14
        pT_evac15 o_evac0 o_evac1 ot_evac0 ot_evac1""",
    "attn1_vector": """
        ln_stats0 ln_stats1 ln_mean0 ln_mean1 ln_var ln_norm0 ln_norm1 qk_evac0 qk_evac1 qk_evac2 qk_evac3 qk_evac4
        qk_evac5 qk_evac6 qk_evac7 row_max0 row_max1 rsum0 norm0 row_max2 rsum1 norm1 row_max3 rsum2 norm2 ov_evac0
        row_max4 rsum3 norm3 ov_evac1 opT_evac0 row_max5 rsum4 norm4 ov_evac2 opT_evac1 row_max6 rsum5 norm5
        ov_evac3 opT_evac2 row_max7 rsum6 norm6 ov_evac4 opT_evac3 row_max8 rsum7 norm7 ov_evac5 opT_evac4 row_max9
        rsum8 norm8 ov_evac6 opT_evac5 row_max10 rsum9 norm9 ov_evac7 opT_evac6 row_max11 rsum10 norm10 ov_evac8
        opT_evac7 row_max12 rsum11 norm11 ov_evac9 opT_evac8 row_max13 rsum12 norm12 ov_evac10 opT_evac9 row_max14
        rsum13 norm13 ov_evac11 opT_evac10 row_max15 rsum14 norm14 ov_evac12 opT_evac11 rsum15 norm15 ov_evac13
        opT_evac12 ov_evac14 opT_evac13 ov_evac15 opT_evac14 opT_evac15 bias0 bias1 x0 x1""",
    "attn1_gpsimd": """
        ln_rstd""",
    "attn1_setup_vector": """
        op_zero0 op_zero1 rows_one row_zero""",
    "scan_tensor": """
        tr dt xbc2 xbc0 xbc1 z0 z1 cum cumT0 G0 G1 xs0 xs1 cumT1 y0 y1 yT0 yT1 out0 out1""",
    "scan_scalar": """
        uT xp2 tap3_4 tap3_5 xp0 tap3_0 tap3_1 xp1 tap3_2 tap3_3 dt_exp z_tanh0 z_tanh1 tanh2 tanh0 tanh1 relu0_0
        relu0_1 relu0_2 relu0_3 relu0_4 relu0_5 relu0_6 relu0_7 decay0 relu1_0 relu1_1 relu1_2 relu1_3 relu1_4
        relu1_5 relu1_6 relu1_7 decay1 xs_evac0 xs_evac1 square0 square1 yT_evac0 yT_evac1""",
    "scan_vector": """
        ln1_stats0 ln1_stats1 ln1_mean0 ln1_mean1 ln1_var ln1_norm0 ln1_norm1 ln2_stats0 ln2_stats1 ln2_mean0
        ln2_mean1 ln2_var ln2_norm0 ln2_norm1 ln_w u dt_raw dt_abs dt_pos tap0_4 tap0_5 tap1_4 tap1_5 tap2_4 tap2_5
        dt_2e dt_r dt_s dt_s2 dt_p15 dt_p13 dt_p11 dt_p9 dt_p7 dt_p5 dt_p3 dt_p1 dt dtA tap0_0 tap0_1 tap1_0 tap1_1
        tap2_0 tap2_1 tap0_2 tap0_3 tap1_2 tap1_3 tap2_2 tap2_3 silu2 cum silu0 silu1 z_silu0 z_silu1 gm0 gm1 M0 M1
        xdt0 xdt1 ya0 ya1 yz0 yz1 xr0 xr1 mean_square x0 x1""",
    "scan_gpsimd": """
        ln1_rstd ln2_rstd xD0 xD1 rms""",
    "scan_setup_vector": """
        pad nw0 nw1 nw2 nw3 D A""",
    "scan_setup_scalar": """
        expA""",
    "ffn_tensor": """
        tr g0 u0 g1 u1 g2 u2 down0 down1""",
    "ffn_scalar": """
        xnT silu0 silu1 silu2""",
    "ffn_vector": """
        ln_stats0 ln_stats1 ln_mean0 ln_mean1 ln_var ln_norm0 ln_norm1 h0 h1 h2 x0 x1""",
    "ffn_gpsimd": """
        ln_rstd""",
    "ffn_weights_float": """
        int0 int1 int2""",
}
ORDER = {k: v.split() for k, v in ORDER.items()}

P = 128
B, S, D = 32, 32, 256
TOK = B * S
NT = TOK // P
BT = P // S
KEYS, DC = 257, 192
DC2 = DC - P
NPAIR = NT // 2
PW = 2 * P
H0, HD0 = 16, 16
E, F0 = 16, 512
RING = 4
NOVF = (TOK - 1) // P
H1, HD1 = 8, 64
INNER = H1 * HD1
HM, HDM, NST = 8, 64, 128
DIN = HM * HDM
TAPS = 4
NCH = (DIN + 2 * NST) // P
F1 = 768
MASKED = -(2.0 ** 127)


class Steps:

    def __init__(self, name, sem):
        self.key, self.sem, self.n = name, sem, 0
        self.known = ORDER.get(name)
        self.names = list(self.known or [])

    def done(self, name):
        if self.known:
            assert self.names[self.n % len(self.names)] == name, (self.key, name, self.names[self.n % len(self.names)])
        else:
            self.names.append(name)
        self.n += 1
        return self.sem

    def after(self, name, rnd=0):
        if not self.known:
            return self.sem, 1
        return self.sem, (rnd + 1) * len(self.names) + (self.names.index(name) + 1)

    def sem_value(self, name):
        return self.sem, (self.names.index(name) + 1 if self.known else 1)

    def all(self, rounds=1):
        return self.sem, (rounds + 1) * max(len(self.names), 1)

    def round(self):
        return max(len(self.names), 1)


def host_constants():
    s = np.arange(P)
    same = (s[:, None] // S) == (s[None, :] // S)
    parts = {
        "ident": np.eye(P),
        "tri": same & (s[:, None] <= s[None, :]),
        "gmask": (same & (s[:, None] <= s[None, :])) / 16.0,
        "same": same,
        "before": s[:, None] < s[None, :],
        "hmask": ((s[:, None] // HD0) == (s[None, :] // HD0)) * HD0 ** -0.5,
        "ones": np.ones((P, P)),
        "inb": (s[:, None] // S) == np.arange(BT)[None, :],
        "iota": np.tile(np.arange(E), (P, 1)),
        "caps": np.tile(P * np.arange(1, NT), (P, 1)),
        "nth": np.tile(np.arange(NOVF), (P, 1)),
        "mhalf": np.full((P, 64), -0.5),
        "zeros": np.zeros((P, E)),
    }
    at, cols = {}, 0
    for k, v in parts.items():
        at[k] = (cols, v.shape[1])
        cols += v.shape[1]
    return np.concatenate([np.asarray(v, np.float32) for v in parts.values()], 1), at


def perceiver_kernel(nc, I, out):
    fp32, i32, u32, u8 = mybir.dt.float32, mybir.dt.int32, mybir.dt.uint32, mybir.dt.uint8
    ALU, ACT, AX = mybir.AluOpType, mybir.ActivationFunctionType, mybir.AxisListType.X
    _, CONST = host_constants()
    ctx = ExitStack()
    with ctx:
        big = ctx.enter_context(nc.sbuf_tensor("big", [P, SBUF_COLS], fp32))
        ps = ctx.enter_context(nc.psum_tensor("ps", [P, 8, 512], fp32))
        high = [0]

        def region(start):
            at = [start]

            def take(*dims):
                n = int(np.prod(dims))
                v = big[:, at[0]:at[0] + n]
                at[0] += n + (n & 1)
                high[0] = max(high[0], at[0])
                if len(dims) == 2:
                    v = v.rearrange("p (a b) -> p a b", b=dims[1])
                elif len(dims) == 3:
                    v = v.rearrange("p (a b c) -> p a b c", b=dims[1], c=dims[2])
                elif len(dims) == 4:
                    v = v.rearrange("p (a b c d) -> p a b c d", b=dims[1], c=dims[2], d=dims[3])
                return v
            return take, at

        keep, at = region(0)
        x = keep(NT, D)
        const = keep(CONST["zeros"][0] + CONST["zeros"][1])
        K = {k: const[:, a:a + n] for k, (a, n) in CONST.items()}
        ident = K["ident"]
        st, mv, ve, rstd = keep(2, 6), keep(2, 2), keep(2), keep(2)
        idx_f, oneh, eidx = keep(2), keep(NT, E), keep(NT)
        negmask, zrow = keep(KEYS), keep(D)
        etab = keep(NOVF + 1)
        mask8 = keep(66)
        cT1 = [keep(BT, KEYS) for _ in range(2)]
        cT2 = [keep(BT, KEYS) for _ in range(2)]
        cN = [keep(BT, 2, DC + 1) for _ in range(2)]
        cLq = [keep(DC + 1) for _ in range(2)]
        cLb = [keep(BT, DC) for _ in range(2)]
        w0 = at[0]
        wts, at = region(w0)
        wq, bq, wk, wv1, wv2 = wts(2, D), wts(2), wts(2, DC + 1), wts(D), wts(D)
        wqkv, wr = wts(2, 3 * D), wts(2, E)
        sg_w, su_w, sd_w = wts(2, F0), wts(2, F0), wts(4, D)
        w1 = at[0]
        ring_gu = [wts(2, 2 * F0) for _ in range(RING)]
        ring_dn = [wts(4, D) for _ in range(RING)]
        w2 = at[0]
        w4, at4 = region(w0)
        m_in, m_out = w4(2, 2 * DIN + 2 * NST + HM), w4(4, D)
        m_lnw, m_lnb, m_D, m_conv, m_cb = w4(D), w4(D), w4(HM), w4(NCH, TAPS), w4(NCH)
        m_nw, m_dtb, m_A = w4(4), w4(HM), w4(HM)
        assert at4[0] <= w1, (at4[0], w1)
        w5, at5 = region(w1)
        f_gi, f_ui, f_di = w5(2, F1), w5(2, F1), w5(6, D)
        f_g, f_u, f_d = w5(2, F1), w5(2, F1), w5(6, D)
        assert at5[0] <= w2, (at5[0], w2)
        w3, at = region(w2)
        c_wq, c_wk, c_wv, c_wo, c_bo = w3(2, INNER), w3(H1, DC), w3(2, INNER), w3(4, D), w3(D)
        work0 = at[0]
        a12, at = region(work0)
        xm, xnT_all = a12(NT, D), a12(2, TOK)
        work1 = at[0]
        a1, _ = region(work1)
        xn = [a1(D) for _ in range(2)]
        xnT, qT, qpT = a1(2, PW), a1(2, PW), a1(2, PW)
        pr = [a1(KEYS) for _ in range(2)]
        nmx, sm, ri = a1(2), a1(2), a1(2)
        pT = [a1(2, P) for _ in range(2)]
        op = [a1(DC + 1) for _ in range(2)]
        oT = [a1(2, P) for _ in range(2)]
        sq = [a1(32, 16) for _ in range(2)]
        ss, rn = a1(2, 32), a1(2, 32)
        fqk = [a1(512) for _ in range(2)]
        vblk = [a1(2, BT, P) for _ in range(2)]
        kvm = [a1(2, BT, P) for _ in range(2)]
        dtmp = [a1(16, 16) for _ in range(2)]
        den = a1(2, 16)
        qtT = [a1(2, P) for _ in range(2)]
        lg, m8, mi = a1(2, 16), a1(2, 8), a1(2, 8)
        sc_e, score = a1(2), a1(2)

        a2, _ = region(work1)
        hs = a2(4, TOK)
        sgate = [a2(F0) for _ in range(2)]
        xg = [a2(D) for _ in range(RING)]
        xgT = [a2(2, P) for _ in range(2)]
        egate = [a2(4, P) for _ in range(2)]
        eh = [a2(4, P) for _ in range(2)]
        ey = [a2(D) for _ in range(RING)]
        r_oh, rank, cnt7, novf, oend, obase = a2(NT, E), a2(NT), a2(E, NT - 1), a2(E), a2(E), a2(E)
        r_q7, rq, r_bt, r_g, r_t, slot_f, slot_i = a2(NT, NT - 1), a2(NT), a2(NT), a2(NT), a2(NT), a2(NT), a2(NT)
        r_e7, etab_f = a2(NOVF, E), a2(NOVF + 1)
        yg = xm

        a3, _ = region(work0)
        xn3 = [a3(D) for _ in range(2)]
        xnT3, q3 = a3(2, PW), a3(4, PW)
        qp3 = a3(2, 2 * BT, H1 * S)
        pr3 = [a3(KEYS) for _ in range(4)]
        nmx3, sm3, rs3 = a3(4), a3(4), a3(4)
        pT3 = [a3(2, P) for _ in range(2)]
        op3 = [a3(2 * P) for _ in range(2)]
        oT3 = [a3(2, H1, BT, S) for _ in range(2)]
        o3 = [a3(INNER) for _ in range(2)]
        o3T = [a3(4, P) for _ in range(2)]
        t3 = [a3(D) for _ in range(2)]

        a4, _ = region(work0)
        xn4, u4, uT4 = a4(2, D), a4(2, D), a4(2, PW)
        xp = a4(NCH, 2 * BT, S + TAPS - 1)
        cv, th = a4(NCH, PW), a4(NCH, PW)
        xs4, xdt, xD = ([a4(DIN) for _ in range(2)] for _ in range(3))
        zt, zs, y4 = ([a4(DIN) for _ in range(2)] for _ in range(3))
        dec = [a4(HM, P) for _ in range(2)]
        gm4 = [a4(P) for _ in range(2)]
        yT4 = [a4(4, P) for _ in range(2)]
        dts = {n: a4(2, HM) for n in ("d", "a", "m", "e", "e2", "r", "s", "s2", "p", "dt", "dtA", "cum")}
        ssq, rms = a4(2), a4(2)
        a5, _ = region(work0)
        xn5 = [a5(D) for _ in range(2)]
        xnT5, sg5, h5 = a5(2, PW), a5(6, PW), a5(6, PW)

        bank = [ps[:, n, :] for n in range(8)]

        def sem(name):
            return ctx.enter_context(nc.semaphore(name))

        all_steps = []

        def steps(name):
            all_steps.append(Steps(name, sem(name + "_done")))
            return all_steps[-1]

        weights1_in, weights2_in, weights3_in, weights4_in, weights5_in = (sem(f"weights{n}_in") for n in range(1, 6))
        x_in = sem("x_in")
        ctx_in = [sem(f"ctx_in{j}") for j in range(2)]
        x_out = sem("x_out")
        setup = steps("setup_vector")
        PE1, AC1, VE1, GP1 = (steps("attn0_" + e) for e in ("tensor", "scalar", "vector", "gpsimd"))

        def view(a, pat, **kw):
            return a.rearrange(pat, **kw)

        tiles_dram = nc.dram_tensor("expert_in", ((E + NOVF) * P, D), fp32, kind="Internal").ap()
        ytiles_dram = nc.dram_tensor("expert_out", ((E + NOVF) * P, D), fp32, kind="Internal").ap()
        mask_dram = nc.dram_tensor("mask_add", (B, KEYS), fp32, kind="Internal").ap()
        zero_in, mask_out, scattered, gathered, weights_sh = (sem(n) for n in ("zero_in", "mask_out", "scattered", "gathered", "shared_weights_in"))
        gu_in = [sem(f"gate_up_in{r}") for r in range(RING)]
        dn_in = [sem(f"down_in{r}") for r in range(RING)]
        xg_in = [sem(f"expert_tokens_in{r}") for r in range(RING)]
        y_out, ovf_in, ovf_out = sem("expert_out_stored"), sem("overflow_in"), sem("overflow_out")
        RT, SHP, SHA, SHV = steps("routing_vector"), steps("shared_tensor"), steps("shared_scalar"), steps("shared_vector")
        PE2, AC2, VE2 = (steps("experts_" + e) for e in ("tensor", "scalar", "vector"))
        PEO, ACO, VEO = (steps("overflow_" + e) for e in ("tensor", "scalar", "vector"))
        XE = steps("x_experts_vector")
        NR = E // RING
        PE3, AC3, VE3, GP3 = (steps("attn1_" + e) for e in ("tensor", "scalar", "vector", "gpsimd"))
        set3 = steps("attn1_setup_vector")
        PE4, AC4, VE4, GP4 = (steps("scan_" + e) for e in ("tensor", "scalar", "vector", "gpsimd"))
        set4, set4a = steps("scan_setup_vector"), steps("scan_setup_scalar")
        PE5, AC5, VE5, GP5 = (steps("ffn_" + e) for e in ("tensor", "scalar", "vector", "gpsimd"))
        ints = steps("ffn_weights_float")
        wk_zero = sem("attn1_zero_done")
        NU = 2 * BT * 2
        CTX3 = 16 * 5

        passed = sem("waits_passed")

        def wait_alone(eng, semaphore, value):
            eng.wait_ge(semaphore, value)
            eng.sem_inc(passed, 1)

        def layer_norm_vector(dve, V, G, tag, p, src, dst, eps):
            for j in range(2):
                nc.vector.bn_stats(st[:, j, :], src(j)).then_inc(V.done(f"{tag}_stats{j}"), 1)
            for j in range(2):
                wait_alone(dve, *V.after(f"{tag}_stats{j}", p))
                nc.vector.bn_aggr(mv[:, j, :], st[:, j, :]).then_inc(V.done(f"{tag}_mean{j}"), 1)
            dve.wait_ge(*V.after(f"{tag}_mean1", p))
            nc.vector.tensor_scalar_add(ve, mv[:, :, 1], eps).then_inc(V.done(f"{tag}_var"), 1)
            dve.wait_ge(*G.after(f"{tag}_rstd", p))
            for j in range(2):
                nc.vector.tensor_scalar(dst(j), src(j), mv[:, j, 0:1], rstd[:, j:j + 1], ALU.subtract,
                                        ALU.mult).then_inc(V.done(f"{tag}_norm{j}"), 1)

        def layer_norm_gpsimd(pool, V, G, tag, p):
            pool.wait_ge(*V.after(f"{tag}_var", p))
            nc.gpsimd.tensor_tensor(rstd, ve, K["mhalf"][:, 0:2], ALU.pow).then_inc(G.done(f"{tag}_rstd"), 1)

        def load_expert(sp, r, e):
            if isinstance(e, int):
                gu, dn = I["e_gu"][e], I["e_dn"][e]
                sp.dma_start(ring_gu[r], gu.rearrange("(k p) n -> p k n", p=P)).then_inc(gu_in[r], 16)
                sp.dma_start(ring_dn[r], dn.rearrange("(k p) n -> p k n", p=P)).then_inc(dn_in[r], 16)
            else:
                sp.dma_start(ring_gu[r], I["e_gu"][bass.ds(e, 1), :, :].rearrange("a (k p) n -> p (a k) n", p=P)).then_inc(gu_in[r], 16)
                sp.dma_start(ring_dn[r], I["e_dn"][bass.ds(e, 1), :, :].rearrange("a (k p) n -> p (a k) n", p=P)).then_inc(dn_in[r], 16)

        def load_tokens(sp, r, it):
            sp.wait_ge(scattered, 16 * NT)
            sp.dma_start(xg[r], tiles_dram[bass.ds(it * (RING * P) + r * P, P), :]).then_inc(xg_in[r], 16)

        def load_context3(sp, j, t):
            load_context(sp, j, t)
            sp.dma_start(cT2[j][DC2 + 1:DC2 + 2], mask_dram[bass.ds(t * BT, BT), :].unsqueeze(0)).then_inc(ctx_in[j], 16)
            sp.dma_start(view(cLb[j], "p a b -> p (a b)"),
                         I["ctx_last"].rearrange("(t b) d -> t (b d)", b=BT)[bass.ds(t, 1), :].partition_broadcast(P)).then_inc(ctx_in[j], 16)

        def load_context(sp, j, t):
            sp.dma_start(cT1[j], I["ctx_T"][t, 0:P, :, :]).then_inc(ctx_in[j], 16)
            sp.dma_start(cT2[j][0:DC2], I["ctx_T"][t, P:DC, :, :]).then_inc(ctx_in[j], 16)
            sp.dma_start(cN[j].rearrange("p b c d -> p (b c) d")[:, :, 0:DC], I["ctx_N"][t]).then_inc(ctx_in[j], 16)

        CTX1 = 16 * (3 + BT)

        block = ctx.enter_context(nc.Block())

        @block.sync
        def _(sp):
            sp.dma_start(const, I["consts"]).then_inc(x_in, 16)
            sp.dma_start(x, I["x"].rearrange("(t p) d -> p t d", p=P)).then_inc(x_in, 16)
            for dst, src in ((wq, I["wq"]), (wk, I["wk"]), (wqkv, I["wqkv"]), (wr, I["wr"])):
                sp.dma_start(dst, src.rearrange("(k p) n -> p k n", p=P)).then_inc(weights1_in, 16)
            sp.dma_start(bq, I["bq"]).then_inc(weights1_in, 16)
            sp.dma_start(wv1, I["wv"][0:P, :]).then_inc(weights1_in, 16)
            sp.dma_start(wv2[0:DC2 + 1, :], I["wv"][P:DC + 1, :]).then_inc(weights1_in, 16)
            sp.dma_start(mask8[0:B, 0:65].bitcast(u8)[:, 0:KEYS], I["mask"]).then_inc(weights1_in, 16)

            for dst, src in ((sg_w, I["s_g"]), (su_w, I["s_u"]), (sd_w, I["s_d"])):
                sp.dma_start(dst, src.rearrange("(k p) n -> p k n", p=P)).then_inc(weights_sh, 16)
            with sp.Fori(0, NPAIR) as p:
                for j in range(2):
                    t = p * 2 + j
                    wait_alone(sp, *PE1.after(f"ov_{j}", p - 1))
                    wait_alone(sp, *VE1.after(f"ov_evac{j}", p - 1))
                    load_context(sp, j, t)
                    for b in range(BT):
                        sp.dma_start(cLq[j][S * b:S * b + S, 0:DC],
                                     I["ctx_last"][bass.ds(t * BT + b, 1), :].partition_broadcast(S)).then_inc(ctx_in[j], 16)
            for r in range(RING):
                load_expert(sp, r, r)
            sp.wait_ge(*setup.sem_value("zero"))
            sp.dma_start(tiles_dram.rearrange("(n p) d -> p n d", p=P), zrow.unsqueeze(1).broadcast_to((P, E + NOVF, D)))\
                .then_inc(zero_in, 16)
            sp.dma_start(ytiles_dram[E * P:, :].rearrange("(n p) d -> p n d", p=P), zrow.unsqueeze(1).broadcast_to((P, NOVF, D)))\
                .then_inc(zero_in, 16)
            sp.wait_ge(*setup.sem_value("negmask"))
            sp.dma_start(mask_dram, negmask[0:B, :]).then_inc(mask_out, 16)
            sp.wait_ge(*PE1.all(NPAIR))
            sp.wait_ge(*VE1.all(NPAIR))
            sp.wait_ge(mask_out, 16)
            for j in range(2):
                load_context3(sp, j, j)
            for dst, src in ((c_wq, I["c_wq"]), (c_wo, I["c_wo"])):
                sp.dma_start(dst, src.rearrange("(k p) n -> p k n", p=P)).then_inc(weights3_in, 16)
            sp.wait_ge(wk_zero, 1)
            for hp in range(2):
                sp.dma_start(view(c_wk, "p (g two) d -> p g two d", two=2)[hp * HD1:(hp + 1) * HD1, :, hp, :],
                             I["c_wk"].rearrange("(g two e) d -> e g two d", two=2, e=HD1)[:, :, hp, :]).then_inc(weights3_in, 16)
            sp.dma_start(c_wv[:, 0, :], I["c_wv"][0:P, :]).then_inc(weights3_in, 16)
            sp.dma_start(c_wv[0:DC2, 1, :], I["c_wv"][P:DC, :]).then_inc(weights3_in, 16)
            sp.dma_start(c_bo, I["c_bo"].partition_broadcast(P)).then_inc(weights3_in, 16)
            for r in range(RING):
                load_tokens(sp, r, 0)
            with sp.Fori(1, NR) as it:
                for r in range(RING):
                    sp.wait_ge(*PE2.after(f"dn{r}", it - 1))
                    load_expert(sp, r, it * RING + r)
                    load_tokens(sp, r, it)
            sp.wait_ge(*RT.sem_value("etab"))
            n_over = sp.value_load(etab.bitcast(i32)[0:1, NOVF:NOVF + 1], min_val=0, max_val=NOVF)
            with sp.If(n_over > 0):
                sp.wait_ge(*PE2.all(NR))
                with sp.Fori(0, NOVF) as i:
                    sp.wait_ge(*PEO.after("dn", i - 1))
                    e = sp.value_load(etab.bitcast(i32)[0:1, bass.ds(i, 1)], min_val=0, max_val=E - 1)
                    sp.dma_start(ring_gu[0], I["e_gu"][bass.ds(e, 1), :, :].rearrange("a (k p) n -> p (a k) n", p=P)).then_inc(ovf_in, 16)
                    sp.dma_start(ring_dn[0], I["e_dn"][bass.ds(e, 1), :, :].rearrange("a (k p) n -> p (a k) n", p=P)).then_inc(ovf_in, 16)
                    sp.dma_start(xg[0], tiles_dram[bass.ds(i * P + E * P, P), :]).then_inc(ovf_in, 16)
            sp.wait_ge(*XE.sem_value("x7"))
            sp.dma_start(m_in, I["m_in"].rearrange("(k p) n -> p k n", p=P)).then_inc(weights4_in, 16)
            sp.dma_start(m_out, I["m_out"].rearrange("(k p) n -> p k n", p=P)).then_inc(weights4_in, 16)
            for dst, src in ((m_lnw, "m_lnw"), (m_lnb, "m_lnb"), (m_D, "m_D"), (m_dtb, "m_dtb"), (m_A, "m_A")):
                sp.dma_start(dst, I[src].partition_broadcast(P)).then_inc(weights4_in, 16)
            sp.dma_start(m_conv, I["m_conv"].rearrange("(c p) t -> p c t", p=P)).then_inc(weights4_in, 16)
            sp.dma_start(m_cb, I["m_cb"]).then_inc(weights4_in, 16)
            sp.dma_start(m_nw, I["m_nw"]).then_inc(weights4_in, 16)
            for dst, src in ((f_gi, "f_g"), (f_ui, "f_u"), (f_di, "f_d")):
                sp.dma_start(dst.bitcast(i32), I[src].rearrange("(k p) n -> p k n", p=P)).then_inc(weights5_in, 16)
            with sp.Fori(1, NPAIR) as p:
                for j in range(2):
                    u = NU // 2 * (j + 1) - 1
                    wait_alone(sp, *PE3.after(f"ov{u}", p - 1))
                    wait_alone(sp, *VE3.after(f"ov_evac{u}", p - 1))
                    load_context3(sp, j, p * 2 + j)
            with sp.Fori(0, NPAIR) as p:
                sp.wait_ge(*VE5.after("x1", p))
                sp.dma_start(out.rearrange("(t p) d -> p t d", p=P)[:, bass.ds(p * 2, 2), :], x[:, bass.ds(p * 2, 2), :]).then_inc(x_out, 16)
            sp.wait_ge(x_out, 16 * NPAIR)

        @block.gpsimd
        def _(pool):
            nc.gpsimd.memset(view(c_wk, "p a b -> p (a b)"), 0.0).then_inc(wk_zero, 1)
            pool.sem_inc(GP1.sem, GP1.round())
            with pool.Fori(0, NPAIR) as p:
                layer_norm_gpsimd(pool, VE1, GP1, "lnA", p)
                layer_norm_gpsimd(pool, VE1, GP1, "lnB", p)
                pool.wait_ge(*VE1.after("ss_max", p))
                nc.gpsimd.tensor_tensor(view(rn, "p a b -> p (a b)"), view(ss, "p a b -> p (a b)"), K["mhalf"],
                                        ALU.pow).then_inc(GP1.done("rnorm"), 1)
                layer_norm_gpsimd(pool, VE1, GP1, "lnC", p)
                pool.wait_ge(*AC1.after("xnT_C", p))
                nc.gpsimd.tensor_copy(xnT_all[:, :, bass.ds(p * PW, PW)], xnT).then_inc(GP1.done("xnT_all"), 1)
            pool.wait_ge(zero_in, 32)
            pool.wait_ge(*RT.sem_value("slot"))
            for t in range(NT):
                pool.indirect_dma_start(out=tiles_dram, out_offset=bass.IndirectOffsetOnAxis(slot_i[:, t:t + 1].bitcast(i32), 0),
                                        in_=xm[:, t, :], in_offset=None).then_inc(scattered, 16)
            with pool.Fori(0, NR) as it:
                for r in range(RING):
                    pool.wait_ge(*VE2.after(f"y{r}", it))
                    pool.dma_start(ytiles_dram[bass.ds(it * (RING * P) + r * P, P), :], ey[r]).then_inc(y_out, 16)
            pool.wait_ge(y_out, 16 * E)
            n_over = pool.value_load(etab.bitcast(i32)[0:1, NOVF:NOVF + 1], min_val=0, max_val=NOVF)
            with pool.If(n_over > 0):
                with pool.Fori(0, NOVF) as i:
                    pool.wait_ge(*VEO.after("y", i))
                    pool.dma_start(ytiles_dram[bass.ds(i * P + E * P, P), :], ey[0]).then_inc(ovf_out, 16)
                pool.wait_ge(ovf_out, 16 * NOVF)
            pool.wait_ge(scattered, 16 * NT)
            for t in range(NT):
                pool.indirect_dma_start(out=yg[:, t, :], out_offset=None, in_=ytiles_dram,
                                        in_offset=bass.IndirectOffsetOnAxis(slot_i[:, t:t + 1].bitcast(i32), 0)).then_inc(gathered, 16)
            pool.sem_inc(GP3.sem, GP3.round())
            with pool.Fori(0, NPAIR) as p:
                layer_norm_gpsimd(pool, VE3, GP3, "ln", p)
            pool.wait_ge(weights5_in, 48)
            for n, (dst, src) in enumerate(((f_g, f_gi), (f_u, f_ui), (f_d, f_di))):
                nc.gpsimd.tensor_copy(dst, src.bitcast(i32)).then_inc(ints.done(f"int{n}"), 1)
            pool.sem_inc(GP4.sem, GP4.round())
            with pool.Fori(0, NPAIR) as p:
                layer_norm_gpsimd(pool, VE4, GP4, "ln1", p)
                layer_norm_gpsimd(pool, VE4, GP4, "ln2", p)
                for j in range(2):
                    pool.wait_ge(*AC4.after(f"xs_evac{j}", p))
                    if j == 0:
                        pool.wait_ge(*set4.sem_value("D"))
                    nc.gpsimd.tensor_tensor(view(xD[j], "p (h e) -> p h e", h=HM), view(xs4[j], "p (h e) -> p h e", h=HM),
                                            m_D.unsqueeze(2).broadcast_to((P, HM, HDM)), ALU.mult).then_inc(GP4.done(f"xD{j}"), 1)
                pool.wait_ge(*VE4.after("mean_square", p))
                nc.gpsimd.tensor_tensor(rms, ssq, K["mhalf"][:, 0:2], ALU.pow).then_inc(GP4.done("rms"), 1)
            pool.sem_inc(GP5.sem, GP5.round())
            with pool.Fori(0, NPAIR) as p:
                layer_norm_gpsimd(pool, VE5, GP5, "ln", p)

        @block.scalar
        def _(act):
            act.sem_inc(AC1.sem, AC1.round())
            act.wait_ge(weights1_in, 16 * 8)
            with act.Fori(0, NPAIR) as p:
                def xnT_evac(tag, pe_step):
                    act.wait_ge(*PE1.after(pe_step, p))
                    nc.scalar.copy(view(xnT, "p a b -> p (a b)"), bank[0]).then_inc(AC1.done(tag), 1)

                xnT_evac("xnT_A", "trA")
                act.wait_ge(*PE1.after("q", p))
                for k in range(2):
                    nc.scalar.activation(qT[:, k, :], bank[1][:, k * PW:(k + 1) * PW], ACT.Identity,
                                         bias=bq[:, k:k + 1]).then_inc(AC1.done(f"q_bias{k}"), 1)
                act.wait_ge(*PE1.after("qk", p))
                nc.scalar.mul(qpT[:, 0, :], bank[2][:, 0:PW], D ** -0.5).then_inc(AC1.done("qk_evac0"), 1)
                nc.scalar.mul(qpT[0:DC2 + 1, 1, :], bank[2][0:DC2 + 1, PW:2 * PW], D ** -0.5)\
                    .then_inc(AC1.done("qk_evac1"), 1)
                for j in range(2):
                    act.wait_ge(*VE1.after(f"row_max{j}", p))
                    nc.scalar.activation(pr[j], bank[3 + j][:, 0:KEYS], ACT.Exp, bias=nmx[:, j:j + 1],
                                         accum_out=sm[:, j:j + 1]).then_inc(AC1.done(f"exp{j}"), 1)
                for j in range(2):
                    act.wait_ge(*PE1.after(f"ot_{j}", p))
                    nc.scalar.copy(oT[j][:, 0, :], bank[1 + j][:, 0:P]).then_inc(AC1.done(f"oT_evac0_{j}"), 1)
                    nc.scalar.copy(oT[j][0:DC2 + 1, 1, :], bank[1 + j][0:DC2 + 1, P:2 * P])\
                        .then_inc(AC1.done(f"oT_evac1_{j}"), 1)
                xnT_evac("xnT_B", "trB")
                for j in range(2):
                    act.wait_ge(*PE1.after(f"qkv_{j}", p))
                    nc.scalar.activation(view(sq[j], "p a b -> p (a b)"), bank[3 + j], ACT.Square)\
                        .then_inc(AC1.done(f"square{j}"), 1)
                    for b in range(BT):
                        nc.scalar.activation(vblk[j][:, :, b, :], view(bank[5 + j][:, 0:D], "p (a b) -> p a b", b=P),
                                             ACT.Copy, scale=K["inb"][:, b:b + 1]).then_inc(AC1.done(f"vblk{j}_{b}"), 1)
                for j in range(2):
                    act.wait_ge(*VE1.after(f"unit{j}", p))
                    nc.scalar.activation(fqk[j], fqk[j], ACT.Exp).then_inc(AC1.done(f"sp_exp{j}"), 1)
                for j in range(2):
                    act.wait_ge(*AC1.after(f"sp_exp{j}", p))
                    nc.scalar.activation(fqk[j], fqk[j], ACT.Ln, bias=K["ones"][:, 0:1]).then_inc(AC1.done(f"softplus{j}"), 1)
                for j in range(2):
                    act.wait_ge(*PE1.after(f"qt_{j}", p))
                    nc.scalar.copy(view(qtT[j], "p a b -> p (a b)"), bank[7 * j][:, 0:2 * P])\
                        .then_inc(AC1.done(f"qt_evac{j}"), 1)
                xnT_evac("xnT_C", "trC")
                act.wait_ge(*VE1.after("top1", p))
                nc.scalar.activation(sc_e, m8[:, :, 0], ACT.Exp, scale=-1.0).then_inc(AC1.done("gate_exp"), 1)
            for s in range(8):
                act.wait_ge(*SHP.sem_value(f"gu{s}"))
                if s >= 2:
                    act.wait_ge(*SHV.sem_value(f"h{s - 2}"))
                nc.scalar.activation(sgate[s % 2], bank[2 * (s % 2)], ACT.Silu).then_inc(SHA.done(f"silu{s}"), 1)
            act.sem_inc(AC2.sem, AC2.round())

            def expert_scalar(PEx, ACx, VEx, s, i, h):
                act.wait_ge(*PEx.after("xt" + s, i))
                nc.scalar.copy(view(xgT[h], "p a b -> p (a b)"), bank[6 + h][:, 0:D]).then_inc(ACx.done("xT" + s), 1)
                act.wait_ge(*PEx.after("gu" + s, i))
                nc.scalar.activation(view(egate[h], "p a b -> p (a b)"), bank[2 * h], ACT.Silu).then_inc(ACx.done("silu" + s), 1)

            with act.Fori(0, NR) as it:
                for r in range(RING):
                    if r < 2:
                        act.wait_ge(*VE2.after(f"h{r + 2}", it - 1))
                    else:
                        act.wait_ge(*VE2.after(f"h{r - 2}", it))
                    expert_scalar(PE2, AC2, VE2, str(r), it, r % 2)
            n_over = act.value_load(etab.bitcast(i32)[0:1, NOVF:NOVF + 1], min_val=0, max_val=NOVF)
            with act.If(n_over > 0):
                act.sem_inc(ACO.sem, ACO.round())
                act.wait_ge(*VE2.all(NR))
                with act.Fori(0, NOVF) as i:
                    expert_scalar(PEO, ACO, VEO, "", i, 0)
                act.wait_ge(*VEO.all(NOVF))
            act.sem_inc(AC3.sem, AC3.round())
            with act.Fori(0, NPAIR) as p:
                act.wait_ge(*PE3.after("tr", p))
                nc.scalar.copy(view(xnT3, "p a b -> p (a b)"), bank[0]).then_inc(AC3.done("xnT"), 1)
                for n in range(2):
                    act.wait_ge(*PE3.after(f"q{n}", p))
                    nc.scalar.copy(view(q3[:, 2 * n:2 * n + 2, :], "p a b -> p (a b)"), bank[2 + n]).then_inc(AC3.done(f"q_evac{n}"), 1)
                for h in range(H1):
                    act.wait_ge(*PE3.after(f"qk{h}", p))
                    nc.scalar.mul(qp3[:, 0, :, h * S:(h + 1) * S], view(bank[4 + h % 4][:, 0:PW], "p (b s) -> p b s", s=S),
                                  HD1 ** -0.5).then_inc(AC3.done(f"qk_evac{h}"), 1)
                for s in range(NU + 2):
                    if s < NU:
                        act.wait_ge(*VE3.after(f"row_max{s}", p))
                        if s >= 4:
                            act.wait_ge(*VE3.after(f"ov_evac{s - 4}", p))
                        nc.scalar.activation(pr3[s % 4], bank[s % 2][:, 0:KEYS], ACT.Exp, bias=nmx3[:, s % 4:s % 4 + 1],
                                             accum_out=sm3[:, s % 4:s % 4 + 1]).then_inc(AC3.done(f"exp{s}"), 1)
                    if s >= 2:
                        act.wait_ge(*PE3.after(f"pt{s - 2}", p))
                        nc.scalar.copy(view(pT3[s % 2], "p a b -> p (a b)"), bank[2 + s % 2][:, 0:2 * P])\
                            .then_inc(AC3.done(f"pT_evac{s - 2}"), 1)
                for j in range(2):
                    act.wait_ge(*PE3.after(f"o{j}", p))
                    nc.scalar.copy(o3[j], bank[j]).then_inc(AC3.done(f"o_evac{j}"), 1)
                for j in range(2):
                    act.wait_ge(*PE3.after(f"ot{j}", p))
                    nc.scalar.copy(view(o3T[j], "p a b -> p (a b)"), bank[2 + j]).then_inc(AC3.done(f"ot_evac{j}"), 1)
            act.wait_ge(weights4_in, 16 * 10)
            nc.scalar.activation(m_A, m_A, ACT.Exp).then_inc(set4a.done("expA"), 1)
            act.sem_inc(AC4.sem, AC4.round())
            with act.Fori(0, NPAIR) as p:
                act.wait_ge(*PE4.after("tr", p))
                nc.scalar.copy(view(uT4, "p a b -> p (a b)"), bank[0]).then_inc(AC4.done("uT"), 1)
                for n in (2, 0, 1):
                    act.wait_ge(*PE4.after(f"xbc{n}", p))
                    nc.scalar.copy(xp[:, 2 * n:2 * n + 2, :, TAPS - 1:TAPS - 1 + S],
                                   view(bank[1 + n], "p (c b s) -> p c b s", c=2, s=S)).then_inc(AC4.done(f"xp{n}"), 1)
                    for c in range(2):
                        nc.scalar.activation(cv[:, 2 * n + c, :], bank[1 + n][:, c * PW:(c + 1) * PW], ACT.Identity,
                                             bias=m_cb[:, 2 * n + c:2 * n + c + 1], scale=m_conv[:, 2 * n + c, TAPS - 1:TAPS])\
                            .then_inc(AC4.done(f"tap3_{2 * n + c}"), 1)
                act.wait_ge(*VE4.after("dt_abs", p))
                nc.scalar.activation(dts["e"], dts["a"], ACT.Exp, scale=-1.0).then_inc(AC4.done("dt_exp"), 1)
                for j in range(2):
                    act.wait_ge(*PE4.after(f"z{j}", p))
                    nc.scalar.activation(zt[j], bank[4 + j], ACT.Tanh, scale=0.5).then_inc(AC4.done(f"z_tanh{j}"), 1)
                for n in (2, 0, 1):
                    act.wait_ge(*VE4.after(f"tap2_{2 * n + 1}", p))
                    nc.scalar.activation(th[:, 2 * n:2 * n + 2, :], cv[:, 2 * n:2 * n + 2, :], ACT.Tanh, scale=0.5)\
                        .then_inc(AC4.done(f"tanh{n}"), 1)
                for j in range(2):
                    act.wait_ge(*VE4.after("cum", p))
                    act.wait_ge(*PE4.after(f"cumT{j}", p))
                    for h in range(HM):
                        nc.scalar.activation(dec[j][:, h, :], bank[(3, 0)[h // 4]][:, (h % 4) * P:(h % 4 + 1) * P], ACT.Relu,
                                             scale=-1.0, bias=dts["cum"][:, j, h:h + 1]).then_inc(AC4.done(f"relu{j}_{h}"), 1)
                    act.wait_ge(*AC4.after(f"relu{j}_7", p))
                    nc.scalar.activation(dec[j], dec[j], ACT.Exp, scale=-1.0).then_inc(AC4.done(f"decay{j}"), 1)
                for j in range(2):
                    act.wait_ge(*PE4.after(f"xs{j}", p))
                    nc.scalar.copy(xs4[j], bank[1 + j]).then_inc(AC4.done(f"xs_evac{j}"), 1)
                for j in range(2):
                    act.wait_ge(*VE4.after(f"yz{j}", p))
                    nc.scalar.activation(zt[j], y4[j], ACT.Square, accum_out=ssq[:, j:j + 1]).then_inc(AC4.done(f"square{j}"), 1)
                for j in range(2):
                    act.wait_ge(*PE4.after(f"yT{j}", p))
                    nc.scalar.copy(view(yT4[j], "p a b -> p (a b)"), bank[1 + j]).then_inc(AC4.done(f"yT_evac{j}"), 1)
            act.sem_inc(AC5.sem, AC5.round())
            with act.Fori(0, NPAIR) as p:
                act.wait_ge(*PE5.after("tr", p))
                nc.scalar.copy(view(xnT5, "p a b -> p (a b)"), bank[6]).then_inc(AC5.done("xnT"), 1)
                for n in range(3):
                    act.wait_ge(*PE5.after(f"g{n}", p))
                    nc.scalar.activation(sg5[:, 2 * n:2 * n + 2, :], view(bank[n], "p (c t) -> p c t", c=2), ACT.Silu, scale=1.0 / 127.0)\
                        .then_inc(AC5.done(f"silu{n}"), 1)

        @block.vector
        def _(dve):
            nc.vector.memset(view(cT2[0], "p a b -> p (a b)")[DC2:DC2 + 1, :], 1.0).then_inc(setup.done("ones0"), 1)
            nc.vector.memset(view(cT2[1], "p a b -> p (a b)")[DC2:DC2 + 1, :], 1.0).then_inc(setup.done("ones1"), 1)
            for j in range(2):
                nc.vector.memset(cN[j][:, :, :, DC:DC + 1], 1.0).then_inc(setup.done(f"ones_n{j}"), 1)
                nc.vector.memset(cLq[j][:, DC:DC + 1], 1.0).then_inc(setup.done(f"ones_l{j}"), 1)
            nc.vector.memset(zrow, 0.0).then_inc(setup.done("zero"), 1)
            dve.wait_ge(weights1_in, 16 * 8)
            nc.vector.tensor_scalar(negmask[0:B, :], mask8[0:B, 0:65].bitcast(u8)[:, 0:KEYS], 1.0, -MASKED, ALU.subtract,
                                    ALU.mult).then_inc(setup.done("negmask"), 1)
            dve.sem_inc(VE1.sem, VE1.round())
            dve.wait_ge(x_in, 32)
            dve.wait_ge(*setup.sem_value("ones_l1"))
            with dve.Fori(0, NPAIR) as p:
                def xt(j):
                    return x[:, p * 2 + j, :]

                wait_alone(dve, *PE1.after("trC", p - 1))
                layer_norm_vector(dve, VE1, GP1, "lnA", p, xt, lambda j: xn[j], 1e-5)
                for j in range(2):
                    dve.wait_ge(*PE1.after(f"sc_{j}", p))
                    nc.vector.reduce_max(nmx[:, j:j + 1], bank[3 + j][:, 0:KEYS], AX, negate=True)\
                        .then_inc(VE1.done(f"row_max{j}"), 1)
                for j in range(2):
                    dve.wait_ge(*PE1.after(f"pt_{j}", p))
                    nc.vector.tensor_copy(view(pT[j], "p a b -> p (a b)"), bank[5 + j][:, 0:2 * P])\
                        .then_inc(VE1.done(f"pT_evac{j}"), 1)
                dve.wait_ge(*AC1.after("exp1", p))
                nc.vector.reciprocal(ri, sm).then_inc(VE1.done("rsum"), 1)
                for j in range(2):
                    dve.wait_ge(*PE1.after(f"ov_{j}", p))
                    dve.wait_ge(ctx_in[j], (p + 1) * CTX1)
                    nc.vector.scalar_tensor_tensor(op[j], cLq[j], pr[j][:, KEYS - 1:KEYS], bank[7 * j][:, 0:DC + 1],
                                                   ALU.mult, ALU.add).then_inc(VE1.done(f"ov_evac{j}"), 1)
                for j in range(2):
                    dve.wait_ge(*PE1.after(f"wv_{j}", p))
                    nc.vector.scalar_tensor_tensor(xt(j), bank[5 + j][:, 0:D], ri[:, j:j + 1], xt(j), ALU.mult,
                                                   ALU.add).then_inc(VE1.done(f"x_attn{j}"), 1)
                wait_alone(dve, *VE1.after("x_attn1", p))
                layer_norm_vector(dve, VE1, GP1, "lnB", p, xt, lambda j: xn[j], 1e-5)
                for j in range(2):
                    dve.wait_ge(*AC1.after(f"square{j}", p))
                    nc.vector.reduce_sum(ss[:, j, :], sq[j], AX).then_inc(VE1.done(f"ss{j}"), 1)
                dve.wait_ge(*VE1.after("ss1", p))
                nc.vector.tensor_scalar_max(ss, ss, 1e-24).then_inc(VE1.done("ss_max"), 1)
                dve.wait_ge(*GP1.after("rnorm", p))
                for j in range(2):
                    nc.vector.tensor_tensor(view(fqk[j], "p (a b) -> p a b", b=16), view(bank[3 + j], "p (a b) -> p a b", b=16),
                                            rn[:, j, :].unsqueeze(2).broadcast_to((P, 32, 16)), ALU.mult)\
                        .then_inc(VE1.done(f"unit{j}"), 1)
                for j in range(2):
                    dve.wait_ge(*PE1.after(f"ks_{j}", p))
                    nc.vector.scalar_tensor_tensor(view(dtmp[j], "p a b -> p (a b)"), bank[5 + j][:, D:2 * D], 1e-6,
                                                   fqk[j][:, 0:D], ALU.add, ALU.mult).then_inc(VE1.done(f"den_mul{j}"), 1)
                    for hf in range(2):
                        dve.wait_ge(*PE1.after(f"kv_{j}_{hf}", p))
                        nc.vector.tensor_tensor(kvm[j][:, hf, :, :], view(bank[1 + 2 * j + hf], "p (a b) -> p a b", b=P),
                                                K["hmask"].unsqueeze(1).broadcast_to((P, BT, P)), ALU.mult)\
                            .then_inc(VE1.done(f"kv_evac{j}_{hf}"), 1)
                    dve.wait_ge(*VE1.after(f"den_mul{j}", p))
                    nc.vector.reduce_sum(den[:, j, :], dtmp[j], AX).then_inc(VE1.done(f"den{j}"), 1)
                dve.wait_ge(*VE1.after("den1", p))
                nc.vector.reciprocal(den, den).then_inc(VE1.done("rden"), 1)
                dve.wait_ge(*VE1.after("rden", p))
                for j in range(2):
                    dve.wait_ge(*PE1.after(f"at_{j}", p))
                    nc.vector.tensor_tensor(dtmp[j], view(bank[5 + j][:, 0:D], "p (a b) -> p a b", b=16),
                                            den[:, j, :].unsqueeze(2).broadcast_to((P, 16, 16)), ALU.mult)\
                        .then_inc(VE1.done(f"at_norm{j}"), 1)
                for j in range(2):
                    dve.wait_ge(*VE1.after(f"at_norm{j}", p))
                    nc.vector.tensor_tensor(xt(j), xt(j), view(dtmp[j], "p a b -> p (a b)"), ALU.add)\
                        .then_inc(VE1.done(f"x_lin{j}"), 1)
                wait_alone(dve, *VE1.after("x_lin1", p))
                layer_norm_vector(dve, VE1, GP1, "lnC", p, xt, lambda j: xn[j], 1e-5)
                dve.wait_ge(*PE1.after("lg", p))
                nc.vector.tensor_copy(lg, view(bank[7][:, 0:2 * E], "p (a b) -> p a b", b=E)).then_inc(VE1.done("logits"), 1)
                wait_alone(dve, *VE1.after("logits", p))
                for j in range(2):
                    nc.vector.max(m8[:, j, :], lg[:, j, :]).then_inc(VE1.done(f"top{j}"), 1)
                for j in range(2):
                    wait_alone(dve, *VE1.after(f"top{j}", p))
                    nc.vector.max_index(mi[:, j, :].bitcast(u32), m8[:, j, :], lg[:, j, :]).then_inc(VE1.done(f"argmax{j}"), 1)
                dve.wait_ge(*VE1.after("argmax1", p))
                nc.vector.tensor_copy(idx_f, mi[:, :, 0].bitcast(u32)).then_inc(VE1.done("arg_f"), 1)
                dve.wait_ge(*AC1.after("gate_exp", p))
                nc.vector.tensor_scalar_add(score, sc_e, 1.0).then_inc(VE1.done("gate_1p"), 1)
                dve.wait_ge(*VE1.after("gate_1p", p))
                nc.vector.reciprocal(score, score).then_inc(VE1.done("gate"), 1)
                nc.vector.tensor_copy(eidx[:, bass.ds(p * 2, 2)], idx_f).then_inc(VE1.done("eidx"), 1)
                for j in range(2):
                    nc.vector.tensor_scalar(oneh[:, p * 2 + j, :], K["iota"], idx_f[:, j:j + 1], None, ALU.is_equal)\
                        .then_inc(VE1.done(f"onehot{j}"), 1)
                dve.wait_ge(*VE1.after("gate", p))
                for j in range(2):
                    nc.vector.tensor_scalar_mul(xm[:, p * 2 + j, :], xn[j], score[:, j:j + 1]).then_inc(VE1.done(f"xm{j}"), 1)
                dve.wait_ge(*VE1.after("xm1", p))
            def flat3(a):
                return view(a, "p a b -> p (a b)")

            dve.wait_ge(*SHP.sem_value("rank"))
            nc.vector.tensor_tensor(flat3(r_oh), bank[6][:, 0:NT * E], flat3(oneh), ALU.mult).then_inc(RT.done("rank_oh"), 1)
            dve.wait_ge(*SHP.sem_value("count"))
            nc.vector.tensor_tensor(cnt7, bank[7][:, 0:E].unsqueeze(2).broadcast_to((P, E, NT - 1)),
                                    K["caps"].unsqueeze(1).broadcast_to((P, E, NT - 1)), ALU.is_gt).then_inc(RT.done("over7"), 1)
            dve.wait_ge(*RT.sem_value("rank_oh"))
            nc.vector.reduce_sum(rank, r_oh, AX).then_inc(RT.done("rank"), 1)
            dve.wait_ge(*RT.sem_value("over7"))
            nc.vector.reduce_sum(novf, cnt7, AX).then_inc(RT.done("novf"), 1)
            dve.wait_ge(*RT.sem_value("rank"))
            nc.vector.tensor_tensor(r_q7, rank.unsqueeze(2).broadcast_to((P, NT, NT - 1)),
                                    K["caps"].unsqueeze(1).broadcast_to((P, NT, NT - 1)), ALU.is_ge).then_inc(RT.done("q7"), 1)
            dve.wait_ge(*RT.sem_value("novf"))
            nc.vector.tensor_tensor_scan(oend, K["ones"][:, 0:E], novf, 0.0, ALU.mult, ALU.add).then_inc(RT.done("oend"), 1)
            dve.wait_ge(*RT.sem_value("q7"))
            nc.vector.reduce_sum(rq, r_q7, AX).then_inc(RT.done("q"), 1)
            dve.wait_ge(*RT.sem_value("oend"))
            nc.vector.tensor_tensor(obase, oend, novf, ALU.subtract).then_inc(RT.done("obase"), 1)
            nc.vector.tensor_tensor(r_e7, oend.unsqueeze(1).broadcast_to((P, NOVF, E)),
                                    K["nth"].unsqueeze(2).broadcast_to((P, NOVF, E)), ALU.is_le).then_inc(RT.done("e7"), 1)
            dve.wait_ge(*RT.sem_value("obase"))
            nc.vector.tensor_tensor(r_oh, oneh, obase.unsqueeze(1).broadcast_to((P, NT, E)), ALU.mult).then_inc(RT.done("base_oh"), 1)
            dve.wait_ge(*RT.sem_value("e7"))
            nc.vector.reduce_sum(etab_f[:, 0:NOVF], r_e7, AX).then_inc(RT.done("etab_sum"), 1)
            dve.wait_ge(*RT.sem_value("base_oh"))
            nc.vector.reduce_sum(r_bt, r_oh, AX).then_inc(RT.done("base"), 1)
            dve.wait_ge(*RT.sem_value("etab_sum"))
            nc.vector.tensor_scalar_min(etab_f[:, 0:NOVF], etab_f[:, 0:NOVF], E - 1.0).then_inc(RT.done("etab_min"), 1)
            nc.vector.tensor_copy(etab_f[:, NOVF:NOVF + 1], oend[:, E - 1:E]).then_inc(RT.done("etab_n"), 1)
            dve.wait_ge(*RT.sem_value("base"))
            nc.vector.tensor_tensor(r_t, r_bt, rq, ALU.add).then_inc(RT.done("t1"), 1)
            dve.wait_ge(*RT.sem_value("etab_n"))
            nc.vector.tensor_copy(etab.bitcast(i32), etab_f).then_inc(RT.done("etab"), 1)
            nc.vector.tensor_scalar_min(r_g, rq, 1.0).then_inc(RT.done("past"), 1)
            dve.wait_ge(*RT.sem_value("t1"))
            nc.vector.scalar_tensor_tensor(r_t, r_t, E - 1.0, eidx, ALU.add, ALU.subtract).then_inc(RT.done("t2"), 1)
            dve.wait_ge(*RT.sem_value("t2"))
            nc.vector.tensor_tensor(r_t, r_t, r_g, ALU.mult).then_inc(RT.done("t3"), 1)
            dve.wait_ge(*RT.sem_value("t3"))
            nc.vector.tensor_tensor(r_t, r_t, eidx, ALU.add).then_inc(RT.done("tile"), 1)
            dve.wait_ge(*RT.sem_value("tile"))
            nc.vector.scalar_tensor_tensor(slot_f, r_t, float(P), rank, ALU.mult, ALU.add).then_inc(RT.done("slot1"), 1)
            dve.wait_ge(*RT.sem_value("slot1"))
            nc.vector.scalar_tensor_tensor(slot_f, rq, -float(P), slot_f, ALU.mult, ALU.add).then_inc(RT.done("slot2"), 1)
            dve.wait_ge(*RT.sem_value("slot2"))
            nc.vector.tensor_copy(slot_i.bitcast(i32), slot_f).then_inc(RT.done("slot"), 1)
            for s in range(8):
                n, c = s // 4, s % 4
                dve.wait_ge(*SHA.sem_value(f"silu{s}"))
                nc.vector.tensor_tensor(hs[:, c, n * 512:(n + 1) * 512], sgate[s % 2], bank[2 * (s % 2) + 1], ALU.mult)\
                    .then_inc(SHV.done(f"h{s}"), 1)
            for t in range(NT):
                dve.wait_ge(*SHP.sem_value(f"down{t}"))
                nc.vector.tensor_tensor(x[:, t, :], x[:, t, :], bank[4 + t % 2][:, 0:D], ALU.add).then_inc(SHV.done(f"x{t}"), 1)
            dve.sem_inc(VE2.sem, VE2.round())

            def expert_vector(PEx, ACx, VEx, s, i, h, y):
                dve.wait_ge(*ACx.after("silu" + s, i))
                nc.vector.tensor_tensor(flat3(eh[h]), flat3(egate[h]), bank[2 * h + 1], ALU.mult).then_inc(VEx.done("h" + s), 1)
                dve.wait_ge(*PEx.after("dn" + s, i))
                nc.vector.tensor_copy(y, bank[4 + h][:, 0:D]).then_inc(VEx.done("y" + s), 1)

            with dve.Fori(0, NR) as it:
                dve.wait_ge(y_out, it * (16 * RING))
                for r in range(RING):
                    expert_vector(PE2, AC2, VE2, str(r), it, r % 2, ey[r])
            n_over = dve.value_load(etab.bitcast(i32)[0:1, NOVF:NOVF + 1], min_val=0, max_val=NOVF)
            with dve.If(n_over > 0):
                dve.sem_inc(VEO.sem, VEO.round())
                dve.wait_ge(y_out, 16 * E)
                with dve.Fori(0, NOVF) as i:
                    dve.wait_ge(ovf_out, i * 16)
                    expert_vector(PEO, ACO, VEO, "", i, 0, ey[0])
            dve.wait_ge(gathered, 16 * NT)
            for t in range(NT):
                nc.vector.tensor_tensor(x[:, t, :], x[:, t, :], yg[:, t, :], ALU.add).then_inc(XE.done(f"x{t}"), 1)
            for j in range(2):
                nc.vector.memset(op3[j], 0.0).then_inc(set3.done(f"op_zero{j}"), 1)
            dve.wait_ge(*XE.sem_value("x7"))
            nc.vector.memset(qp3[DC2:DC2 + 2, 1, :, :], 1.0).then_inc(set3.done("rows_one"), 1)
            dve.wait_ge(*set3.sem_value("rows_one"))
            nc.vector.memset(qp3[DC2:DC2 + 1, 1, :, :], 0.0).then_inc(set3.done("row_zero"), 1)
            dve.wait_ge(*set3.sem_value("row_zero"))
            dve.wait_ge(weights3_in, 16 * 7)
            dve.sem_inc(VE3.sem, VE3.round())
            with dve.Fori(0, NPAIR) as p:
                wait_alone(dve, *PE3.after("tr", p - 1))
                layer_norm_vector(dve, VE3, GP3, "ln", p, lambda j: x[:, p * 2 + j, :], lambda j: xn3[j], 1e-5)
                for h in range(H1):
                    dve.wait_ge(*AC3.after(f"qk_evac{h}", p))
                    nc.vector.tensor_scalar_mul(qp3[0:DC2, 1, :, h * S:(h + 1) * S],
                                                view(bank[4 + h % 4][0:DC2, PW:2 * PW], "p (b s) -> p b s", s=S),
                                                HD1 ** -0.5).then_inc(VE3.done(f"qk_evac{h}"), 1)
                for s in range(NU + 4):
                    if s < NU:
                        dve.wait_ge(*PE3.after(f"sc{s}", p))
                        nc.vector.reduce_max(nmx3[:, s % 4:s % 4 + 1], bank[s % 2][:, 0:KEYS], AX, negate=True)\
                            .then_inc(VE3.done(f"row_max{s}"), 1)
                    if 1 <= s <= NU:
                        u = s - 1
                        dve.wait_ge(*AC3.after(f"exp{u}", p))
                        nc.vector.reciprocal(rs3[:, u % 4:u % 4 + 1], sm3[:, u % 4:u % 4 + 1]).then_inc(VE3.done(f"rsum{u}"), 1)
                        dve.wait_ge(*VE3.after(f"rsum{u}", p))
                        nc.vector.tensor_scalar_mul(pr3[u % 4], pr3[u % 4], rs3[:, u % 4:u % 4 + 1]).then_inc(VE3.done(f"norm{u}"), 1)
                    if 3 <= s < NU + 3:
                        u = s - 3
                        b = u // 2
                        if u == 0 or u == NU // 2:
                            dve.wait_ge(ctx_in[b // BT], (p + 1) * CTX3 + NPAIR * CTX1)
                        dve.wait_ge(*PE3.after(f"ov{u}", p))
                        nc.vector.scalar_tensor_tensor(op3[u % 2][:, 0:DC], cLb[b // BT][:, b % BT, :], pr3[u % 4][:, KEYS - 1:KEYS],
                                                       bank[4 + u % 2][:, 0:DC], ALU.mult, ALU.add).then_inc(VE3.done(f"ov_evac{u}"), 1)
                    if s >= 4:
                        u = s - 4
                        b, g = u // 2, u % 2
                        dve.wait_ge(*PE3.after(f"opT{u}", p))
                        if u == 0:
                            dve.wait_ge(*PE3.after("o1", p - 1))
                        nc.vector.tensor_copy(oT3[b // BT][:, :, 4 * g:4 * g + 4, b % BT, :],
                                              view(bank[6 + u % 2][:, 0:2 * P], "p (c h s) -> p c h s", c=2, s=S))\
                            .then_inc(VE3.done(f"opT_evac{u}"), 1)
                for j in range(2):
                    dve.wait_ge(*PE3.after(f"wo{j}", p))
                    nc.vector.tensor_tensor(t3[j], bank[4 + j][:, 0:D], c_bo, ALU.add).then_inc(VE3.done(f"bias{j}"), 1)
                for j in range(2):
                    dve.wait_ge(*VE3.after(f"bias{j}", p))
                    nc.vector.tensor_tensor(x[:, p * 2 + j, :], x[:, p * 2 + j, :], t3[j], ALU.add).then_inc(VE3.done(f"x{j}"), 1)
                dve.wait_ge(*VE3.after("x1", p))
            dve.wait_ge(weights4_in, 16 * 10)
            nc.vector.memset(xp[:, :, :, 0:TAPS - 1], 0.0).then_inc(set4.done("pad"), 1)
            for c in range(4):
                nc.vector.tensor_scalar_mul(m_out[:, c, :], m_out[:, c, :], m_nw[:, c:c + 1]).then_inc(set4.done(f"nw{c}"), 1)
            nc.vector.tensor_scalar_mul(m_D, m_D, 0.25).then_inc(set4.done("D"), 1)
            dve.wait_ge(*set4a.sem_value("expA"))
            nc.vector.tensor_scalar_mul(m_A, m_A, -1.0).then_inc(set4.done("A"), 1)
            dve.wait_ge(*set4.sem_value("A"))
            dve.sem_inc(VE4.sem, VE4.round())
            with dve.Fori(0, NPAIR) as p:
                wait_alone(dve, *PE4.after("out1", p - 1))
                layer_norm_vector(dve, VE4, GP4, "ln1", p, lambda j: x[:, p * 2 + j, :], lambda j: xn4[:, j, :], 1e-5)
                wait_alone(dve, *VE4.after("ln1_norm1", p))
                layer_norm_vector(dve, VE4, GP4, "ln2", p, lambda j: xn4[:, j, :], lambda j: u4[:, j, :], 1e-5)
                dve.wait_ge(*VE4.after("ln2_norm1", p))
                nc.vector.tensor_tensor(u4, u4, m_lnw.unsqueeze(1).broadcast_to((P, 2, D)), ALU.mult).then_inc(VE4.done("ln_w"), 1)
                dve.wait_ge(*VE4.after("ln_w", p))
                nc.vector.tensor_tensor(u4, u4, m_lnb.unsqueeze(1).broadcast_to((P, 2, D)), ALU.add).then_inc(VE4.done("u"), 1)
                dve.wait_ge(*PE4.after("dt", p))
                nc.vector.tensor_tensor(dts["d"], view(bank[6][:, 0:2 * HM], "p (a b) -> p a b", b=HM),
                                        m_dtb.unsqueeze(1).broadcast_to((P, 2, HM)), ALU.add).then_inc(VE4.done("dt_raw"), 1)
                dve.wait_ge(*VE4.after("dt_raw", p))
                nc.vector.scalar_tensor_tensor(dts["a"], dts["d"], -1.0, dts["d"], ALU.mult, ALU.max).then_inc(VE4.done("dt_abs"), 1)
                nc.vector.tensor_scalar_max(dts["m"], dts["d"], 0.0).then_inc(VE4.done("dt_pos"), 1)
                for n in (2, 0, 1):
                    for k in range(TAPS - 1):
                        for c in (2 * n, 2 * n + 1):
                            if k:
                                dve.wait_ge(*VE4.after(f"tap{k - 1}_{c}", p))
                            else:
                                dve.wait_ge(*AC4.after(f"tap3_{2 * n + 1}", p))
                            nc.vector.scalar_tensor_tensor(view(cv[:, c, :], "p (b s) -> p b s", s=S), xp[:, c, :, k:k + S],
                                                           m_conv[:, c, k:k + 1], view(cv[:, c, :], "p (b s) -> p b s", s=S),
                                                           ALU.mult, ALU.add).then_inc(VE4.done(f"tap{k}_{c}"), 1)
                    if n == 2:
                        dve.wait_ge(*AC4.after("dt_exp", p))
                        nc.vector.tensor_scalar_add(dts["e2"], dts["e"], 2.0).then_inc(VE4.done("dt_2e"), 1)
                        dve.wait_ge(*VE4.after("dt_2e", p))
                        nc.vector.reciprocal(dts["r"], dts["e2"]).then_inc(VE4.done("dt_r"), 1)
                        dve.wait_ge(*VE4.after("dt_r", p))
                        nc.vector.tensor_tensor(dts["s"], dts["e"], dts["r"], ALU.mult).then_inc(VE4.done("dt_s"), 1)
                        dve.wait_ge(*VE4.after("dt_s", p))
                        nc.vector.tensor_tensor(dts["s2"], dts["s"], dts["s"], ALU.mult).then_inc(VE4.done("dt_s2"), 1)
                        dve.wait_ge(*VE4.after("dt_s2", p))
                        nc.vector.tensor_scalar_mul(dts["p"], dts["s2"], 1.0 / 15.0).then_inc(VE4.done("dt_p15"), 1)
                        for i in (13, 11, 9, 7, 5, 3):
                            dve.wait_ge(*VE4.after(f"dt_p{i + 2}", p))
                            nc.vector.scalar_tensor_tensor(dts["p"], dts["p"], 1.0 / i, dts["s2"], ALU.add, ALU.mult)\
                                .then_inc(VE4.done(f"dt_p{i}"), 1)
                        dve.wait_ge(*VE4.after("dt_p3", p))
                        nc.vector.scalar_tensor_tensor(dts["p"], dts["p"], 1.0, dts["s"], ALU.add, ALU.mult)\
                            .then_inc(VE4.done("dt_p1"), 1)
                        dve.wait_ge(*VE4.after("dt_p1", p))
                        nc.vector.scalar_tensor_tensor(dts["dt"], dts["p"], 2.0, dts["m"], ALU.mult, ALU.add)\
                            .then_inc(VE4.done("dt"), 1)
                        dve.wait_ge(*VE4.after("dt", p))
                        nc.vector.tensor_tensor(dts["dtA"], dts["dt"], m_A.unsqueeze(1).broadcast_to((P, 2, HM)), ALU.mult)\
                            .then_inc(VE4.done("dtA"), 1)
                for n in (2, 0, 1):
                    dve.wait_ge(*AC4.after(f"tanh{n}", p))
                    nc.vector.scalar_tensor_tensor(cv[:, 2 * n:2 * n + 2, :], th[:, 2 * n:2 * n + 2, :], 1.0, cv[:, 2 * n:2 * n + 2, :],
                                                   ALU.add, ALU.mult).then_inc(VE4.done(f"silu{n}"), 1)
                    if n == 2:
                        dve.wait_ge(*PE4.after("cum", p))
                        nc.vector.tensor_copy(dts["cum"], view(bank[6][:, 2 * HM:4 * HM], "p (a b) -> p a b", b=HM)).then_inc(VE4.done("cum"), 1)
                for j in range(2):
                    dve.wait_ge(*AC4.after(f"z_tanh{j}", p))
                    nc.vector.scalar_tensor_tensor(zs[j], zt[j], 1.0, bank[4 + j], ALU.add, ALU.mult).then_inc(VE4.done(f"z_silu{j}"), 1)
                for j in range(2):
                    dve.wait_ge(*PE4.after("G1", p))
                    nc.vector.tensor_tensor(gm4[j], bank[7][:, j * P:(j + 1) * P], K["gmask"], ALU.mult).then_inc(VE4.done(f"gm{j}"), 1)
                for j in range(2):
                    dve.wait_ge(*AC4.after(f"decay{j}", p))
                    dve.wait_ge(*VE4.after(f"gm{j}", p))
                    nc.vector.tensor_tensor(dec[j], dec[j], gm4[j].unsqueeze(1).broadcast_to((P, HM, P)), ALU.mult)\
                        .then_inc(VE4.done(f"M{j}"), 1)
                for j in range(2):
                    dve.wait_ge(*AC4.after(f"xs_evac{j}", p))
                    nc.vector.tensor_tensor(view(xdt[j], "p (h e) -> p h e", h=HM), view(xs4[j], "p (h e) -> p h e", h=HM),
                                            dts["dt"][:, j, :].unsqueeze(2).broadcast_to((P, HM, HDM)), ALU.mult)\
                        .then_inc(VE4.done(f"xdt{j}"), 1)
                for j in range(2):
                    dve.wait_ge(*PE4.after(f"y{j}", p))
                    dve.wait_ge(*GP4.after(f"xD{j}", p))
                    nc.vector.tensor_tensor(y4[j], bank[4 + j], xD[j], ALU.add).then_inc(VE4.done(f"ya{j}"), 1)
                for j in range(2):
                    dve.wait_ge(*VE4.after(f"ya{j}", p))
                    nc.vector.tensor_tensor(y4[j], y4[j], zs[j], ALU.mult).then_inc(VE4.done(f"yz{j}"), 1)
                for j in range(2):
                    nc.vector.tensor_tensor(x[:, p * 2 + j, :], x[:, p * 2 + j, :], xn4[:, j, :], ALU.add).then_inc(VE4.done(f"xr{j}"), 1)
                dve.wait_ge(*AC4.after("square1", p))
                nc.vector.tensor_scalar(ssq, ssq, 1.0 / DIN, 1e-5, ALU.mult, ALU.add).then_inc(VE4.done("mean_square"), 1)
                dve.wait_ge(*GP4.after("rms", p))
                for j in range(2):
                    dve.wait_ge(*PE4.after(f"out{j}", p))
                    nc.vector.scalar_tensor_tensor(x[:, p * 2 + j, :], bank[6 + j][:, 0:D], rms[:, j:j + 1], x[:, p * 2 + j, :],
                                                   ALU.mult, ALU.add).then_inc(VE4.done(f"x{j}"), 1)
                dve.wait_ge(*VE4.after("x1", p))
            dve.sem_inc(VE5.sem, VE5.round())
            with dve.Fori(0, NPAIR) as p:
                wait_alone(dve, *PE5.after("tr", p - 1))
                layer_norm_vector(dve, VE5, GP5, "ln", p, lambda j: x[:, p * 2 + j, :], lambda j: xn5[j], 1e-5)
                for n in range(3):
                    dve.wait_ge(*AC5.after(f"silu{n}", p))
                    dve.wait_ge(*PE5.after(f"u{n}", p))
                    nc.vector.tensor_tensor(h5[:, 2 * n:2 * n + 2, :], sg5[:, 2 * n:2 * n + 2, :], view(bank[3 + n], "p (c t) -> p c t", c=2),
                                            ALU.mult).then_inc(VE5.done(f"h{n}"), 1)
                for j in range(2):
                    dve.wait_ge(*PE5.after(f"down{j}", p))
                    nc.vector.scalar_tensor_tensor(x[:, p * 2 + j, :], bank[7 - j][:, 0:D], 1.0 / 127.0 ** 2, x[:, p * 2 + j, :],
                                                   ALU.mult, ALU.add).then_inc(VE5.done(f"x{j}"), 1)

        @block.tensor
        def _(pe):
            def mm(o, l, r, first=True, last=True):
                return nc.tensor.matmul(o, l, r, start=first, stop=last)

            pe.sem_inc(PE1.sem, PE1.round())
            pe.wait_ge(weights1_in, 16 * 8)
            with pe.Fori(0, NPAIR) as p:
                def transpose_xn(tag, ln):
                    for j in range(2):
                        pe.wait_ge(*VE1.after(f"{ln}_norm{j}", p))
                        for k in range(2):
                            last = nc.tensor.transpose(bank[0][:, k * PW + j * P:k * PW + (j + 1) * P],
                                                       xn[j][:, k * P:(k + 1) * P], ident)
                    last.then_inc(PE1.done(tag), 1)

                pe.wait_ge(*AC1.after("xnT_C", p - 1))
                transpose_xn("trA", "lnA")
                pe.wait_ge(*AC1.after("xnT_A", p))
                pe.wait_ge(*VE1.after("kv_evac0_1", p - 1))
                for o in range(2):
                    for k in range(2):
                        last = mm(bank[1][:, o * PW:(o + 1) * PW], wq[:, k, o * P:(o + 1) * P], xnT[:, k, :], k == 0, k == 1)
                last.then_inc(PE1.done("q"), 1)
                pe.wait_ge(*AC1.after("q_bias1", p))
                for o, m in ((0, P), (1, DC2 + 1)):
                    for k in range(2):
                        last = mm(bank[2][0:m, o * PW:(o + 1) * PW], wk[:, k, o * P:o * P + m], qT[:, k, :], k == 0, k == 1)
                last.then_inc(PE1.done("qk"), 1)
                pe.wait_ge(*AC1.after("qk_evac1", p))
                pe.wait_ge(*VE1.after("kv_evac1_1", p - 1))
                pe.wait_ge(*setup.sem_value("ones_l1"))
                for j in range(2):
                    pe.wait_ge(ctx_in[j], (p + 1) * CTX1)
                    for b in range(BT):
                        mm(bank[3 + j][S * b:S * b + S, 0:KEYS], qpT[:, 0, j * P + S * b:j * P + S * b + S],
                           cT1[j][:, b, :], True, False)
                    for b in range(BT):
                        last = mm(bank[3 + j][S * b:S * b + S, 0:KEYS], qpT[0:DC2 + 1, 1, j * P + S * b:j * P + S * b + S],
                                  cT2[j][0:DC2 + 1, b, :], False, True)
                    last.then_inc(PE1.done(f"sc_{j}"), 1)
                for j in range(2):
                    pe.wait_ge(*AC1.after(f"exp{j}", p))
                    pe.wait_ge(*VE1.after(f"at_norm{j}", p - 1))
                    for c in range(2):
                        last = nc.tensor.transpose(bank[5 + j][:, c * P:(c + 1) * P], pr[j][:, c * P:(c + 1) * P], ident)
                    last.then_inc(PE1.done(f"pt_{j}"), 1)
                for j in range(2):
                    pe.wait_ge(*VE1.after(f"pT_evac{j}", p))
                    pe.wait_ge(*VE1.after("logits", p - 1))
                    for c in range(2):
                        for b in range(BT):
                            last = mm(bank[7 * j][S * b:S * b + S, 0:DC + 1], pT[j][:, c, S * b:S * b + S],
                                      cN[j][:, b, c, :], c == 0, c == 1)
                    last.then_inc(PE1.done(f"ov_{j}"), 1)
                for j in range(2):
                    pe.wait_ge(*VE1.after(f"ov_evac{j}", p))
                    nc.tensor.transpose(bank[1 + j][:, 0:P], op[j][:, 0:P], ident)
                    last = nc.tensor.transpose(bank[1 + j][0:DC2 + 1, P:2 * P], op[j][:, P:DC + 1], ident)
                    last.then_inc(PE1.done(f"ot_{j}"), 1)
                for j in range(2):
                    pe.wait_ge(*AC1.after(f"oT_evac1_{j}", p))
                    mm(bank[5 + j][:, 0:D], oT[j][:, 0, :], wv1, True, False)
                    mm(bank[5 + j][:, 0:D], oT[j][0:DC2 + 1, 1, :], wv2[0:DC2 + 1, :], False, True)\
                        .then_inc(PE1.done(f"wv_{j}"), 1)
                transpose_xn("trB", "lnB")
                pe.wait_ge(*AC1.after("xnT_B", p))
                for j in range(2):
                    pe.wait_ge(*VE1.after(f"x_attn{j}", p))
                    for k in range(2):
                        mm(bank[3 + j], xnT[:, k, j * P:(j + 1) * P], wqkv[:, k, 0:2 * D], k == 0, k == 1)
                    for k in range(2):
                        last = mm(bank[5 + j][:, 0:D], xnT[:, k, j * P:(j + 1) * P], wqkv[:, k, 2 * D:3 * D], k == 0, k == 1)
                    last.then_inc(PE1.done(f"qkv_{j}"), 1)
                for j in range(2):
                    pe.wait_ge(*AC1.after(f"softplus{j}", p))
                    pe.wait_ge(*VE1.after("unit1", p))
                    mm(bank[5 + j][:, D:2 * D], K["same"], fqk[j][:, D:2 * D]).then_inc(PE1.done(f"ks_{j}"), 1)
                    for hf in range(2):
                        mm(bank[1 + 2 * j + hf], fqk[j][:, D + hf * P:D + (hf + 1) * P],
                           view(vblk[j][:, hf, :, :], "p a b -> p (a b)")).then_inc(PE1.done(f"kv_{j}_{hf}"), 1)
                    for hf in range(2):
                        last = nc.tensor.transpose(bank[7 * j][:, hf * P:(hf + 1) * P], fqk[j][:, hf * P:(hf + 1) * P], ident)
                    last.then_inc(PE1.done(f"qt_{j}"), 1)
                for j in range(2):
                    pe.wait_ge(*AC1.after(f"qt_evac{j}", p))
                    pe.wait_ge(*VE1.after(f"kv_evac{j}_1", p))
                    pe.wait_ge(*VE1.after(f"den_mul{j}", p))
                    for hf in range(2):
                        for b in range(BT):
                            last = mm(bank[5 + j][S * b:S * b + S, hf * P:(hf + 1) * P], qtT[j][:, hf, S * b:S * b + S],
                                      kvm[j][:, hf, b, :])
                    last.then_inc(PE1.done(f"at_{j}"), 1)
                pe.wait_ge(*AC1.after("qt_evac0", p))
                pe.wait_ge(*GP1.after("xnT_all", p - 1))
                transpose_xn("trC", "lnC")
                pe.wait_ge(*AC1.after("xnT_C", p))
                for j in range(2):
                    for k in range(2):
                        last = mm(bank[7][:, j * E:(j + 1) * E], xnT[:, k, j * P:(j + 1) * P], wr[:, k, :], k == 0, k == 1)
                last.then_inc(PE1.done("lg"), 1)
            pe.wait_ge(*VE1.all(NPAIR))
            oneh_all = view(oneh, "p a b -> p (a b)")
            mm(bank[6][:, 0:NT * E], K["before"], oneh_all, True, False)
            for t in range(1, NT):
                last = mm(bank[6][:, t * E:NT * E], K["ones"], oneh_all[:, 0:(NT - t) * E], False, t == NT - 1)
            last.then_inc(SHP.done("rank"), 1)
            for t in range(NT):
                last = mm(bank[7][:, 0:E], K["ones"], oneh[:, t, :], t == 0, t == NT - 1)
            last.then_inc(SHP.done("count"), 1)
            pe.wait_ge(weights_sh, 48)
            pe.wait_ge(*GP1.all(NPAIR))
            for s in range(8):
                n, c = s // 4, s % 4
                if s >= 2:
                    pe.wait_ge(*SHV.sem_value(f"h{s - 2}"))
                for w, o in ((sg_w, 0), (su_w, 1)):
                    for k in range(2):
                        last = mm(bank[2 * (s % 2) + o], w[:, k, c * P:(c + 1) * P], xnT_all[:, k, n * 512:(n + 1) * 512], k == 0, k == 1)
                last.then_inc(SHP.done(f"gu{s}"), 1)
            for t in range(NT):
                pe.wait_ge(*SHV.sem_value("h3" if t < 4 else "h7"))
                if t >= 2:
                    pe.wait_ge(*SHV.sem_value(f"x{t - 2}"))
                for c in range(4):
                    last = mm(bank[4 + t % 2][:, 0:D], hs[:, c, t * P:(t + 1) * P], sd_w[:, c, :], c == 0, c == 3)
                last.then_inc(SHP.done(f"down{t}"), 1)
            pe.wait_ge(*SHV.sem_value("x7"))
            pe.wait_ge(*RT.sem_value("slot"))
            pe.sem_inc(PE2.sem, PE2.round())

            def expert_up(PEx, ACx, s, i, h, r):
                for k in range(2):
                    last = nc.tensor.transpose(bank[6 + h][:, k * P:(k + 1) * P], xg[r][:, k * P:(k + 1) * P], ident)
                last.then_inc(PEx.done("xt" + s), 1)
                pe.wait_ge(*ACx.after("xT" + s, i))
                for o in range(2):
                    for c in range(4):
                        for k in range(2):
                            last = mm(bank[2 * h + o][:, c * P:(c + 1) * P], ring_gu[r][:, k, o * F0 + c * P:o * F0 + (c + 1) * P],
                                      xgT[h][:, k, :], k == 0, k == 1)
                last.then_inc(PEx.done("gu" + s), 1)

            def expert_down(PEx, VEx, s, i, h, r):
                pe.wait_ge(*VEx.after("h" + s, i))
                for c in range(4):
                    last = mm(bank[4 + h][:, 0:D], eh[h][:, c, :], ring_dn[r][:, c, :], c == 0, c == 3)
                last.then_inc(PEx.done("dn" + s), 1)

            with pe.Fori(0, NR) as it:
                for r in range(RING):
                    pe.wait_ge(xg_in[r], it * 16 + 16)
                    pe.wait_ge(gu_in[r], it * 16 + 16)
                    expert_up(PE2, AC2, str(r), it, r % 2, r)
                    if r >= 1:
                        q = r - 1
                        pe.wait_ge(dn_in[q], it * 16 + 16)
                        pe.wait_ge(*VE2.after(f"y{q - 2}", it) if q >= 2 else VE2.after(f"y{q + 2}", it - 1))
                        expert_down(PE2, VE2, str(q), it, q % 2, q)
                q = RING - 1
                pe.wait_ge(dn_in[q], it * 16 + 16)
                pe.wait_ge(*VE2.after(f"y{q - 2}", it))
                expert_down(PE2, VE2, str(q), it, q % 2, q)
            n_over = pe.value_load(etab.bitcast(i32)[0:1, NOVF:NOVF + 1], min_val=0, max_val=NOVF)
            with pe.If(n_over > 0):
                pe.sem_inc(PEO.sem, PEO.round())
                pe.wait_ge(*VE2.all(NR))
                with pe.Fori(0, NOVF) as i:
                    pe.wait_ge(ovf_in, i * 48 + 48)
                    pe.wait_ge(*VEO.after("y", i - 1))
                    expert_up(PEO, ACO, "", i, 0, 0)
                    expert_down(PEO, VEO, "", i, 0, 0)
                pe.wait_ge(*VEO.all(NOVF))
            pe.wait_ge(weights3_in, 16 * 7)
            pe.sem_inc(PE3.sem, PE3.round())
            pe.wait_ge(*set3.sem_value("row_zero"))
            with pe.Fori(0, NPAIR) as p:
                pe.wait_ge(*AC3.after("o_evac0", p - 1))
                for j in range(2):
                    pe.wait_ge(*VE3.after(f"ln_norm{j}", p))
                    for k in range(2):
                        last = nc.tensor.transpose(bank[0][:, k * PW + j * P:k * PW + (j + 1) * P], xn3[j][:, k * P:(k + 1) * P], ident)
                last.then_inc(PE3.done("tr"), 1)
                pe.wait_ge(*AC3.after("xnT", p))
                pe.wait_ge(*AC3.after("ot_evac1", p - 1))
                for n in range(2):
                    for o in range(2 * n, 2 * n + 2):
                        for k in range(2):
                            last = mm(bank[2 + n][:, (o % 2) * PW:(o % 2 + 1) * PW], c_wq[:, k, o * P:(o + 1) * P], xnT3[:, k, :], k == 0, k == 1)
                    last.then_inc(PE3.done(f"q{n}"), 1)
                for h in range(H1):
                    pe.wait_ge(*AC3.after(f"q_evac{h // 4}", p))
                    if h >= 4:
                        pe.wait_ge(*VE3.after(f"qk_evac{h - 4}", p))
                    elif h < 2:
                        pe.wait_ge(*VE3.after(f"bias{h}", p - 1))
                    else:
                        pe.wait_ge(*VE3.after(f"opT_evac{NU - 4 + h}", p - 1))
                    mm(bank[4 + h % 4][:, 0:PW], c_wk[:, h, 0:P], q3[:, h // 2, :])
                    mm(bank[4 + h % 4][0:DC2, PW:2 * PW], c_wk[:, h, P:DC], q3[:, h // 2, :]).then_inc(PE3.done(f"qk{h}"), 1)
                pe.wait_ge(*AC3.after("o_evac1", p - 1))
                pe.wait_ge(*VE3.after("qk_evac7", p))
                for s in range(NU + 4):
                    if s < NU:
                        b, g = s // 2, s % 2
                        j = b // BT
                        if s % (NU // 2) == 0:
                            pe.wait_ge(ctx_in[j], (p + 1) * CTX3 + NPAIR * CTX1)
                        if s >= 2:
                            pe.wait_ge(*AC3.after(f"exp{s - 2}", p))
                        mm(bank[s % 2][:, 0:KEYS], qp3[:, 0, b, g * P:(g + 1) * P], cT1[j][:, b % BT, :], True, False)
                        mm(bank[s % 2][:, 0:KEYS], qp3[0:DC2 + 2, 1, b, g * P:(g + 1) * P], cT2[j][0:DC2 + 2, b % BT, :], False, True)\
                            .then_inc(PE3.done(f"sc{s}"), 1)
                    if 2 <= s < NU + 2:
                        u = s - 2
                        pe.wait_ge(*VE3.after(f"norm{u}", p))
                        if u >= 2:
                            pe.wait_ge(*AC3.after(f"pT_evac{u - 2}", p))
                        for c in range(2):
                            last = nc.tensor.transpose(bank[2 + u % 2][:, c * P:(c + 1) * P], pr3[u % 4][:, c * P:(c + 1) * P], ident)
                        last.then_inc(PE3.done(f"pt{u}"), 1)
                    if 3 <= s < NU + 3:
                        u = s - 3
                        b = u // 2
                        pe.wait_ge(*AC3.after(f"pT_evac{u}", p))
                        if u >= 2:
                            pe.wait_ge(*VE3.after(f"ov_evac{u - 2}", p))
                        for c in range(2):
                            last = mm(bank[4 + u % 2][:, 0:DC], pT3[u % 2][:, c, :], cN[b // BT][:, b % BT, c, 0:DC], c == 0, c == 1)
                        last.then_inc(PE3.done(f"ov{u}"), 1)
                    if s >= 4:
                        u = s - 4
                        pe.wait_ge(*VE3.after(f"ov_evac{u}", p))
                        if u >= 2:
                            pe.wait_ge(*VE3.after(f"opT_evac{u - 2}", p))
                        for c in range(2):
                            last = nc.tensor.transpose(bank[6 + u % 2][:, c * P:(c + 1) * P], op3[u % 2][:, c * P:(c + 1) * P], ident)
                        last.then_inc(PE3.done(f"opT{u}"), 1)
                for j in range(2):
                    pe.wait_ge(*VE3.after(f"opT_evac{NU // 2 * (j + 1) - 1}", p))
                    pe.wait_ge(*AC3.after(f"exp{NU - 2 + j}", p))
                    for h in range(H1):
                        o = bank[j][:, h * HD1:(h + 1) * HD1]
                        mm(o, view(oT3[j][:, 0, h, :, :], "p b s -> p (b s)"), c_wv[:, 0, h * HD1:(h + 1) * HD1], True, False)
                        last = mm(o, view(oT3[j][0:DC2, 1, h, :, :], "p b s -> p (b s)"), c_wv[0:DC2, 1, h * HD1:(h + 1) * HD1], False, True)
                    last.then_inc(PE3.done(f"o{j}"), 1)
                for j in range(2):
                    pe.wait_ge(*AC3.after(f"o_evac{j}", p))
                    for c in range(4):
                        last = nc.tensor.transpose(bank[2 + j][:, c * P:(c + 1) * P], o3[j][:, c * P:(c + 1) * P], ident)
                    last.then_inc(PE3.done(f"ot{j}"), 1)
                for j in range(2):
                    pe.wait_ge(*AC3.after(f"ot_evac{j}", p))
                    for c in range(4):
                        last = mm(bank[4 + j][:, 0:D], o3T[j][:, c, :], c_wo[:, c, :], c == 0, c == 3)
                    last.then_inc(PE3.done(f"wo{j}"), 1)
            pe.wait_ge(weights4_in, 16 * 10)
            pe.wait_ge(*set4.sem_value("A"))
            pe.sem_inc(PE4.sem, PE4.round())
            ZC, XC, DTC = 0, DIN, 2 * DIN + 2 * NST
            with pe.Fori(0, NPAIR) as p:
                pe.wait_ge(*VE4.after("u", p))
                pe.wait_ge(*AC4.after("decay1", p - 1))
                for j in range(2):
                    for k in range(2):
                        last = nc.tensor.transpose(bank[0][:, k * PW + j * P:k * PW + (j + 1) * P], u4[:, j, k * P:(k + 1) * P], ident)
                last.then_inc(PE4.done("tr"), 1)
                pe.wait_ge(*AC4.after("uT", p))
                pe.wait_ge(*VE4.after("x1", p - 1))
                for j in range(2):
                    for k in range(2):
                        last = mm(bank[6][:, j * HM:(j + 1) * HM], uT4[:, k, j * P:(j + 1) * P], m_in[:, k, DTC:DTC + HM], k == 0, k == 1)
                last.then_inc(PE4.done("dt"), 1)
                pe.wait_ge(*AC4.after("yT_evac1", p - 1))
                for n in (2, 0, 1):
                    for c in range(2):
                        for k in range(2):
                            last = mm(bank[1 + n][:, c * PW:(c + 1) * PW], m_in[:, k, XC + (2 * n + c) * P:XC + (2 * n + c + 1) * P],
                                      uT4[:, k, :], k == 0, k == 1)
                    last.then_inc(PE4.done(f"xbc{n}"), 1)
                for j in range(2):
                    for k in range(2):
                        last = mm(bank[4 + j], uT4[:, k, j * P:(j + 1) * P], m_in[:, k, ZC:ZC + DIN], k == 0, k == 1)
                    last.then_inc(PE4.done(f"z{j}"), 1)
                pe.wait_ge(*VE4.after("dtA", p))
                for j in range(2):
                    last = mm(bank[6][:, (2 + j) * HM:(3 + j) * HM], K["tri"], dts["dtA"][:, j, :])
                last.then_inc(PE4.done("cum"), 1)

                def cum_rows(j):
                    for h in range(HM):
                        last = mm(bank[(3, 0)[h // 4]][:, (h % 4) * P:(h % 4 + 1) * P],
                                  dts["dtA"][:, j, h:h + 1].broadcast_to((P, P)), K["tri"])
                    last.then_inc(PE4.done(f"cumT{j}"), 1)

                pe.wait_ge(*AC4.after("tap3_5", p))
                cum_rows(0)
                pe.wait_ge(*VE4.after("silu2", p))
                for j in range(2):
                    mm(bank[7][:, j * P:(j + 1) * P], cv[:, 4, j * P:(j + 1) * P], cv[:, 5, j * P:(j + 1) * P]).then_inc(PE4.done(f"G{j}"), 1)
                pe.wait_ge(*VE4.after("silu1", p))
                for j in range(2):
                    for c in range(4):
                        last = nc.tensor.transpose(bank[1 + j][:, c * P:(c + 1) * P], cv[:, c, j * P:(j + 1) * P], ident)
                    last.then_inc(PE4.done(f"xs{j}"), 1)
                pe.wait_ge(*AC4.after("relu0_7", p))
                cum_rows(1)
                for j in range(2):
                    pe.wait_ge(*VE4.after(f"M{j}", p))
                    pe.wait_ge(*VE4.after(f"xdt{j}", p))
                    pe.wait_ge(*VE4.after(f"z_silu{j}", p))
                    for h in range(HM):
                        last = mm(bank[4 + j][:, h * HDM:(h + 1) * HDM], dec[j][:, h, :], xdt[j][:, h * HDM:(h + 1) * HDM])
                    last.then_inc(PE4.done(f"y{j}"), 1)
                for j in range(2):
                    pe.wait_ge(*VE4.after(f"yz{j}", p))
                    for c in range(4):
                        last = nc.tensor.transpose(bank[1 + j][:, c * P:(c + 1) * P], y4[j][:, c * P:(c + 1) * P], ident)
                    last.then_inc(PE4.done(f"yT{j}"), 1)
                for j in range(2):
                    pe.wait_ge(*AC4.after(f"yT_evac{j}", p))
                    for c in range(4):
                        last = mm(bank[6 + j][:, 0:D], yT4[j][:, c, :], m_out[:, c, :], c == 0, c == 3)
                    last.then_inc(PE4.done(f"out{j}"), 1)
            pe.wait_ge(*ints.sem_value("int2"))
            pe.sem_inc(PE5.sem, PE5.round())
            with pe.Fori(0, NPAIR) as p:
                pe.wait_ge(*VE5.after("x1", p - 1))
                for j in range(2):
                    pe.wait_ge(*VE5.after(f"ln_norm{j}", p))
                    for k in range(2):
                        last = nc.tensor.transpose(bank[6][:, k * PW + j * P:k * PW + (j + 1) * P], xn5[j][:, k * P:(k + 1) * P], ident)
                last.then_inc(PE5.done("tr"), 1)
                pe.wait_ge(*AC5.after("xnT", p))
                for n in range(3):
                    pe.wait_ge(*VE5.after(f"h{n}", p - 1))
                    for w, o, tag in ((f_g, 0, "g"), (f_u, 3, "u")):
                        for c in (2 * n, 2 * n + 1):
                            for k in range(2):
                                last = mm(bank[o + n][:, (c % 2) * PW:(c % 2 + 1) * PW], w[:, k, c * P:(c + 1) * P], xnT5[:, k, :], k == 0, k == 1)
                        last.then_inc(PE5.done(f"{tag}{n}"), 1)
                for j in range(2):
                    for c in range(6):
                        if c % 2 == 0:
                            pe.wait_ge(*VE5.after(f"h{c // 2}", p))
                        last = mm(bank[7 - j][:, 0:D], h5[:, c, j * P:(j + 1) * P], f_d[:, c, :], c == 0, c == 5)
                    last.then_inc(PE5.done(f"down{j}"), 1)

        return high[0], all_steps


SBUF_COLS = 53200


def layouts(a):
    T = lambda w: np.ascontiguousarray(np.asarray(w).T)
    ctx = a["ctx_768"]
    first = ctx[:, :2 * P, :].reshape(NT, BT, 2, P, DC)
    return {
        "consts": host_constants()[0],
        "x": a["x"].reshape(TOK, D),
        "ctx_T": np.ascontiguousarray(ctx.reshape(NT, BT, KEYS, DC).transpose(0, 3, 1, 2)),
        "ctx_N": np.ascontiguousarray(first.transpose(0, 3, 1, 2, 4)).reshape(NT, P, 2 * BT, DC),
        "ctx_last": np.ascontiguousarray(ctx[:, KEYS - 1, :]),
        "mask": a["mask_BxS2_bk0"],
        "wq": T(a["L0_xattn_Wq"]), "bq": T(a["L0_xattn_bq"].reshape(2, P)),
        "wk": np.concatenate([a["L0_xattn_Wk"], a["L0_xattn_bk"][:, None]], 1),
        "wv": np.concatenate([T(a["L0_xattn_Wv"]), a["L0_xattn_bv"][None, :]], 0),
        "wqkv": T(a["L0_attn_W_qkv"]), "wr": T(a["L0_ffn_w_router"]),
        "s_g": T(a["L0_ffn_w_gate"]), "s_u": T(a["L0_ffn_w_up"]), "s_d": T(a["L0_ffn_w_down"]),
        "c_wq": a["L1_xattn_W_q"], "c_wk": T(a["L1_xattn_W_k"]), "c_wv": a["L1_xattn_W_v"], "c_wo": a["L1_xattn_W_o"],
        "c_bo": a["L1_xattn_b_o"],
        "m_in": T(a["L1_attn_in_proj_w"]), "m_out": T(a["L1_attn_out_proj_w"]), "m_lnw": a["L1_attn_ln_w"],
        "m_lnb": a["L1_attn_ln_b"], "m_D": a["L1_attn_D"], "m_dtb": a["L1_attn_dt_bias"], "m_A": a["L1_attn_A_log"],
        "m_conv": a["L1_attn_conv_w"], "m_cb": T(a["L1_attn_conv_b"].reshape(NCH, P)), "m_nw": T(a["L1_attn_norm_w"].reshape(4, P)),
        "f_g": T(a["L1_ffn_w_gate"]), "f_u": T(a["L1_ffn_w_up"]), "f_d": T(a["L1_ffn_w_down"]),
        "e_gu": a["L0_ffn_gate_up_proj"], "e_dn": a["L0_ffn_down_proj"],
    }


def build(nc, arrays):
    I = {k: nc.dram_tensor("in_" + k, v.shape, mybir.dt.from_np(v.dtype), kind="ExternalInput").ap() for k, v in arrays.items()}
    out = nc.dram_tensor("out_x", (TOK, D), mybir.dt.float32, kind="ExternalOutput").ap()
    return perceiver_kernel(nc, I, out)


def kernel(**inputs):
    import concourse.bacc as bacc
    from concourse.bass_utils import run_bass_kernel_spmd

    arrays = layouts({k: np.asarray(v) for k, v in inputs.items()})
    nc = bacc.Bacc("TRN2", target_bir_lowering=False, num_devices=1)
    build(nc, arrays)
    r = run_bass_kernel_spmd(nc, [{"in_" + k: v for k, v in arrays.items()}], core_ids=[0])
    return r.results[0]["out_x"].reshape(B, S, D)
```

```python
import concourse.bass as bass
from concourse import mybir
from contextlib import ExitStack
import numpy as np

ORDER = {
    "setup_vector": """
        ones0 ones1 ones_n0 ones_l0 ones_n1 ones_l1 zero negmask""",
    "attn0_tensor": """
        trA q qk sc_0 sc_1 pt ov_0 ov_1 ot_0 ot_1 wv_0 wv_1""",
    "attn0_scalar": """
        xnT_A q_bias0 q_bias1 qk_evac0 qk_evac1 exp0 exp1 oT_evac0_0 oT_evac1_0 oT_evac0_1 oT_evac1_1""",
    "attn0_vector": """
        lnA_stats0 lnA_stats1 lnA_mean0 lnA_mean1 lnA_var lnA_norm0 lnA_norm1 row_max0 row_max1 pT_evac rsum
        ov_evac0 ov_evac1 x_attn0 x_attn1""",
    "attn0_gpsimd": """
        lnA_rstd""",
    "norm_tensor": """
        trB""",
    "norm_scalar": """
        xnT_B""",
    "norm_vector": """
        lnB_stats0 lnB_stats1 lnB_mean0 lnB_mean1 lnB_var lnB_norm0 lnB_norm1""",
    "norm_gpsimd": """
        lnB_rstd""",
    "linear_tensor": """
        qkv_0 qkv_1 qt ks kv_0_0 kv_0_1 kv_1_0 kv_1_1 at trC""",
    "linear_scalar": """
        square0 square1 vblk0_0 vblk0_1 vblk0_2 vblk0_3 sp_exp0 sp_exp1 vblk1_0 vblk1_1 vblk1_2 vblk1_3 softplus0
        softplus1 qt_evac xnT_C""",
    "linear_vector": """
        ss0 ss1 ss_max rn_half rn_y0 rn_yy0 rn_syy0 rn_y1 rn_yy1 rn_syy1 rn_y2 rn_yy2 rn_syy2 rn_y3 unit0 unit1
        den_mul kv_evac0_0 kv_evac0_1 den rden kv_evac1_0 kv_evac1_1 at_norm x_lin lnC_stats0 lnC_stats1 lnC_mean0
        lnC_mean1 lnC_var lnC_norm0 lnC_norm1 xm0 xm1""",
    "linear_gpsimd": """
        lnC_rstd xnT_all""",
    "routing_vector": """
        logits top tops tops_down down expert onehot gate_1p gate rank_oh over7 rank novf q7 oend q obase e7 base_oh
        etab_sum base etab_min etab_n t1 etab past t2 t3 tile slot1 slot2 slot""",
    "shared_tensor": """
        lg gu0 gu1 rank count gu2 gu3 gu4 gu5 gu6 gu7 down0 down1 down2 down3 down4 down5 down6 down7""",
    "shared_scalar": """
        gate_exp xm0 xm1 xm2 xm3 xm4 xm5 xm6 xm7 silu0 silu1 silu2 silu3 silu4 silu5 silu6 silu7""",
    "shared_vector": """
        h0 h1 h2 h3 h4 h5 h6 h7 x0 x1 x2 x3 x4 x5 x6 x7""",
    "experts_tensor": """
        xt0 gu0 xt1 gu1 dn0 xt2 gu2 dn1 xt3 gu3 dn2 dn3""",
    "experts_scalar": """
        xT0 silu0 xT1 silu1 xT2 silu2 xT3 silu3""",
    "experts_vector": """
        h0 y0 h1 y1 h2 y2 h3 y3""",
    "overflow_tensor": """
        xt gu dn""",
    "overflow_scalar": """
        xT silu""",
    "overflow_vector": """
        h y""",
    "x_experts_vector": """
        x0 x1 x2 x3 x4 x5 x6 x7""",
    "attn1_tensor": """
        tr q0 q1 qk0 qk1 qk2 qk3 qk4 qk5 qk6 qk7 sc0 sc1 sc2 pt0 sc3 pt1 ov0 sc4 pt2 ov1 opT0 sc5 pt3 ov2 opT1 sc6
        pt4 ov3 opT2 sc7 pt5 ov4 opT3 sc8 pt6 ov5 opT4 sc9 pt7 ov6 opT5 sc10 pt8 ov7 opT6 sc11 pt9 ov8 opT7 sc12
        pt10 ov9 opT8 sc13 pt11 ov10 opT9 sc14 pt12 ov11 opT10 sc15 pt13 ov12 opT11 pt14 ov13 opT12 pt15 ov14 opT13
        ov15 opT14 opT15 o0 o1 ot0 ot1 wo0 wo1""",
    "attn1_scalar": """
        xnT q_evac0 q_evac1 qk_evac0 qk_evac1 qk_evac2 qk_evac3 qk_evac4 qk_evac5 qk_evac6 qk_evac7 exp0 exp1 exp2
        pT_evac0 exp3 pT_evac1 exp4 pT_evac2 exp5 pT_evac3 exp6 pT_evac4 exp7 pT_evac5 exp8 pT_evac6 exp9 pT_evac7
        exp10 pT_evac8 exp11 pT_evac9 exp12 pT_evac10 exp13 pT_evac11 exp14 pT_evac12 exp15 pT_evac13 pT_evac14
        pT_evac15 o_evac0 o_evac1 ot_evac0 ot_evac1""",
    "attn1_vector": """
        ln_stats0 ln_stats1 ln_mean0 ln_mean1 ln_var ln_norm0 ln_norm1 qk_evac0 qk_evac1 qk_evac2 qk_evac3 qk_evac4
        qk_evac5 qk_evac6 qk_evac7 row_max0 row_max1 rsum0 norm0 row_max2 rsum1 norm1 row_max3 rsum2 norm2 ov_evac0
        row_max4 rsum3 norm3 ov_evac1 opT_evac0 row_max5 rsum4 norm4 ov_evac2 opT_evac1 row_max6 rsum5 norm5
        ov_evac3 opT_evac2 row_max7 rsum6 norm6 ov_evac4 opT_evac3 row_max8 rsum7 norm7 ov_evac5 opT_evac4 row_max9
        rsum8 norm8 ov_evac6 opT_evac5 row_max10 rsum9 norm9 ov_evac7 opT_evac6 row_max11 rsum10 norm10 ov_evac8
        opT_evac7 row_max12 rsum11 norm11 ov_evac9 opT_evac8 row_max13 rsum12 norm12 ov_evac10 opT_evac9 row_max14
        rsum13 norm13 ov_evac11 opT_evac10 row_max15 rsum14 norm14 ov_evac12 opT_evac11 rsum15 norm15 ov_evac13
        opT_evac12 ov_evac14 opT_evac13 ov_evac15 opT_evac14 opT_evac15 bias0 bias1 x0 x1""",
    "attn1_gpsimd": """
        ln_rstd""",
    "attn1_setup_vector": """
        op_zero0 op_zero1 rows_one row_zero""",
    "scan_tensor": """
        tr dt xbc2 xbc0 xbc1 z0 z1 cum cumT0 G0 G1 xs0 xs1 cumT1 y0 y1 yT0 yT1 out0 out1""",
    "scan_scalar": """
        uT xp2 tap3_4 tap3_5 xp0 tap3_0 tap3_1 xp1 tap3_2 tap3_3 dt_exp z_tanh0 z_tanh1 tanh2 tanh0 tanh1 relu0_0
        relu0_1 relu0_2 relu0_3 relu0_4 relu0_5 relu0_6 relu0_7 decay0 relu1_0 relu1_1 relu1_2 relu1_3 relu1_4
        relu1_5 relu1_6 relu1_7 decay1 xs_evac0 xs_evac1 square0 square1 yT_evac0 yT_evac1""",
    "scan_vector": """
        ln1_stats0 ln1_stats1 ln1_mean0 ln1_mean1 ln1_var ln1_norm0 ln1_norm1 ln2_stats0 ln2_stats1 ln2_mean0
        ln2_mean1 ln2_var ln2_norm0 ln2_norm1 ln_w u dt_raw dt_abs dt_pos tap0_4 tap0_5 tap1_4 tap1_5 tap2_4 tap2_5
        dt_2e dt_r dt_s dt_s2 dt_p15 dt_p13 dt_p11 dt_p9 dt_p7 dt_p5 dt_p3 dt_p1 dt dtA tap0_0 tap0_1 tap1_0 tap1_1
        tap2_0 tap2_1 tap0_2 tap0_3 tap1_2 tap1_3 tap2_2 tap2_3 silu2 cum silu0 silu1 z_silu0 z_silu1 gm0 gm1 M0 M1
        xdt0 xdt1 ya0 ya1 yz0 yz1 xr0 xr1 mean_square x0 x1""",
    "scan_gpsimd": """
        ln1_rstd ln2_rstd xD0 xD1 rms""",
    "scan_setup_vector": """
        pad nw0 nw1 nw2 nw3 D A""",
    "scan_setup_scalar": """
        expA""",
    "ffn_tensor": """
        tr g0 u0 g1 u1 g2 u2 down0 down1""",
    "ffn_scalar": """
        xnT silu0 silu1 silu2""",
    "ffn_vector": """
        ln_stats0 ln_stats1 ln_mean0 ln_mean1 ln_var ln_norm0 ln_norm1 h0 h1 h2 x0 x1""",
    "ffn_gpsimd": """
        ln_rstd""",
    "ffn_weights_float": """
        int0 int1 int2""",
}
ORDER = {k: v.split() for k, v in ORDER.items()}

P = 128
B, S, D = 32, 32, 256
TOK = B * S
NT = TOK // P
BT = P // S
KEYS, DC = 257, 192
DC2 = DC - P
NPAIR = NT // 2
PW = 2 * P
H0, HD0 = 16, 16
E, F0 = 16, 512
RING = 4
NOVF = (TOK - 1) // P
H1, HD1 = 8, 64
INNER = H1 * HD1
HM, HDM, NST = 8, 64, 128
DIN = HM * HDM
TAPS = 4
NCH = (DIN + 2 * NST) // P
F1 = 768
MASKED = -(2.0 ** 127)


class Steps:

    def __init__(self, name, sem):
        self.key, self.sem, self.n = name, sem, 0
        self.known = ORDER.get(name)
        self.names = list(self.known or [])

    def done(self, name):
        if self.known:
            assert self.names[self.n % len(self.names)] == name, (self.key, name, self.names[self.n % len(self.names)])
        else:
            self.names += [name] * (name not in self.names)
        self.n += 1
        return self.sem

    def after(self, name, rnd=0):
        if not self.known:
            return self.sem, 1
        return self.sem, (rnd + 1) * len(self.names) + (self.names.index(name) + 1)

    def sem_value(self, name):
        return self.sem, (self.names.index(name) + 1 if self.known else 1)

    def all(self, rounds=1):
        return self.sem, (rounds + 1) * max(len(self.names), 1)

    def round(self):
        return max(len(self.names), 1)


def host_constants():
    s = np.arange(P)
    same = (s[:, None] // S) == (s[None, :] // S)
    parts = {
        "ident": np.eye(P),
        "tri": same & (s[:, None] <= s[None, :]),
        "gmask": (same & (s[:, None] <= s[None, :])) / 16.0,
        "same": same,
        "before": s[:, None] < s[None, :],
        "hmask": ((s[:, None] // HD0) == (s[None, :] // HD0)) * HD0 ** -0.5,
        "ones": np.ones((P, P)),
        "inb": (s[:, None] // S) == np.arange(BT)[None, :],
        "iota": np.tile(np.arange(E), (P, 1)),
        "down": np.tile(E - np.arange(E), (P, 1)),
        "caps": np.tile(P * np.arange(1, NT), (P, 1)),
        "nth": np.tile(np.arange(NOVF), (P, 1)),
        "mhalf": np.full((P, 64), -0.5),
        "zeros": np.zeros((P, E)),
    }
    at, cols = {}, 0
    for k, v in parts.items():
        at[k] = (cols, v.shape[1])
        cols += v.shape[1]
    return np.concatenate([np.asarray(v, np.float32) for v in parts.values()], 1), at


def perceiver_kernel(nc, I, out):
    fp32, i32, u32, u8 = mybir.dt.float32, mybir.dt.int32, mybir.dt.uint32, mybir.dt.uint8
    ALU, ACT, AX = mybir.AluOpType, mybir.ActivationFunctionType, mybir.AxisListType.X
    _, CONST = host_constants()
    ctx = ExitStack()
    with ctx:
        big = ctx.enter_context(nc.sbuf_tensor("big", [P, SBUF_COLS], fp32))
        ps = ctx.enter_context(nc.psum_tensor("ps", [P, 8, 512], fp32))
        high = [0]

        def region(start):
            at = [start]

            def take(*dims):
                n = int(np.prod(dims))
                v = big[:, at[0]:at[0] + n]
                at[0] += n + (n & 1)
                high[0] = max(high[0], at[0])
                if len(dims) == 2:
                    v = v.rearrange("p (a b) -> p a b", b=dims[1])
                elif len(dims) == 3:
                    v = v.rearrange("p (a b c) -> p a b c", b=dims[1], c=dims[2])
                elif len(dims) == 4:
                    v = v.rearrange("p (a b c d) -> p a b c d", b=dims[1], c=dims[2], d=dims[3])
                return v
            return take, at

        keep, at = region(0)
        x = keep(NT, D)
        const = keep(CONST["zeros"][0] + CONST["zeros"][1])
        K = {k: const[:, a:a + n] for k, (a, n) in CONST.items()}
        ident = K["ident"]
        LN, LNX, LNB = ((keep(2, 6), keep(2, 2), keep(2), keep(2)) for _ in range(3))
        oneh, eidx = keep(NT, E), keep(NT)
        negmask, zrow = keep(KEYS), keep(D)
        etab = keep(NOVF + 1)
        mask8 = keep(66)
        cT1 = [keep(BT, KEYS) for _ in range(2)]
        cT2 = [keep(BT, KEYS) for _ in range(2)]
        cN = [keep(BT, 2, DC + 1) for _ in range(2)]
        cLq = [keep(DC + 1) for _ in range(2)]
        cLb = [keep(BT, DC) for _ in range(2)]
        w0 = at[0]
        wts, at = region(w0)
        wq, bq, wk, wv1, wv2 = wts(2, D), wts(2), wts(2, DC + 1), wts(D), wts(D)
        wqkv, wr = wts(2, 3 * D), wts(2, E)
        sg_w, su_w, sd_w = wts(2, F0), wts(2, F0), wts(4, D)
        w1 = at[0]
        ring_gu = [wts(2, 2 * F0) for _ in range(RING)]
        ring_dn = [wts(4, D) for _ in range(RING)]
        w2 = at[0]
        w4, at4 = region(w0)
        m_in, m_out = w4(2, 2 * DIN + 2 * NST + HM), w4(4, D)
        m_lnw, m_lnb, m_D, m_conv, m_cb = w4(D), w4(D), w4(HM), w4(NCH, TAPS), w4(NCH)
        m_nw, m_dtb, m_A = w4(4), w4(HM), w4(HM)
        assert at4[0] <= w1, (at4[0], w1)
        w5, at5 = region(w1)
        f_gi, f_ui, f_di = w5(2, F1), w5(2, F1), w5(6, D)
        f_g, f_u, f_d = w5(2, F1), w5(2, F1), w5(6, D)
        assert at5[0] <= w2, (at5[0], w2)
        w3, at = region(w2)
        c_wq, c_wk, c_wv, c_wo, c_bo = w3(2, INNER), w3(H1, DC), w3(2, INNER), w3(4, D), w3(D)
        work0 = at[0]
        a12, at = region(work0)
        xm, xnT_all = a12(NT, D), a12(2, TOK)
        lg, lg_top, gate = a12(NT, E), a12(NT), a12(NT)
        work1 = at[0]
        a1, _ = region(work1)
        xnx, xn = ([a1(D) for _ in range(2)] for _ in range(2))
        xnT_x, xnT_a, xnT, qT, qpT = (a1(2, PW) for _ in range(5))
        pr = [a1(KEYS) for _ in range(2)]
        nmx, sm, ri = a1(2), a1(2), a1(2)
        pT = a1(2, 2, P)
        op = [a1(DC + 1) for _ in range(2)]
        oT = [a1(2, P) for _ in range(2)]
        ss, rn, rt = a1(2, 32), a1(2, 32), a1(2, 32)
        fqk2 = a1(2, 512)
        fqk = [fqk2[:, j, :] for j in range(2)]
        vblk = [a1(2, BT, P) for _ in range(2)]
        kvm = [a1(2, BT, P) for _ in range(2)]
        dtmp = a1(2, D)
        den = a1(32)
        qtT = a1(2, 2, P)

        a2, _ = region(work1)
        hs = a2(4, TOK)
        sgate = [a2(F0) for _ in range(2)]
        xg = [a2(D) for _ in range(RING)]
        xgT = [a2(2, P) for _ in range(2)]
        egate = [a2(4, P) for _ in range(2)]
        eh = [a2(4, P) for _ in range(2)]
        ey = [a2(D) for _ in range(RING)]
        r_oh, rank, cnt7, novf, oend, obase = a2(NT, E), a2(NT), a2(E, NT - 1), a2(E), a2(E), a2(E)
        r_q7, rq, r_bt, r_g, r_t, slot_f, slot_i = a2(NT, NT - 1), a2(NT), a2(NT), a2(NT), a2(NT), a2(NT), a2(NT)
        r_e7, etab_f = a2(NOVF, E), a2(NOVF + 1)
        yg = xm

        a3, _ = region(work0)
        xn3 = [a3(D) for _ in range(2)]
        xnT3, q3 = a3(2, PW), a3(4, PW)
        qp3 = a3(2, 2 * BT, H1 * S)
        pr3 = [a3(KEYS) for _ in range(4)]
        nmx3, sm3, rs3 = a3(4), a3(4), a3(4)
        pT3 = [a3(2, P) for _ in range(2)]
        op3 = [a3(2 * P) for _ in range(2)]
        oT3 = [a3(2, H1, BT, S) for _ in range(2)]
        o3 = [a3(INNER) for _ in range(2)]
        o3T = [a3(4, P) for _ in range(2)]
        t3 = [a3(D) for _ in range(2)]

        a4, _ = region(work0)
        xn4, u4, uT4 = a4(2, D), a4(2, D), a4(2, PW)
        xp = a4(NCH, 2 * BT, S + TAPS - 1)
        cv, th = a4(NCH, PW), a4(NCH, PW)
        xs4, xdt, xD = ([a4(DIN) for _ in range(2)] for _ in range(3))
        zt, zs, y4 = ([a4(DIN) for _ in range(2)] for _ in range(3))
        dec = [a4(HM, P) for _ in range(2)]
        gm4 = [a4(P) for _ in range(2)]
        yT4 = [a4(4, P) for _ in range(2)]
        dts = {n: a4(2, HM) for n in ("d", "a", "m", "e", "e2", "r", "s", "s2", "p", "dt", "dtA", "cum")}
        ssq, rms = a4(2), a4(2)
        a5, _ = region(work0)
        xn5 = [a5(D) for _ in range(2)]
        xnT5, sg5, h5 = a5(2, PW), a5(6, PW), a5(6, PW)

        bank = [ps[:, n, :] for n in range(8)]

        def sem(name):
            return ctx.enter_context(nc.semaphore(name))

        all_steps = []

        def steps(name):
            all_steps.append(Steps(name, sem(name + "_done")))
            return all_steps[-1]

        weights1_in, weights2_in, weights3_in, weights4_in, weights5_in = (sem(f"weights{n}_in") for n in range(1, 6))
        x_in = sem("x_in")
        ctx_in = [sem(f"ctx_in{j}") for j in range(2)]
        x_out = sem("x_out")
        setup = steps("setup_vector")
        PEX, ACX, VEX, GPX = (steps("attn0_" + e) for e in ("tensor", "scalar", "vector", "gpsimd"))
        PEB, ACB, VEB, GPB = (steps("norm_" + e) for e in ("tensor", "scalar", "vector", "gpsimd"))
        PEL, ACL, VEL, GPL = (steps("linear_" + e) for e in ("tensor", "scalar", "vector", "gpsimd"))

        def view(a, pat, **kw):
            return a.rearrange(pat, **kw)

        tiles_dram = nc.dram_tensor("expert_in", ((E + NOVF) * P, D), fp32, kind="Internal").ap()
        ytiles_dram = nc.dram_tensor("expert_out", ((E + NOVF) * P, D), fp32, kind="Internal").ap()
        mask_dram = nc.dram_tensor("mask_add", (B, KEYS), fp32, kind="Internal").ap()
        zero_in, mask_out, scattered, gathered, weights_sh = (sem(n) for n in ("zero_in", "mask_out", "scattered", "gathered", "shared_weights_in"))
        gu_in = [sem(f"gate_up_in{r}") for r in range(RING)]
        dn_in = [sem(f"down_in{r}") for r in range(RING)]
        xg_in = [sem(f"expert_tokens_in{r}") for r in range(RING)]
        y_out, ovf_in, ovf_out = sem("expert_out_stored"), sem("overflow_in"), sem("overflow_out")
        RT, SHP, SHA, SHV = steps("routing_vector"), steps("shared_tensor"), steps("shared_scalar"), steps("shared_vector")
        PE2, AC2, VE2 = (steps("experts_" + e) for e in ("tensor", "scalar", "vector"))
        PEO, ACO, VEO = (steps("overflow_" + e) for e in ("tensor", "scalar", "vector"))
        XE = steps("x_experts_vector")
        NR = E // RING
        PE3, AC3, VE3, GP3 = (steps("attn1_" + e) for e in ("tensor", "scalar", "vector", "gpsimd"))
        set3 = steps("attn1_setup_vector")
        PE4, AC4, VE4, GP4 = (steps("scan_" + e) for e in ("tensor", "scalar", "vector", "gpsimd"))
        set4, set4a = steps("scan_setup_vector"), steps("scan_setup_scalar")
        PE5, AC5, VE5, GP5 = (steps("ffn_" + e) for e in ("tensor", "scalar", "vector", "gpsimd"))
        ints = steps("ffn_weights_float")
        wk_zero = sem("attn1_zero_done")
        NU = 2 * BT * 2
        CTX3 = 16 * 5

        passed = sem("waits_passed")

        def wait_alone(eng, semaphore, value):
            eng.wait_ge(semaphore, value)
            eng.sem_inc(passed, 1)

        def norm_stats(dve, V, tag, p, src, eps, scratch=LN):
            st, mv, ve, _ = scratch
            for j in range(2):
                nc.vector.bn_stats(st[:, j, :], src(j)).then_inc(V.done(f"{tag}_stats{j}"), 1)
            for j in range(2):
                wait_alone(dve, *V.after(f"{tag}_stats{j}", p))
                nc.vector.bn_aggr(mv[:, j, :], st[:, j, :]).then_inc(V.done(f"{tag}_mean{j}"), 1)
            dve.wait_ge(*V.after(f"{tag}_mean1", p))
            nc.vector.tensor_scalar_add(ve, mv[:, :, 1], eps).then_inc(V.done(f"{tag}_var"), 1)

        def norm_apply(dve, V, G, tag, p, src, dst, scratch=LN):
            _, mv, _, rstd = scratch
            dve.wait_ge(*G.after(f"{tag}_rstd", p))
            for j in range(2):
                nc.vector.tensor_scalar(dst(j), src(j), mv[:, j, 0:1], rstd[:, j:j + 1], ALU.subtract,
                                        ALU.mult).then_inc(V.done(f"{tag}_norm{j}"), 1)

        def layer_norm_vector(dve, V, G, tag, p, src, dst, eps):
            norm_stats(dve, V, tag, p, src, eps)
            norm_apply(dve, V, G, tag, p, src, dst)

        def layer_norm_gpsimd(pool, V, G, tag, p, scratch=LN):
            pool.wait_ge(*V.after(f"{tag}_var", p))
            nc.gpsimd.tensor_tensor(scratch[3], scratch[2], K["mhalf"][:, 0:2], ALU.pow).then_inc(G.done(f"{tag}_rstd"), 1)

        def load_expert(sp, r, e):
            if isinstance(e, int):
                gu, dn = I["e_gu"][e], I["e_dn"][e]
                sp.dma_start(ring_gu[r], gu.rearrange("(k p) n -> p k n", p=P)).then_inc(gu_in[r], 16)
                sp.dma_start(ring_dn[r], dn.rearrange("(k p) n -> p k n", p=P)).then_inc(dn_in[r], 16)
            else:
                sp.dma_start(ring_gu[r], I["e_gu"][bass.ds(e, 1), :, :].rearrange("a (k p) n -> p (a k) n", p=P)).then_inc(gu_in[r], 16)
                sp.dma_start(ring_dn[r], I["e_dn"][bass.ds(e, 1), :, :].rearrange("a (k p) n -> p (a k) n", p=P)).then_inc(dn_in[r], 16)

        def load_tokens(sp, r, it):
            sp.wait_ge(scattered, 16 * NT)
            sp.dma_start(xg[r], tiles_dram[bass.ds(it * (RING * P) + r * P, P), :]).then_inc(xg_in[r], 16)

        def load_context3(sp, j, t):
            load_context(sp, j, t)
            sp.dma_start(cT2[j][DC2 + 1:DC2 + 2], mask_dram[bass.ds(t * BT, BT), :].unsqueeze(0)).then_inc(ctx_in[j], 16)
            sp.dma_start(view(cLb[j], "p a b -> p (a b)"),
                         I["ctx_last"].rearrange("(t b) d -> t (b d)", b=BT)[bass.ds(t, 1), :].partition_broadcast(P)).then_inc(ctx_in[j], 16)

        def load_context(sp, j, t):
            sp.dma_start(cT1[j], I["ctx_T"][t, 0:P, :, :]).then_inc(ctx_in[j], 16)
            sp.dma_start(cT2[j][0:DC2], I["ctx_T"][t, P:DC, :, :]).then_inc(ctx_in[j], 16)
            sp.dma_start(cN[j].rearrange("p b c d -> p (b c) d")[:, :, 0:DC], I["ctx_N"][t]).then_inc(ctx_in[j], 16)

        SC, OV, OT, WV, KV = (0, 3), (2, 0), (3, 1), (2, 0), ((5, 6), (4, 5))
        CTX1 = 16 * (3 + BT)

        block = ctx.enter_context(nc.Block())

        @block.sync
        def _(sp):
            sp.dma_start(const, I["consts"]).then_inc(x_in, 16)
            sp.dma_start(x, I["x"].rearrange("(t p) d -> p t d", p=P)).then_inc(x_in, 16)
            for dst, src in ((wq, I["wq"]), (wk, I["wk"]), (wqkv, I["wqkv"]), (wr, I["wr"])):
                sp.dma_start(dst, src.rearrange("(k p) n -> p k n", p=P)).then_inc(weights1_in, 16)
            sp.dma_start(bq, I["bq"]).then_inc(weights1_in, 16)
            sp.dma_start(wv1, I["wv"][0:P, :]).then_inc(weights1_in, 16)
            sp.dma_start(wv2[0:DC2 + 1, :], I["wv"][P:DC + 1, :]).then_inc(weights1_in, 16)
            sp.dma_start(mask8[0:B, 0:65].bitcast(u8)[:, 0:KEYS], I["mask"]).then_inc(weights1_in, 16)

            for dst, src in ((sg_w, I["s_g"]), (su_w, I["s_u"]), (sd_w, I["s_d"])):
                sp.dma_start(dst, src.rearrange("(k p) n -> p k n", p=P)).then_inc(weights_sh, 16)
            with sp.Fori(0, NPAIR) as p:
                for j in range(2):
                    t = p * 2 + j
                    wait_alone(sp, *PEX.after(f"ov_{j}", p - 1))
                    wait_alone(sp, *VEX.after(f"ov_evac{j}", p - 1))
                    load_context(sp, j, t)
                    for b in range(BT):
                        sp.dma_start(cLq[j][S * b:S * b + S, 0:DC],
                                     I["ctx_last"][bass.ds(t * BT + b, 1), :].partition_broadcast(S)).then_inc(ctx_in[j], 16)
            for r in range(RING):
                load_expert(sp, r, r)
            sp.wait_ge(*setup.sem_value("zero"))
            sp.dma_start(tiles_dram.rearrange("(n p) d -> p n d", p=P), zrow.unsqueeze(1).broadcast_to((P, E + NOVF, D)))\
                .then_inc(zero_in, 16)
            sp.dma_start(ytiles_dram[E * P:, :].rearrange("(n p) d -> p n d", p=P), zrow.unsqueeze(1).broadcast_to((P, NOVF, D)))\
                .then_inc(zero_in, 16)
            sp.wait_ge(*setup.sem_value("negmask"))
            sp.dma_start(mask_dram, negmask[0:B, :]).then_inc(mask_out, 16)
            sp.wait_ge(*PEX.all(NPAIR))
            sp.wait_ge(*VEX.all(NPAIR))
            sp.wait_ge(mask_out, 16)
            for j in range(2):
                load_context3(sp, j, j)
            for dst, src in ((c_wq, I["c_wq"]), (c_wo, I["c_wo"])):
                sp.dma_start(dst, src.rearrange("(k p) n -> p k n", p=P)).then_inc(weights3_in, 16)
            sp.wait_ge(wk_zero, 1)
            for hp in range(2):
                sp.dma_start(view(c_wk, "p (g two) d -> p g two d", two=2)[hp * HD1:(hp + 1) * HD1, :, hp, :],
                             I["c_wk"].rearrange("(g two e) d -> e g two d", two=2, e=HD1)[:, :, hp, :]).then_inc(weights3_in, 16)
            sp.dma_start(c_wv[:, 0, :], I["c_wv"][0:P, :]).then_inc(weights3_in, 16)
            sp.dma_start(c_wv[0:DC2, 1, :], I["c_wv"][P:DC, :]).then_inc(weights3_in, 16)
            sp.dma_start(c_bo, I["c_bo"].partition_broadcast(P)).then_inc(weights3_in, 16)
            for r in range(RING):
                load_tokens(sp, r, 0)
            with sp.Fori(1, NR) as it:
                for r in range(RING):
                    sp.wait_ge(*PE2.after(f"dn{r}", it - 1))
                    load_expert(sp, r, it * RING + r)
                    load_tokens(sp, r, it)
            sp.wait_ge(*RT.sem_value("etab"))
            n_over = sp.value_load(etab.bitcast(i32)[0:1, NOVF:NOVF + 1], min_val=0, max_val=NOVF)
            with sp.If(n_over > 0):
                sp.wait_ge(*PE2.all(NR))
                with sp.Fori(0, NOVF) as i:
                    sp.wait_ge(*PEO.after("dn", i - 1))
                    e = sp.value_load(etab.bitcast(i32)[0:1, bass.ds(i, 1)], min_val=0, max_val=E - 1)
                    sp.dma_start(ring_gu[0], I["e_gu"][bass.ds(e, 1), :, :].rearrange("a (k p) n -> p (a k) n", p=P)).then_inc(ovf_in, 16)
                    sp.dma_start(ring_dn[0], I["e_dn"][bass.ds(e, 1), :, :].rearrange("a (k p) n -> p (a k) n", p=P)).then_inc(ovf_in, 16)
                    sp.dma_start(xg[0], tiles_dram[bass.ds(i * P + E * P, P), :]).then_inc(ovf_in, 16)
            sp.wait_ge(*XE.sem_value("x7"))
            sp.dma_start(m_in, I["m_in"].rearrange("(k p) n -> p k n", p=P)).then_inc(weights4_in, 16)
            sp.dma_start(m_out, I["m_out"].rearrange("(k p) n -> p k n", p=P)).then_inc(weights4_in, 16)
            for dst, src in ((m_lnw, "m_lnw"), (m_lnb, "m_lnb"), (m_D, "m_D"), (m_dtb, "m_dtb"), (m_A, "m_A")):
                sp.dma_start(dst, I[src].partition_broadcast(P)).then_inc(weights4_in, 16)
            sp.dma_start(m_conv, I["m_conv"].rearrange("(c p) t -> p c t", p=P)).then_inc(weights4_in, 16)
            sp.dma_start(m_cb, I["m_cb"]).then_inc(weights4_in, 16)
            sp.dma_start(m_nw, I["m_nw"]).then_inc(weights4_in, 16)
            for dst, src in ((f_gi, "f_g"), (f_ui, "f_u"), (f_di, "f_d")):
                sp.dma_start(dst.bitcast(i32), I[src].rearrange("(k p) n -> p k n", p=P)).then_inc(weights5_in, 16)
            with sp.Fori(1, NPAIR) as p:
                for j in range(2):
                    u = NU // 2 * (j + 1) - 1
                    wait_alone(sp, *PE3.after(f"ov{u}", p - 1))
                    wait_alone(sp, *VE3.after(f"ov_evac{u}", p - 1))
                    load_context3(sp, j, p * 2 + j)
            with sp.Fori(0, NPAIR) as p:
                sp.wait_ge(*VE5.after("x1", p))
                sp.dma_start(out.rearrange("(t p) d -> p t d", p=P)[:, bass.ds(p * 2, 2), :], x[:, bass.ds(p * 2, 2), :]).then_inc(x_out, 16)
            sp.wait_ge(x_out, 16 * NPAIR)

        @block.gpsimd
        def _(pool):
            nc.gpsimd.memset(view(c_wk, "p a b -> p (a b)"), 0.0).then_inc(wk_zero, 1)
            pool.sem_inc(GPX.sem, GPX.round())
            pool.sem_inc(GPL.sem, GPL.round())
            pool.sem_inc(GPB.sem, GPB.round())

            def linear_gpsimd(p, nxt):
                if nxt is not None:
                    layer_norm_gpsimd(pool, VEX, GPX, "lnA", nxt, LNX)
                if nxt is not None:
                    layer_norm_gpsimd(pool, VEB, GPB, "lnB", nxt, LNB)
                layer_norm_gpsimd(pool, VEL, GPL, "lnC", p)
                pool.wait_ge(*ACL.after("xnT_C", p))
                nc.gpsimd.tensor_copy(xnT_all[:, :, bass.ds(p * PW, PW)], xnT).then_inc(GPL.done("xnT_all"), 1)

            layer_norm_gpsimd(pool, VEX, GPX, "lnA", 0, LNX)
            layer_norm_gpsimd(pool, VEB, GPB, "lnB", 0, LNB)
            with pool.Fori(0, NPAIR - 1) as p:
                linear_gpsimd(p, p + 1)
            linear_gpsimd(NPAIR - 1, None)
            pool.wait_ge(zero_in, 32)
            pool.wait_ge(*RT.sem_value("slot"))
            pool.wait_ge(*SHA.sem_value(f"xm{NT - 1}"))
            for t in range(NT):
                pool.indirect_dma_start(out=tiles_dram, out_offset=bass.IndirectOffsetOnAxis(slot_i[:, t:t + 1].bitcast(i32), 0),
                                        in_=xm[:, t, :], in_offset=None).then_inc(scattered, 16)
            with pool.Fori(0, NR) as it:
                for r in range(RING):
                    pool.wait_ge(*VE2.after(f"y{r}", it))
                    pool.dma_start(ytiles_dram[bass.ds(it * (RING * P) + r * P, P), :], ey[r]).then_inc(y_out, 16)
            pool.wait_ge(y_out, 16 * E)
            n_over = pool.value_load(etab.bitcast(i32)[0:1, NOVF:NOVF + 1], min_val=0, max_val=NOVF)
            with pool.If(n_over > 0):
                with pool.Fori(0, NOVF) as i:
                    pool.wait_ge(*VEO.after("y", i))
                    pool.dma_start(ytiles_dram[bass.ds(i * P + E * P, P), :], ey[0]).then_inc(ovf_out, 16)
                pool.wait_ge(ovf_out, 16 * NOVF)
            pool.wait_ge(scattered, 16 * NT)
            for t in range(NT):
                pool.indirect_dma_start(out=yg[:, t, :], out_offset=None, in_=ytiles_dram,
                                        in_offset=bass.IndirectOffsetOnAxis(slot_i[:, t:t + 1].bitcast(i32), 0)).then_inc(gathered, 16)
            pool.sem_inc(GP3.sem, GP3.round())
            with pool.Fori(0, NPAIR) as p:
                layer_norm_gpsimd(pool, VE3, GP3, "ln", p)
            pool.wait_ge(weights5_in, 48)
            for n, (dst, src) in enumerate(((f_g, f_gi), (f_u, f_ui), (f_d, f_di))):
                nc.gpsimd.tensor_copy(dst, src.bitcast(i32)).then_inc(ints.done(f"int{n}"), 1)
            pool.sem_inc(GP4.sem, GP4.round())
            with pool.Fori(0, NPAIR) as p:
                layer_norm_gpsimd(pool, VE4, GP4, "ln1", p)
                layer_norm_gpsimd(pool, VE4, GP4, "ln2", p)
                for j in range(2):
                    pool.wait_ge(*AC4.after(f"xs_evac{j}", p))
                    if j == 0:
                        pool.wait_ge(*set4.sem_value("D"))
                    nc.gpsimd.tensor_tensor(view(xD[j], "p (h e) -> p h e", h=HM), view(xs4[j], "p (h e) -> p h e", h=HM),
                                            m_D.unsqueeze(2).broadcast_to((P, HM, HDM)), ALU.mult).then_inc(GP4.done(f"xD{j}"), 1)
                pool.wait_ge(*VE4.after("mean_square", p))
                nc.gpsimd.tensor_tensor(rms, ssq, K["mhalf"][:, 0:2], ALU.pow).then_inc(GP4.done("rms"), 1)
            pool.sem_inc(GP5.sem, GP5.round())
            with pool.Fori(0, NPAIR) as p:
                layer_norm_gpsimd(pool, VE5, GP5, "ln", p)

        @block.scalar
        def _(act):
            act.sem_inc(ACX.sem, ACX.round())
            act.sem_inc(ACL.sem, ACL.round())
            act.sem_inc(ACB.sem, ACB.round())
            act.wait_ge(weights1_in, 16 * 8)

            def xnT_evac(PEn, ACn, dst, bk, tag, pe_step, p):
                act.wait_ge(*PEn.after(pe_step, p))
                nc.scalar.copy(view(dst, "p a b -> p (a b)"), bk).then_inc(ACn.done(tag), 1)

            def queries(p):
                act.wait_ge(*PEX.after("q", p))
                for k in range(2):
                    nc.scalar.activation(qT[:, k, :], bank[1][:, k * PW:(k + 1) * PW], ACT.Identity,
                                         bias=bq[:, k:k + 1]).then_inc(ACX.done(f"q_bias{k}"), 1)

            def queries_keys(p):
                act.wait_ge(*PEX.after("qk", p))
                nc.scalar.mul(qpT[:, 0, :], bank[2][:, 0:PW], D ** -0.5).then_inc(ACX.done("qk_evac0"), 1)
                nc.scalar.mul(qpT[0:DC2 + 1, 1, :], bank[2][0:DC2 + 1, PW:2 * PW], D ** -0.5)\
                    .then_inc(ACX.done("qk_evac1"), 1)

            def probabilities(p):
                for j in range(2):
                    act.wait_ge(*VEX.after(f"row_max{j}", p))
                    nc.scalar.activation(pr[j], bank[SC[j]][:, 0:KEYS], ACT.Exp, bias=nmx[:, j:j + 1],
                                         accum_out=sm[:, j:j + 1]).then_inc(ACX.done(f"exp{j}"), 1)

            def context_sums(p):
                for j in range(2):
                    act.wait_ge(*PEX.after(f"ot_{j}", p))
                    nc.scalar.copy(oT[j][:, 0, :], bank[OT[j]][:, 0:P]).then_inc(ACX.done(f"oT_evac0_{j}"), 1)
                    nc.scalar.copy(oT[j][0:DC2 + 1, 1, :], bank[OT[j]][0:DC2 + 1, P:2 * P])\
                        .then_inc(ACX.done(f"oT_evac1_{j}"), 1)

            def linear_scalar(p, nxt):
                for j in range(2):
                    act.wait_ge(*PEL.after(f"qkv_{j}", p))
                    nc.scalar.activation(fqk[j], bank[5 + j], ACT.Square)\
                        .then_inc(ACL.done(f"square{j}"), 1)
                    if nxt is not None and j == 0:
                        xnT_evac(PEX, ACX, xnT_a, bank[0], "xnT_A", "trA", nxt)
                if nxt is not None:
                    queries(nxt)

                def value_blocks(j):
                    for b in range(BT):
                        nc.scalar.activation(vblk[j][:, :, b, :], view(bank[7][:, j * D:(j + 1) * D], "p (a b) -> p a b", b=P),
                                             ACT.Copy, scale=K["inb"][:, b:b + 1]).then_inc(ACL.done(f"vblk{j}_{b}"), 1)

                value_blocks(0)
                if nxt is not None:
                    queries_keys(nxt)
                for j in range(2):
                    act.wait_ge(*VEL.after(f"unit{j}", p))
                    nc.scalar.activation(fqk[j], fqk[j], ACT.Exp).then_inc(ACL.done(f"sp_exp{j}"), 1)
                value_blocks(1)
                if nxt is not None:
                    probabilities(nxt)
                for j in range(2):
                    act.wait_ge(*ACL.after(f"sp_exp{j}", p))
                    nc.scalar.activation(fqk[j], fqk[j], ACT.Ln, bias=K["ones"][:, 0:1]).then_inc(ACL.done(f"softplus{j}"), 1)
                act.wait_ge(*PEL.after("qt", p))
                nc.scalar.copy(view(qtT, "p a b c -> p (a b c)"), bank[4]).then_inc(ACL.done("qt_evac"), 1)
                if nxt is not None:
                    context_sums(nxt)
                if nxt is not None:
                    xnT_evac(PEB, ACB, xnT_x, bank[6], "xnT_B", "trB", nxt)
                act.wait_ge(*GPL.after("xnT_all", p - 1))
                xnT_evac(PEL, ACL, xnT, bank[4], "xnT_C", "trC", p)

            xnT_evac(PEX, ACX, xnT_a, bank[0], "xnT_A", "trA", 0)
            queries(0)
            queries_keys(0)
            probabilities(0)
            context_sums(0)
            xnT_evac(PEB, ACB, xnT_x, bank[6], "xnT_B", "trB", 0)
            with act.Fori(0, NPAIR - 1) as p:
                linear_scalar(p, p + 1)
            linear_scalar(NPAIR - 1, None)
            act.wait_ge(*RT.sem_value("top"))
            nc.scalar.activation(gate, lg_top, ACT.Exp, scale=-1.0).then_inc(SHA.done("gate_exp"), 1)
            act.wait_ge(*RT.sem_value("gate"))
            for t in range(NT):
                nc.scalar.activation(xm[:, t, :], xm[:, t, :], ACT.Copy, scale=gate[:, t:t + 1]).then_inc(SHA.done(f"xm{t}"), 1)
            for s in range(8):
                act.wait_ge(*SHP.sem_value(f"gu{s}"))
                if s >= 2:
                    act.wait_ge(*SHV.sem_value(f"h{s - 2}"))
                nc.scalar.activation(sgate[s % 2], bank[2 * (s % 2)], ACT.Silu).then_inc(SHA.done(f"silu{s}"), 1)
            act.sem_inc(AC2.sem, AC2.round())

            def expert_scalar(PEx, ACx, VEx, s, i, h):
                act.wait_ge(*PEx.after("xt" + s, i))
                nc.scalar.copy(view(xgT[h], "p a b -> p (a b)"), bank[6 + h][:, 0:D]).then_inc(ACx.done("xT" + s), 1)
                act.wait_ge(*PEx.after("gu" + s, i))
                nc.scalar.activation(view(egate[h], "p a b -> p (a b)"), bank[2 * h], ACT.Silu).then_inc(ACx.done("silu" + s), 1)

            with act.Fori(0, NR) as it:
                for r in range(RING):
                    if r < 2:
                        act.wait_ge(*VE2.after(f"h{r + 2}", it - 1))
                    else:
                        act.wait_ge(*VE2.after(f"h{r - 2}", it))
                    expert_scalar(PE2, AC2, VE2, str(r), it, r % 2)
            n_over = act.value_load(etab.bitcast(i32)[0:1, NOVF:NOVF + 1], min_val=0, max_val=NOVF)
            with act.If(n_over > 0):
                act.sem_inc(ACO.sem, ACO.round())
                act.wait_ge(*VE2.all(NR))
                with act.Fori(0, NOVF) as i:
                    expert_scalar(PEO, ACO, VEO, "", i, 0)
                act.wait_ge(*VEO.all(NOVF))
            act.sem_inc(AC3.sem, AC3.round())
            with act.Fori(0, NPAIR) as p:
                act.wait_ge(*PE3.after("tr", p))
                nc.scalar.copy(view(xnT3, "p a b -> p (a b)"), bank[0]).then_inc(AC3.done("xnT"), 1)
                for n in range(2):
                    act.wait_ge(*PE3.after(f"q{n}", p))
                    nc.scalar.copy(view(q3[:, 2 * n:2 * n + 2, :], "p a b -> p (a b)"), bank[2 + n]).then_inc(AC3.done(f"q_evac{n}"), 1)
                for h in range(H1):
                    act.wait_ge(*PE3.after(f"qk{h}", p))
                    nc.scalar.mul(qp3[:, 0, :, h * S:(h + 1) * S], view(bank[4 + h % 4][:, 0:PW], "p (b s) -> p b s", s=S),
                                  HD1 ** -0.5).then_inc(AC3.done(f"qk_evac{h}"), 1)
                for s in range(NU + 2):
                    if s < NU:
                        act.wait_ge(*VE3.after(f"row_max{s}", p))
                        if s >= 4:
                            act.wait_ge(*VE3.after(f"ov_evac{s - 4}", p))
                        nc.scalar.activation(pr3[s % 4], bank[s % 2][:, 0:KEYS], ACT.Exp, bias=nmx3[:, s % 4:s % 4 + 1],
                                             accum_out=sm3[:, s % 4:s % 4 + 1]).then_inc(AC3.done(f"exp{s}"), 1)
                    if s >= 2:
                        act.wait_ge(*PE3.after(f"pt{s - 2}", p))
                        nc.scalar.copy(view(pT3[s % 2], "p a b -> p (a b)"), bank[2 + s % 2][:, 0:2 * P])\
                            .then_inc(AC3.done(f"pT_evac{s - 2}"), 1)
                for j in range(2):
                    act.wait_ge(*PE3.after(f"o{j}", p))
                    nc.scalar.copy(o3[j], bank[j]).then_inc(AC3.done(f"o_evac{j}"), 1)
                for j in range(2):
                    act.wait_ge(*PE3.after(f"ot{j}", p))
                    nc.scalar.copy(view(o3T[j], "p a b -> p (a b)"), bank[2 + j]).then_inc(AC3.done(f"ot_evac{j}"), 1)
            act.wait_ge(weights4_in, 16 * 10)
            nc.scalar.activation(m_A, m_A, ACT.Exp).then_inc(set4a.done("expA"), 1)
            act.sem_inc(AC4.sem, AC4.round())
            with act.Fori(0, NPAIR) as p:
                act.wait_ge(*PE4.after("tr", p))
                nc.scalar.copy(view(uT4, "p a b -> p (a b)"), bank[0]).then_inc(AC4.done("uT"), 1)
                for n in (2, 0, 1):
                    act.wait_ge(*PE4.after(f"xbc{n}", p))
                    nc.scalar.copy(xp[:, 2 * n:2 * n + 2, :, TAPS - 1:TAPS - 1 + S],
                                   view(bank[1 + n], "p (c b s) -> p c b s", c=2, s=S)).then_inc(AC4.done(f"xp{n}"), 1)
                    for c in range(2):
                        nc.scalar.activation(cv[:, 2 * n + c, :], bank[1 + n][:, c * PW:(c + 1) * PW], ACT.Identity,
                                             bias=m_cb[:, 2 * n + c:2 * n + c + 1], scale=m_conv[:, 2 * n + c, TAPS - 1:TAPS])\
                            .then_inc(AC4.done(f"tap3_{2 * n + c}"), 1)
                act.wait_ge(*VE4.after("dt_abs", p))
                nc.scalar.activation(dts["e"], dts["a"], ACT.Exp, scale=-1.0).then_inc(AC4.done("dt_exp"), 1)
                for j in range(2):
                    act.wait_ge(*PE4.after(f"z{j}", p))
                    nc.scalar.activation(zt[j], bank[4 + j], ACT.Tanh, scale=0.5).then_inc(AC4.done(f"z_tanh{j}"), 1)
                for n in (2, 0, 1):
                    act.wait_ge(*VE4.after(f"tap2_{2 * n + 1}", p))
                    nc.scalar.activation(th[:, 2 * n:2 * n + 2, :], cv[:, 2 * n:2 * n + 2, :], ACT.Tanh, scale=0.5)\
                        .then_inc(AC4.done(f"tanh{n}"), 1)
                for j in range(2):
                    act.wait_ge(*VE4.after("cum", p))
                    act.wait_ge(*PE4.after(f"cumT{j}", p))
                    for h in range(HM):
                        nc.scalar.activation(dec[j][:, h, :], bank[(3, 0)[h // 4]][:, (h % 4) * P:(h % 4 + 1) * P], ACT.Relu,
                                             scale=-1.0, bias=dts["cum"][:, j, h:h + 1]).then_inc(AC4.done(f"relu{j}_{h}"), 1)
                    act.wait_ge(*AC4.after(f"relu{j}_7", p))
                    nc.scalar.activation(dec[j], dec[j], ACT.Exp, scale=-1.0).then_inc(AC4.done(f"decay{j}"), 1)
                for j in range(2):
                    act.wait_ge(*PE4.after(f"xs{j}", p))
                    nc.scalar.copy(xs4[j], bank[1 + j]).then_inc(AC4.done(f"xs_evac{j}"), 1)
                for j in range(2):
                    act.wait_ge(*VE4.after(f"yz{j}", p))
                    nc.scalar.activation(zt[j], y4[j], ACT.Square, accum_out=ssq[:, j:j + 1]).then_inc(AC4.done(f"square{j}"), 1)
                for j in range(2):
                    act.wait_ge(*PE4.after(f"yT{j}", p))
                    nc.scalar.copy(view(yT4[j], "p a b -> p (a b)"), bank[1 + j]).then_inc(AC4.done(f"yT_evac{j}"), 1)
            act.sem_inc(AC5.sem, AC5.round())
            with act.Fori(0, NPAIR) as p:
                act.wait_ge(*PE5.after("tr", p))
                nc.scalar.copy(view(xnT5, "p a b -> p (a b)"), bank[6]).then_inc(AC5.done("xnT"), 1)
                for n in range(3):
                    act.wait_ge(*PE5.after(f"g{n}", p))
                    nc.scalar.activation(sg5[:, 2 * n:2 * n + 2, :], view(bank[n], "p (c t) -> p c t", c=2), ACT.Silu, scale=1.0 / 127.0)\
                        .then_inc(AC5.done(f"silu{n}"), 1)

        @block.vector
        def _(dve):
            nc.vector.memset(view(cT2[0], "p a b -> p (a b)")[DC2:DC2 + 1, :], 1.0).then_inc(setup.done("ones0"), 1)
            nc.vector.memset(view(cT2[1], "p a b -> p (a b)")[DC2:DC2 + 1, :], 1.0).then_inc(setup.done("ones1"), 1)
            for j in range(2):
                nc.vector.memset(cN[j][:, :, :, DC:DC + 1], 1.0).then_inc(setup.done(f"ones_n{j}"), 1)
                nc.vector.memset(cLq[j][:, DC:DC + 1], 1.0).then_inc(setup.done(f"ones_l{j}"), 1)
            nc.vector.memset(zrow, 0.0).then_inc(setup.done("zero"), 1)
            dve.wait_ge(weights1_in, 16 * 8)
            nc.vector.tensor_scalar(negmask[0:B, :], mask8[0:B, 0:65].bitcast(u8)[:, 0:KEYS], 1.0, -MASKED, ALU.subtract,
                                    ALU.mult).then_inc(setup.done("negmask"), 1)
            dve.sem_inc(VEX.sem, VEX.round())
            dve.sem_inc(VEL.sem, VEL.round())
            dve.sem_inc(VEB.sem, VEB.round())
            dve.wait_ge(x_in, 32)
            dve.wait_ge(*setup.sem_value("ones_l1"))

            def tiles_of(p):
                return lambda j: x[:, p * 2 + j, :]

            def stats_attn(p):
                norm_stats(dve, VEX, "lnA", p, tiles_of(p), 1e-5, LNX)

            def apply_attn(p):
                wait_alone(dve, *PEB.after("trB", p - 1))
                norm_apply(dve, VEX, GPX, "lnA", p, tiles_of(p), lambda j: xnx[j], LNX)

            def row_maxima(p):
                for j in range(2):
                    dve.wait_ge(*PEX.after(f"sc_{j}", p))
                    nc.vector.reduce_max(nmx[:, j:j + 1], bank[SC[j]][:, 0:KEYS], AX, negate=True)\
                        .then_inc(VEX.done(f"row_max{j}"), 1)

            def probabilities_T(p):
                dve.wait_ge(*PEX.after("pt", p))
                nc.vector.tensor_copy(view(pT, "p a b c -> p (a b c)"), bank[1]).then_inc(VEX.done("pT_evac"), 1)
                dve.wait_ge(*ACX.after("exp1", p))
                nc.vector.reciprocal(ri, sm).then_inc(VEX.done("rsum"), 1)

            def last_key(p):
                for j in range(2):
                    dve.wait_ge(*PEX.after(f"ov_{j}", p))
                    dve.wait_ge(ctx_in[j], (p + 1) * CTX1)
                    nc.vector.scalar_tensor_tensor(op[j], cLq[j], pr[j][:, KEYS - 1:KEYS], bank[OV[j]][:, 0:DC + 1],
                                                   ALU.mult, ALU.add).then_inc(VEX.done(f"ov_evac{j}"), 1)

            def add_attn(p):
                for j in range(2):
                    dve.wait_ge(*PEX.after(f"wv_{j}", p))
                    nc.vector.scalar_tensor_tensor(x[:, p * 2 + j, :], bank[WV[j]][:, 0:D], ri[:, j:j + 1], x[:, p * 2 + j, :],
                                                   ALU.mult, ALU.add).then_inc(VEX.done(f"x_attn{j}"), 1)

            def stats_linear(p):
                wait_alone(dve, *VEX.after("x_attn1", p))
                norm_stats(dve, VEB, "lnB", p, tiles_of(p), 1e-5, LNB)

            def apply_linear(p):
                wait_alone(dve, *PEX.after("trA", p))
                norm_apply(dve, VEB, GPB, "lnB", p, tiles_of(p), lambda j: xnx[j], LNB)

            def linear_vector(p, nxt):
                xt = tiles_of(p)
                if nxt is not None:
                    stats_attn(nxt)
                    apply_attn(nxt)
                for j in range(2):
                    dve.wait_ge(*ACL.after(f"square{j}", p))
                    nc.vector.reduce_sum(ss[:, j, :], view(fqk[j], "p (a b) -> p a b", b=16), AX).then_inc(VEL.done(f"ss{j}"), 1)
                dve.wait_ge(*VEL.after("ss1", p))
                nc.vector.tensor_scalar_max(ss, ss, 1e-24).then_inc(VEL.done("ss_max"), 1)
                dve.wait_ge(*VEL.after("ss_max", p))
                nc.vector.tensor_scalar(rt.bitcast(i32), ss.bitcast(i32), 1, None, ALU.logical_shift_right)\
                    .then_inc(VEL.done("rn_half"), 1)
                dve.wait_ge(*VEL.after("rn_half", p))
                nc.vector.tensor_scalar(rn.bitcast(i32), rt.bitcast(i32), -1.0, float(0x5f3759df), ALU.mult, ALU.add)\
                    .then_inc(VEL.done("rn_y0"), 1)
                for n in range(3):
                    dve.wait_ge(*VEL.after(f"rn_y{n}", p))
                    nc.vector.scalar_tensor_tensor(rt, rn, -0.5, rn, ALU.mult, ALU.mult).then_inc(VEL.done(f"rn_yy{n}"), 1)
                    dve.wait_ge(*VEL.after(f"rn_yy{n}", p))
                    nc.vector.tensor_tensor(rt, rt, ss, ALU.mult).then_inc(VEL.done(f"rn_syy{n}"), 1)
                    dve.wait_ge(*VEL.after(f"rn_syy{n}", p))
                    nc.vector.scalar_tensor_tensor(rn, rt, 1.5, rn, ALU.add, ALU.mult).then_inc(VEL.done(f"rn_y{n + 1}"), 1)
                dve.wait_ge(*VEL.after("rn_y3", p))
                for j in range(2):
                    nc.vector.tensor_tensor(view(fqk[j], "p (a b) -> p a b", b=16), view(bank[5 + j], "p (a b) -> p a b", b=16),
                                            rn[:, j, :].unsqueeze(2).broadcast_to((P, 32, 16)), ALU.mult)\
                        .then_inc(VEL.done(f"unit{j}"), 1)
                if nxt is not None:
                    row_maxima(nxt)
                    probabilities_T(nxt)
                dve.wait_ge(*PEL.after("ks", p))
                nc.vector.scalar_tensor_tensor(dtmp, view(bank[7], "p (a b) -> p a b", b=D), 1e-6, fqk2[:, :, 0:D], ALU.add,
                                               ALU.mult).then_inc(VEL.done("den_mul"), 1)
                for j in range(2):
                    if j == 1:
                        dve.wait_ge(*VEL.after("den_mul", p))
                        nc.vector.reduce_sum(den, view(dtmp, "p a b -> p (a b)").rearrange("p (a b) -> p a b", b=16), AX)\
                            .then_inc(VEL.done("den"), 1)
                        dve.wait_ge(*VEL.after("den", p))
                        nc.vector.reciprocal(den, den).then_inc(VEL.done("rden"), 1)
                    for hf in range(2):
                        dve.wait_ge(*PEL.after(f"kv_{j}_{hf}", p))
                        nc.vector.tensor_tensor(kvm[j][:, hf, :, :], view(bank[KV[j][hf]], "p (a b) -> p a b", b=P),
                                                K["hmask"].unsqueeze(1).broadcast_to((P, BT, P)), ALU.mult)\
                            .then_inc(VEL.done(f"kv_evac{j}_{hf}"), 1)
                    if nxt is not None and j == 0:
                        last_key(nxt)
                dve.wait_ge(*VEL.after("rden", p))
                dve.wait_ge(*PEL.after("at", p))
                heads = (P, 32, 16)
                nc.vector.tensor_tensor(view(dtmp, "p a b -> p (a b)").rearrange("p (a b) -> p a b", b=16),
                                        view(bank[6], "p (a b) -> p a b", b=16), den.unsqueeze(2).broadcast_to(heads),
                                        ALU.mult).then_inc(VEL.done("at_norm"), 1)
                dve.wait_ge(*VEL.after("at_norm", p))
                xpair = x[:, bass.ds(p * 2, 2), :]
                nc.vector.tensor_tensor(xpair, xpair, dtmp, ALU.add).then_inc(VEL.done("x_lin"), 1)
                if nxt is not None:
                    add_attn(nxt)
                    stats_linear(nxt)
                wait_alone(dve, *VEL.after("x_lin", p))
                norm_stats(dve, VEL, "lnC", p, xt, 1e-5)
                if nxt is not None:
                    apply_linear(nxt)
                wait_alone(dve, *PEL.after("trC", p - 1))
                norm_apply(dve, VEL, GPL, "lnC", p, xt, lambda j: xn[j])
                for j in range(2):
                    dve.wait_ge(*VEL.after(f"lnC_norm{j}", p))
                    nc.vector.tensor_scalar_mul(xm[:, p * 2 + j, :], xn[j], 1.0).then_inc(VEL.done(f"xm{j}"), 1)

            stats_attn(0)
            apply_attn(0)
            row_maxima(0)
            probabilities_T(0)
            last_key(0)
            add_attn(0)
            stats_linear(0)
            apply_linear(0)
            with dve.Fori(0, NPAIR - 1) as p:
                linear_vector(p, p + 1)
            linear_vector(NPAIR - 1, None)
            all_t = (P, NT, E)
            dve.wait_ge(*SHP.sem_value("lg"))
            nc.vector.tensor_copy(view(lg, "p a b -> p (a b)"), bank[4][:, 0:NT * E]).then_inc(RT.done("logits"), 1)
            dve.wait_ge(*RT.sem_value("logits"))
            nc.vector.reduce_max(lg_top, lg, AX).then_inc(RT.done("top"), 1)
            dve.wait_ge(*RT.sem_value("top"))
            nc.vector.tensor_tensor(lg, lg, lg_top.unsqueeze(2).broadcast_to(all_t), ALU.is_ge).then_inc(RT.done("tops"), 1)
            dve.wait_ge(*RT.sem_value("tops"))
            nc.vector.tensor_tensor(lg, lg, K["down"].unsqueeze(1).broadcast_to(all_t), ALU.mult).then_inc(RT.done("tops_down"), 1)
            dve.wait_ge(*RT.sem_value("tops_down"))
            nc.vector.reduce_max(eidx, lg, AX).then_inc(RT.done("down"), 1)
            dve.wait_ge(*RT.sem_value("down"))
            nc.vector.tensor_scalar(eidx, eidx, -1.0, float(E), ALU.mult, ALU.add).then_inc(RT.done("expert"), 1)
            dve.wait_ge(*RT.sem_value("expert"))
            nc.vector.tensor_tensor(oneh, K["iota"].unsqueeze(1).broadcast_to(all_t), eidx.unsqueeze(2).broadcast_to(all_t),
                                    ALU.is_equal).then_inc(RT.done("onehot"), 1)
            dve.wait_ge(*SHA.sem_value("gate_exp"))
            nc.vector.tensor_scalar_add(gate, gate, 1.0).then_inc(RT.done("gate_1p"), 1)
            dve.wait_ge(*RT.sem_value("gate_1p"))
            nc.vector.reciprocal(gate, gate).then_inc(RT.done("gate"), 1)
            def shared_hidden(s):
                n, c = s // 4, s % 4
                dve.wait_ge(*SHA.sem_value(f"silu{s}"))
                nc.vector.tensor_tensor(hs[:, c, n * 512:(n + 1) * 512], sgate[s % 2], bank[2 * (s % 2) + 1], ALU.mult)\
                    .then_inc(SHV.done(f"h{s}"), 1)

            for s in range(3):
                shared_hidden(s)
            def flat3(a):
                return view(a, "p a b -> p (a b)")

            dve.wait_ge(*SHP.sem_value("rank"))
            nc.vector.tensor_tensor(flat3(r_oh), bank[6][:, 0:NT * E], flat3(oneh), ALU.mult).then_inc(RT.done("rank_oh"), 1)
            dve.wait_ge(*SHP.sem_value("count"))
            nc.vector.tensor_tensor(cnt7, bank[7][:, 0:E].unsqueeze(2).broadcast_to((P, E, NT - 1)),
                                    K["caps"].unsqueeze(1).broadcast_to((P, E, NT - 1)), ALU.is_gt).then_inc(RT.done("over7"), 1)
            dve.wait_ge(*RT.sem_value("rank_oh"))
            nc.vector.reduce_sum(rank, r_oh, AX).then_inc(RT.done("rank"), 1)
            dve.wait_ge(*RT.sem_value("over7"))
            nc.vector.reduce_sum(novf, cnt7, AX).then_inc(RT.done("novf"), 1)
            dve.wait_ge(*RT.sem_value("rank"))
            nc.vector.tensor_tensor(r_q7, rank.unsqueeze(2).broadcast_to((P, NT, NT - 1)),
                                    K["caps"].unsqueeze(1).broadcast_to((P, NT, NT - 1)), ALU.is_ge).then_inc(RT.done("q7"), 1)
            dve.wait_ge(*RT.sem_value("novf"))
            nc.vector.tensor_tensor_scan(oend, K["ones"][:, 0:E], novf, 0.0, ALU.mult, ALU.add).then_inc(RT.done("oend"), 1)
            dve.wait_ge(*RT.sem_value("q7"))
            nc.vector.reduce_sum(rq, r_q7, AX).then_inc(RT.done("q"), 1)
            dve.wait_ge(*RT.sem_value("oend"))
            nc.vector.tensor_tensor(obase, oend, novf, ALU.subtract).then_inc(RT.done("obase"), 1)
            nc.vector.tensor_tensor(r_e7, oend.unsqueeze(1).broadcast_to((P, NOVF, E)),
                                    K["nth"].unsqueeze(2).broadcast_to((P, NOVF, E)), ALU.is_le).then_inc(RT.done("e7"), 1)
            dve.wait_ge(*RT.sem_value("obase"))
            nc.vector.tensor_tensor(r_oh, oneh, obase.unsqueeze(1).broadcast_to((P, NT, E)), ALU.mult).then_inc(RT.done("base_oh"), 1)
            dve.wait_ge(*RT.sem_value("e7"))
            nc.vector.reduce_sum(etab_f[:, 0:NOVF], r_e7, AX).then_inc(RT.done("etab_sum"), 1)
            dve.wait_ge(*RT.sem_value("base_oh"))
            nc.vector.reduce_sum(r_bt, r_oh, AX).then_inc(RT.done("base"), 1)
            dve.wait_ge(*RT.sem_value("etab_sum"))
            nc.vector.tensor_scalar_min(etab_f[:, 0:NOVF], etab_f[:, 0:NOVF], E - 1.0).then_inc(RT.done("etab_min"), 1)
            nc.vector.tensor_copy(etab_f[:, NOVF:NOVF + 1], oend[:, E - 1:E]).then_inc(RT.done("etab_n"), 1)
            dve.wait_ge(*RT.sem_value("base"))
            nc.vector.tensor_tensor(r_t, r_bt, rq, ALU.add).then_inc(RT.done("t1"), 1)
            dve.wait_ge(*RT.sem_value("etab_n"))
            nc.vector.tensor_copy(etab.bitcast(i32), etab_f).then_inc(RT.done("etab"), 1)
            nc.vector.tensor_scalar_min(r_g, rq, 1.0).then_inc(RT.done("past"), 1)
            dve.wait_ge(*RT.sem_value("t1"))
            nc.vector.scalar_tensor_tensor(r_t, r_t, E - 1.0, eidx, ALU.add, ALU.subtract).then_inc(RT.done("t2"), 1)
            dve.wait_ge(*RT.sem_value("t2"))
            nc.vector.tensor_tensor(r_t, r_t, r_g, ALU.mult).then_inc(RT.done("t3"), 1)
            dve.wait_ge(*RT.sem_value("t3"))
            nc.vector.tensor_tensor(r_t, r_t, eidx, ALU.add).then_inc(RT.done("tile"), 1)
            dve.wait_ge(*RT.sem_value("tile"))
            nc.vector.scalar_tensor_tensor(slot_f, r_t, float(P), rank, ALU.mult, ALU.add).then_inc(RT.done("slot1"), 1)
            dve.wait_ge(*RT.sem_value("slot1"))
            nc.vector.scalar_tensor_tensor(slot_f, rq, -float(P), slot_f, ALU.mult, ALU.add).then_inc(RT.done("slot2"), 1)
            dve.wait_ge(*RT.sem_value("slot2"))
            nc.vector.tensor_copy(slot_i.bitcast(i32), slot_f).then_inc(RT.done("slot"), 1)
            for s in range(3, 8):
                shared_hidden(s)
            for t in range(NT):
                dve.wait_ge(*SHP.sem_value(f"down{t}"))
                nc.vector.tensor_tensor(x[:, t, :], x[:, t, :], bank[4 + t % 2][:, 0:D], ALU.add).then_inc(SHV.done(f"x{t}"), 1)
            dve.sem_inc(VE2.sem, VE2.round())

            def expert_vector(PEx, ACx, VEx, s, i, h, y):
                dve.wait_ge(*ACx.after("silu" + s, i))
                nc.vector.tensor_tensor(flat3(eh[h]), flat3(egate[h]), bank[2 * h + 1], ALU.mult).then_inc(VEx.done("h" + s), 1)
                dve.wait_ge(*PEx.after("dn" + s, i))
                nc.vector.tensor_copy(y, bank[4 + h][:, 0:D]).then_inc(VEx.done("y" + s), 1)

            with dve.Fori(0, NR) as it:
                dve.wait_ge(y_out, it * (16 * RING))
                for r in range(RING):
                    expert_vector(PE2, AC2, VE2, str(r), it, r % 2, ey[r])
            n_over = dve.value_load(etab.bitcast(i32)[0:1, NOVF:NOVF + 1], min_val=0, max_val=NOVF)
            with dve.If(n_over > 0):
                dve.sem_inc(VEO.sem, VEO.round())
                dve.wait_ge(y_out, 16 * E)
                with dve.Fori(0, NOVF) as i:
                    dve.wait_ge(ovf_out, i * 16)
                    expert_vector(PEO, ACO, VEO, "", i, 0, ey[0])
            dve.wait_ge(gathered, 16 * NT)
            for t in range(NT):
                nc.vector.tensor_tensor(x[:, t, :], x[:, t, :], yg[:, t, :], ALU.add).then_inc(XE.done(f"x{t}"), 1)
            for j in range(2):
                nc.vector.memset(op3[j], 0.0).then_inc(set3.done(f"op_zero{j}"), 1)
            dve.wait_ge(*XE.sem_value("x7"))
            nc.vector.memset(qp3[DC2:DC2 + 2, 1, :, :], 1.0).then_inc(set3.done("rows_one"), 1)
            dve.wait_ge(*set3.sem_value("rows_one"))
            nc.vector.memset(qp3[DC2:DC2 + 1, 1, :, :], 0.0).then_inc(set3.done("row_zero"), 1)
            dve.wait_ge(*set3.sem_value("row_zero"))
            dve.wait_ge(weights3_in, 16 * 7)
            dve.sem_inc(VE3.sem, VE3.round())
            with dve.Fori(0, NPAIR) as p:
                wait_alone(dve, *PE3.after("tr", p - 1))
                layer_norm_vector(dve, VE3, GP3, "ln", p, lambda j: x[:, p * 2 + j, :], lambda j: xn3[j], 1e-5)
                for h in range(H1):
                    dve.wait_ge(*AC3.after(f"qk_evac{h}", p))
                    nc.vector.tensor_scalar_mul(qp3[0:DC2, 1, :, h * S:(h + 1) * S],
                                                view(bank[4 + h % 4][0:DC2, PW:2 * PW], "p (b s) -> p b s", s=S),
                                                HD1 ** -0.5).then_inc(VE3.done(f"qk_evac{h}"), 1)
                for s in range(NU + 4):
                    if s < NU:
                        dve.wait_ge(*PE3.after(f"sc{s}", p))
                        nc.vector.reduce_max(nmx3[:, s % 4:s % 4 + 1], bank[s % 2][:, 0:KEYS], AX, negate=True)\
                            .then_inc(VE3.done(f"row_max{s}"), 1)
                    if 1 <= s <= NU:
                        u = s - 1
                        dve.wait_ge(*AC3.after(f"exp{u}", p))
                        nc.vector.reciprocal(rs3[:, u % 4:u % 4 + 1], sm3[:, u % 4:u % 4 + 1]).then_inc(VE3.done(f"rsum{u}"), 1)
                        dve.wait_ge(*VE3.after(f"rsum{u}", p))
                        nc.vector.tensor_scalar_mul(pr3[u % 4], pr3[u % 4], rs3[:, u % 4:u % 4 + 1]).then_inc(VE3.done(f"norm{u}"), 1)
                    if 3 <= s < NU + 3:
                        u = s - 3
                        b = u // 2
                        if u == 0 or u == NU // 2:
                            dve.wait_ge(ctx_in[b // BT], (p + 1) * CTX3 + NPAIR * CTX1)
                        dve.wait_ge(*PE3.after(f"ov{u}", p))
                        nc.vector.scalar_tensor_tensor(op3[u % 2][:, 0:DC], cLb[b // BT][:, b % BT, :], pr3[u % 4][:, KEYS - 1:KEYS],
                                                       bank[4 + u % 2][:, 0:DC], ALU.mult, ALU.add).then_inc(VE3.done(f"ov_evac{u}"), 1)
                    if s >= 4:
                        u = s - 4
                        b, g = u // 2, u % 2
                        dve.wait_ge(*PE3.after(f"opT{u}", p))
                        if u == 0:
                            dve.wait_ge(*PE3.after("o1", p - 1))
                        nc.vector.tensor_copy(oT3[b // BT][:, :, 4 * g:4 * g + 4, b % BT, :],
                                              view(bank[6 + u % 2][:, 0:2 * P], "p (c h s) -> p c h s", c=2, s=S))\
                            .then_inc(VE3.done(f"opT_evac{u}"), 1)
                for j in range(2):
                    dve.wait_ge(*PE3.after(f"wo{j}", p))
                    nc.vector.tensor_tensor(t3[j], bank[4 + j][:, 0:D], c_bo, ALU.add).then_inc(VE3.done(f"bias{j}"), 1)
                for j in range(2):
                    dve.wait_ge(*VE3.after(f"bias{j}", p))
                    nc.vector.tensor_tensor(x[:, p * 2 + j, :], x[:, p * 2 + j, :], t3[j], ALU.add).then_inc(VE3.done(f"x{j}"), 1)
                dve.wait_ge(*VE3.after("x1", p))
            dve.wait_ge(weights4_in, 16 * 10)
            nc.vector.memset(xp[:, :, :, 0:TAPS - 1], 0.0).then_inc(set4.done("pad"), 1)
            for c in range(4):
                nc.vector.tensor_scalar_mul(m_out[:, c, :], m_out[:, c, :], m_nw[:, c:c + 1]).then_inc(set4.done(f"nw{c}"), 1)
            nc.vector.tensor_scalar_mul(m_D, m_D, 0.25).then_inc(set4.done("D"), 1)
            dve.wait_ge(*set4a.sem_value("expA"))
            nc.vector.tensor_scalar_mul(m_A, m_A, -1.0).then_inc(set4.done("A"), 1)
            dve.wait_ge(*set4.sem_value("A"))
            dve.sem_inc(VE4.sem, VE4.round())
            with dve.Fori(0, NPAIR) as p:
                wait_alone(dve, *PE4.after("out1", p - 1))
                layer_norm_vector(dve, VE4, GP4, "ln1", p, lambda j: x[:, p * 2 + j, :], lambda j: xn4[:, j, :], 1e-5)
                wait_alone(dve, *VE4.after("ln1_norm1", p))
                layer_norm_vector(dve, VE4, GP4, "ln2", p, lambda j: xn4[:, j, :], lambda j: u4[:, j, :], 1e-5)
                dve.wait_ge(*VE4.after("ln2_norm1", p))
                nc.vector.tensor_tensor(u4, u4, m_lnw.unsqueeze(1).broadcast_to((P, 2, D)), ALU.mult).then_inc(VE4.done("ln_w"), 1)
                dve.wait_ge(*VE4.after("ln_w", p))
                nc.vector.tensor_tensor(u4, u4, m_lnb.unsqueeze(1).broadcast_to((P, 2, D)), ALU.add).then_inc(VE4.done("u"), 1)
                dve.wait_ge(*PE4.after("dt", p))
                nc.vector.tensor_tensor(dts["d"], view(bank[6][:, 0:2 * HM], "p (a b) -> p a b", b=HM),
                                        m_dtb.unsqueeze(1).broadcast_to((P, 2, HM)), ALU.add).then_inc(VE4.done("dt_raw"), 1)
                dve.wait_ge(*VE4.after("dt_raw", p))
                nc.vector.scalar_tensor_tensor(dts["a"], dts["d"], -1.0, dts["d"], ALU.mult, ALU.max).then_inc(VE4.done("dt_abs"), 1)
                nc.vector.tensor_scalar_max(dts["m"], dts["d"], 0.0).then_inc(VE4.done("dt_pos"), 1)
                for n in (2, 0, 1):
                    for k in range(TAPS - 1):
                        for c in (2 * n, 2 * n + 1):
                            if k:
                                dve.wait_ge(*VE4.after(f"tap{k - 1}_{c}", p))
                            else:
                                dve.wait_ge(*AC4.after(f"tap3_{2 * n + 1}", p))
                            nc.vector.scalar_tensor_tensor(view(cv[:, c, :], "p (b s) -> p b s", s=S), xp[:, c, :, k:k + S],
                                                           m_conv[:, c, k:k + 1], view(cv[:, c, :], "p (b s) -> p b s", s=S),
                                                           ALU.mult, ALU.add).then_inc(VE4.done(f"tap{k}_{c}"), 1)
                    if n == 2:
                        dve.wait_ge(*AC4.after("dt_exp", p))
                        nc.vector.tensor_scalar_add(dts["e2"], dts["e"], 2.0).then_inc(VE4.done("dt_2e"), 1)
                        dve.wait_ge(*VE4.after("dt_2e", p))
                        nc.vector.reciprocal(dts["r"], dts["e2"]).then_inc(VE4.done("dt_r"), 1)
                        dve.wait_ge(*VE4.after("dt_r", p))
                        nc.vector.tensor_tensor(dts["s"], dts["e"], dts["r"], ALU.mult).then_inc(VE4.done("dt_s"), 1)
                        dve.wait_ge(*VE4.after("dt_s", p))
                        nc.vector.tensor_tensor(dts["s2"], dts["s"], dts["s"], ALU.mult).then_inc(VE4.done("dt_s2"), 1)
                        dve.wait_ge(*VE4.after("dt_s2", p))
                        nc.vector.tensor_scalar_mul(dts["p"], dts["s2"], 1.0 / 15.0).then_inc(VE4.done("dt_p15"), 1)
                        for i in (13, 11, 9, 7, 5, 3):
                            dve.wait_ge(*VE4.after(f"dt_p{i + 2}", p))
                            nc.vector.scalar_tensor_tensor(dts["p"], dts["p"], 1.0 / i, dts["s2"], ALU.add, ALU.mult)\
                                .then_inc(VE4.done(f"dt_p{i}"), 1)
                        dve.wait_ge(*VE4.after("dt_p3", p))
                        nc.vector.scalar_tensor_tensor(dts["p"], dts["p"], 1.0, dts["s"], ALU.add, ALU.mult)\
                            .then_inc(VE4.done("dt_p1"), 1)
                        dve.wait_ge(*VE4.after("dt_p1", p))
                        nc.vector.scalar_tensor_tensor(dts["dt"], dts["p"], 2.0, dts["m"], ALU.mult, ALU.add)\
                            .then_inc(VE4.done("dt"), 1)
                        dve.wait_ge(*VE4.after("dt", p))
                        nc.vector.tensor_tensor(dts["dtA"], dts["dt"], m_A.unsqueeze(1).broadcast_to((P, 2, HM)), ALU.mult)\
                            .then_inc(VE4.done("dtA"), 1)
                for n in (2, 0, 1):
                    dve.wait_ge(*AC4.after(f"tanh{n}", p))
                    nc.vector.scalar_tensor_tensor(cv[:, 2 * n:2 * n + 2, :], th[:, 2 * n:2 * n + 2, :], 1.0, cv[:, 2 * n:2 * n + 2, :],
                                                   ALU.add, ALU.mult).then_inc(VE4.done(f"silu{n}"), 1)
                    if n == 2:
                        dve.wait_ge(*PE4.after("cum", p))
                        nc.vector.tensor_copy(dts["cum"], view(bank[6][:, 2 * HM:4 * HM], "p (a b) -> p a b", b=HM)).then_inc(VE4.done("cum"), 1)
                for j in range(2):
                    dve.wait_ge(*AC4.after(f"z_tanh{j}", p))
                    nc.vector.scalar_tensor_tensor(zs[j], zt[j], 1.0, bank[4 + j], ALU.add, ALU.mult).then_inc(VE4.done(f"z_silu{j}"), 1)
                for j in range(2):
                    dve.wait_ge(*PE4.after("G1", p))
                    nc.vector.tensor_tensor(gm4[j], bank[7][:, j * P:(j + 1) * P], K["gmask"], ALU.mult).then_inc(VE4.done(f"gm{j}"), 1)
                for j in range(2):
                    dve.wait_ge(*AC4.after(f"decay{j}", p))
                    dve.wait_ge(*VE4.after(f"gm{j}", p))
                    nc.vector.tensor_tensor(dec[j], dec[j], gm4[j].unsqueeze(1).broadcast_to((P, HM, P)), ALU.mult)\
                        .then_inc(VE4.done(f"M{j}"), 1)
                for j in range(2):
                    dve.wait_ge(*AC4.after(f"xs_evac{j}", p))
                    nc.vector.tensor_tensor(view(xdt[j], "p (h e) -> p h e", h=HM), view(xs4[j], "p (h e) -> p h e", h=HM),
                                            dts["dt"][:, j, :].unsqueeze(2).broadcast_to((P, HM, HDM)), ALU.mult)\
                        .then_inc(VE4.done(f"xdt{j}"), 1)
                for j in range(2):
                    dve.wait_ge(*PE4.after(f"y{j}", p))
                    dve.wait_ge(*GP4.after(f"xD{j}", p))
                    nc.vector.tensor_tensor(y4[j], bank[4 + j], xD[j], ALU.add).then_inc(VE4.done(f"ya{j}"), 1)
                for j in range(2):
                    dve.wait_ge(*VE4.after(f"ya{j}", p))
                    nc.vector.tensor_tensor(y4[j], y4[j], zs[j], ALU.mult).then_inc(VE4.done(f"yz{j}"), 1)
                for j in range(2):
                    nc.vector.tensor_tensor(x[:, p * 2 + j, :], x[:, p * 2 + j, :], xn4[:, j, :], ALU.add).then_inc(VE4.done(f"xr{j}"), 1)
                dve.wait_ge(*AC4.after("square1", p))
                nc.vector.tensor_scalar(ssq, ssq, 1.0 / DIN, 1e-5, ALU.mult, ALU.add).then_inc(VE4.done("mean_square"), 1)
                dve.wait_ge(*GP4.after("rms", p))
                for j in range(2):
                    dve.wait_ge(*PE4.after(f"out{j}", p))
                    nc.vector.scalar_tensor_tensor(x[:, p * 2 + j, :], bank[6 + j][:, 0:D], rms[:, j:j + 1], x[:, p * 2 + j, :],
                                                   ALU.mult, ALU.add).then_inc(VE4.done(f"x{j}"), 1)
                dve.wait_ge(*VE4.after("x1", p))
            dve.sem_inc(VE5.sem, VE5.round())
            with dve.Fori(0, NPAIR) as p:
                wait_alone(dve, *PE5.after("tr", p - 1))
                layer_norm_vector(dve, VE5, GP5, "ln", p, lambda j: x[:, p * 2 + j, :], lambda j: xn5[j], 1e-5)
                for n in range(3):
                    dve.wait_ge(*AC5.after(f"silu{n}", p))
                    dve.wait_ge(*PE5.after(f"u{n}", p))
                    nc.vector.tensor_tensor(h5[:, 2 * n:2 * n + 2, :], sg5[:, 2 * n:2 * n + 2, :], view(bank[3 + n], "p (c t) -> p c t", c=2),
                                            ALU.mult).then_inc(VE5.done(f"h{n}"), 1)
                for j in range(2):
                    dve.wait_ge(*PE5.after(f"down{j}", p))
                    nc.vector.scalar_tensor_tensor(x[:, p * 2 + j, :], bank[7 - j][:, 0:D], 1.0 / 127.0 ** 2, x[:, p * 2 + j, :],
                                                   ALU.mult, ALU.add).then_inc(VE5.done(f"x{j}"), 1)

        @block.tensor
        def _(pe):
            def mm(o, l, r, first=True, last=True):
                return nc.tensor.matmul(o, l, r, start=first, stop=last)

            pe.sem_inc(PEX.sem, PEX.round())
            pe.sem_inc(PEL.sem, PEL.round())
            pe.sem_inc(PEB.sem, PEB.round())
            pe.wait_ge(weights1_in, 16 * 8)

            def transpose_norm(V, PEn, bk, rows, tag, ln, p):
                for j in range(2):
                    pe.wait_ge(*V.after(f"{ln}_norm{j}", p))
                    for k in range(2):
                        last = nc.tensor.transpose(bk[:, k * PW + j * P:k * PW + (j + 1) * P], rows[j][:, k * P:(k + 1) * P], ident)
                last.then_inc(PEn.done(tag), 1)

            def project_queries(p):
                pe.wait_ge(*ACX.after("xnT_A", p))
                for o in range(2):
                    for k in range(2):
                        last = mm(bank[1][:, o * PW:(o + 1) * PW], wq[:, k, o * P:(o + 1) * P], xnT_a[:, k, :], k == 0, k == 1)
                last.then_inc(PEX.done("q"), 1)

            def scores(p):
                pe.wait_ge(*ACX.after("q_bias1", p))
                for o, m in ((0, P), (1, DC2 + 1)):
                    for k in range(2):
                        last = mm(bank[2][0:m, o * PW:(o + 1) * PW], wk[:, k, o * P:o * P + m], qT[:, k, :], k == 0, k == 1)
                last.then_inc(PEX.done("qk"), 1)
                pe.wait_ge(*ACX.after("qk_evac1", p))
                pe.wait_ge(*setup.sem_value("ones_l1"))
                for j in range(2):
                    pe.wait_ge(ctx_in[j], (p + 1) * CTX1)
                    for b in range(BT):
                        mm(bank[SC[j]][S * b:S * b + S, 0:KEYS], qpT[:, 0, j * P + S * b:j * P + S * b + S],
                           cT1[j][:, b, :], True, False)
                    for b in range(BT):
                        last = mm(bank[SC[j]][S * b:S * b + S, 0:KEYS], qpT[0:DC2 + 1, 1, j * P + S * b:j * P + S * b + S],
                                  cT2[j][0:DC2 + 1, b, :], False, True)
                    last.then_inc(PEX.done(f"sc_{j}"), 1)

            def transpose_probabilities(p):
                for j in range(2):
                    pe.wait_ge(*ACX.after(f"exp{j}", p))
                    for c in range(2):
                        last = nc.tensor.transpose(bank[1][:, (j * 2 + c) * P:(j * 2 + c + 1) * P], pr[j][:, c * P:(c + 1) * P], ident)
                last.then_inc(PEX.done("pt"), 1)

            def context_sums(p):
                pe.wait_ge(*VEX.after("pT_evac", p))
                for j in range(2):
                    for c in range(2):
                        for b in range(BT):
                            last = mm(bank[OV[j]][S * b:S * b + S, 0:DC + 1], pT[:, j, c, S * b:S * b + S],
                                      cN[j][:, b, c, :], c == 0, c == 1)
                    last.then_inc(PEX.done(f"ov_{j}"), 1)

            def transpose_sums(p):
                for j in range(2):
                    pe.wait_ge(*VEX.after(f"ov_evac{j}", p))
                    nc.tensor.transpose(bank[OT[j]][:, 0:P], op[j][:, 0:P], ident)
                    last = nc.tensor.transpose(bank[OT[j]][0:DC2 + 1, P:2 * P], op[j][:, P:DC + 1], ident)
                    last.then_inc(PEX.done(f"ot_{j}"), 1)

            def project_values(p):
                for j in range(2):
                    pe.wait_ge(*ACX.after(f"oT_evac1_{j}", p))
                    mm(bank[WV[j]][:, 0:D], oT[j][:, 0, :], wv1, True, False)
                    mm(bank[WV[j]][:, 0:D], oT[j][0:DC2 + 1, 1, :], wv2[0:DC2 + 1, :], False, True)\
                        .then_inc(PEX.done(f"wv_{j}"), 1)

            def linear_tensor(p, nxt):
                pe.wait_ge(*ACB.after("xnT_B", p))
                for j in range(2):
                    for k in range(2):
                        mm(bank[5 + j], xnT_x[:, k, j * P:(j + 1) * P], wqkv[:, k, 0:2 * D], k == 0, k == 1)
                    for k in range(2):
                        last = mm(bank[7][:, j * D:(j + 1) * D], xnT_x[:, k, j * P:(j + 1) * P], wqkv[:, k, 2 * D:3 * D], k == 0, k == 1)
                    last.then_inc(PEL.done(f"qkv_{j}"), 1)
                    if nxt is not None and j == 0:
                        transpose_norm(VEX, PEX, bank[0], xnx, "trA", "lnA", nxt)
                if nxt is not None:
                    project_queries(nxt)
                    scores(nxt)
                    transpose_probabilities(nxt)
                pe.wait_ge(*VEL.after("unit1", p))
                for j in range(2):
                    pe.wait_ge(*ACL.after(f"softplus{j}", p))
                    for hf in range(2):
                        last = nc.tensor.transpose(bank[4][:, (2 * j + hf) * P:(2 * j + hf + 1) * P], fqk[j][:, hf * P:(hf + 1) * P], ident)
                last.then_inc(PEL.done("qt"), 1)
                for j in range(2):
                    last = mm(bank[7][:, j * D:(j + 1) * D], K["same"], fqk[j][:, D:2 * D])
                last.then_inc(PEL.done("ks"), 1)
                for j in range(2):
                    for hf in range(2):
                        if j == 1:
                            pe.wait_ge(*(ACL.after("qt_evac", p) if hf == 0 else VEL.after("kv_evac0_0", p)))
                        mm(bank[KV[j][hf]], fqk[j][:, D + hf * P:D + (hf + 1) * P],
                           view(vblk[j][:, hf, :, :], "p a b -> p (a b)")).then_inc(PEL.done(f"kv_{j}_{hf}"), 1)
                    if nxt is not None and j == 0:
                        context_sums(nxt)
                if nxt is not None:
                    transpose_sums(nxt)
                for j in range(2):
                    pe.wait_ge(*VEL.after(f"kv_evac{j}_1", p))
                    for hf in range(2):
                        for b in range(BT):
                            last = mm(bank[6][S * b:S * b + S, j * D + hf * P:j * D + (hf + 1) * P], qtT[:, j, hf, S * b:S * b + S],
                                      kvm[j][:, hf, b, :])
                last.then_inc(PEL.done("at"), 1)
                if nxt is not None:
                    project_values(nxt)
                if nxt is not None:
                    transpose_norm(VEB, PEB, bank[6], xnx, "trB", "lnB", nxt)
                transpose_norm(VEL, PEL, bank[4], xn, "trC", "lnC", p)

            transpose_norm(VEX, PEX, bank[0], xnx, "trA", "lnA", 0)
            project_queries(0)
            scores(0)
            transpose_probabilities(0)
            context_sums(0)
            transpose_sums(0)
            project_values(0)
            transpose_norm(VEB, PEB, bank[6], xnx, "trB", "lnB", 0)
            with pe.Fori(0, NPAIR - 1) as p:
                linear_tensor(p, p + 1)
            linear_tensor(NPAIR - 1, None)
            def shared_up(s):
                n, c = s // 4, s % 4
                if s >= 2:
                    pe.wait_ge(*SHV.sem_value(f"h{s - 2}"))
                for w, o in ((sg_w, 0), (su_w, 1)):
                    for k in range(2):
                        last = mm(bank[2 * (s % 2) + o], w[:, k, c * P:(c + 1) * P], xnT_all[:, k, n * 512:(n + 1) * 512], k == 0, k == 1)
                last.then_inc(SHP.done(f"gu{s}"), 1)

            pe.wait_ge(weights_sh, 48)
            pe.wait_ge(*GPL.all(NPAIR))
            pe.wait_ge(*VEX.all(NPAIR))
            pe.wait_ge(*VEL.all(NPAIR))
            for t in range(NT):
                for k in range(2):
                    last = mm(bank[4][:, t * E:(t + 1) * E], xnT_all[:, k, t * P:(t + 1) * P], wr[:, k, :], k == 0, k == 1)
            last.then_inc(SHP.done("lg"), 1)
            shared_up(0)
            shared_up(1)
            pe.wait_ge(*RT.sem_value("onehot"))
            oneh_all = view(oneh, "p a b -> p (a b)")
            mm(bank[6][:, 0:NT * E], K["before"], oneh_all, True, False)
            for t in range(1, NT):
                last = mm(bank[6][:, t * E:NT * E], K["ones"], oneh_all[:, 0:(NT - t) * E], False, t == NT - 1)
            last.then_inc(SHP.done("rank"), 1)
            for t in range(NT):
                last = mm(bank[7][:, 0:E], K["ones"], oneh[:, t, :], t == 0, t == NT - 1)
            last.then_inc(SHP.done("count"), 1)
            for s in range(2, 8):
                shared_up(s)
            for t in range(NT):
                pe.wait_ge(*SHV.sem_value("h3" if t < 4 else "h7"))
                if t >= 2:
                    pe.wait_ge(*SHV.sem_value(f"x{t - 2}"))
                for c in range(4):
                    last = mm(bank[4 + t % 2][:, 0:D], hs[:, c, t * P:(t + 1) * P], sd_w[:, c, :], c == 0, c == 3)
                last.then_inc(SHP.done(f"down{t}"), 1)
            pe.wait_ge(*SHV.sem_value("x7"))
            pe.wait_ge(*RT.sem_value("slot"))
            pe.sem_inc(PE2.sem, PE2.round())

            def expert_up(PEx, ACx, s, i, h, r):
                for k in range(2):
                    last = nc.tensor.transpose(bank[6 + h][:, k * P:(k + 1) * P], xg[r][:, k * P:(k + 1) * P], ident)
                last.then_inc(PEx.done("xt" + s), 1)
                pe.wait_ge(*ACx.after("xT" + s, i))
                for o in range(2):
                    for c in range(4):
                        for k in range(2):
                            last = mm(bank[2 * h + o][:, c * P:(c + 1) * P], ring_gu[r][:, k, o * F0 + c * P:o * F0 + (c + 1) * P],
                                      xgT[h][:, k, :], k == 0, k == 1)
                last.then_inc(PEx.done("gu" + s), 1)

            def expert_down(PEx, VEx, s, i, h, r):
                pe.wait_ge(*VEx.after("h" + s, i))
                for c in range(4):
                    last = mm(bank[4 + h][:, 0:D], eh[h][:, c, :], ring_dn[r][:, c, :], c == 0, c == 3)
                last.then_inc(PEx.done("dn" + s), 1)

            with pe.Fori(0, NR) as it:
                for r in range(RING):
                    pe.wait_ge(xg_in[r], it * 16 + 16)
                    pe.wait_ge(gu_in[r], it * 16 + 16)
                    expert_up(PE2, AC2, str(r), it, r % 2, r)
                    if r >= 1:
                        q = r - 1
                        pe.wait_ge(dn_in[q], it * 16 + 16)
                        pe.wait_ge(*VE2.after(f"y{q - 2}", it) if q >= 2 else VE2.after(f"y{q + 2}", it - 1))
                        expert_down(PE2, VE2, str(q), it, q % 2, q)
                q = RING - 1
                pe.wait_ge(dn_in[q], it * 16 + 16)
                pe.wait_ge(*VE2.after(f"y{q - 2}", it))
                expert_down(PE2, VE2, str(q), it, q % 2, q)
            n_over = pe.value_load(etab.bitcast(i32)[0:1, NOVF:NOVF + 1], min_val=0, max_val=NOVF)
            with pe.If(n_over > 0):
                pe.sem_inc(PEO.sem, PEO.round())
                pe.wait_ge(*VE2.all(NR))
                with pe.Fori(0, NOVF) as i:
                    pe.wait_ge(ovf_in, i * 48 + 48)
                    pe.wait_ge(*VEO.after("y", i - 1))
                    expert_up(PEO, ACO, "", i, 0, 0)
                    expert_down(PEO, VEO, "", i, 0, 0)
                pe.wait_ge(*VEO.all(NOVF))
            pe.wait_ge(weights3_in, 16 * 7)
            pe.sem_inc(PE3.sem, PE3.round())
            pe.wait_ge(*set3.sem_value("row_zero"))
            with pe.Fori(0, NPAIR) as p:
                pe.wait_ge(*AC3.after("o_evac0", p - 1))
                for j in range(2):
                    pe.wait_ge(*VE3.after(f"ln_norm{j}", p))
                    for k in range(2):
                        last = nc.tensor.transpose(bank[0][:, k * PW + j * P:k * PW + (j + 1) * P], xn3[j][:, k * P:(k + 1) * P], ident)
                last.then_inc(PE3.done("tr"), 1)
                pe.wait_ge(*AC3.after("xnT", p))
                pe.wait_ge(*AC3.after("ot_evac1", p - 1))
                for n in range(2):
                    for o in range(2 * n, 2 * n + 2):
                        for k in range(2):
                            last = mm(bank[2 + n][:, (o % 2) * PW:(o % 2 + 1) * PW], c_wq[:, k, o * P:(o + 1) * P], xnT3[:, k, :], k == 0, k == 1)
                    last.then_inc(PE3.done(f"q{n}"), 1)
                for h in range(H1):
                    pe.wait_ge(*AC3.after(f"q_evac{h // 4}", p))
                    if h >= 4:
                        pe.wait_ge(*VE3.after(f"qk_evac{h - 4}", p))
                    elif h < 2:
                        pe.wait_ge(*VE3.after(f"bias{h}", p - 1))
                    else:
                        pe.wait_ge(*VE3.after(f"opT_evac{NU - 4 + h}", p - 1))
                    mm(bank[4 + h % 4][:, 0:PW], c_wk[:, h, 0:P], q3[:, h // 2, :])
                    mm(bank[4 + h % 4][0:DC2, PW:2 * PW], c_wk[:, h, P:DC], q3[:, h // 2, :]).then_inc(PE3.done(f"qk{h}"), 1)
                pe.wait_ge(*AC3.after("o_evac1", p - 1))
                pe.wait_ge(*VE3.after("qk_evac7", p))
                for s in range(NU + 4):
                    if s < NU:
                        b, g = s // 2, s % 2
                        j = b // BT
                        if s % (NU // 2) == 0:
                            pe.wait_ge(ctx_in[j], (p + 1) * CTX3 + NPAIR * CTX1)
                        if s >= 2:
                            pe.wait_ge(*AC3.after(f"exp{s - 2}", p))
                        mm(bank[s % 2][:, 0:KEYS], qp3[:, 0, b, g * P:(g + 1) * P], cT1[j][:, b % BT, :], True, False)
                        mm(bank[s % 2][:, 0:KEYS], qp3[0:DC2 + 2, 1, b, g * P:(g + 1) * P], cT2[j][0:DC2 + 2, b % BT, :], False, True)\
                            .then_inc(PE3.done(f"sc{s}"), 1)
                    if 2 <= s < NU + 2:
                        u = s - 2
                        pe.wait_ge(*VE3.after(f"norm{u}", p))
                        if u >= 2:
                            pe.wait_ge(*AC3.after(f"pT_evac{u - 2}", p))
                        for c in range(2):
                            last = nc.tensor.transpose(bank[2 + u % 2][:, c * P:(c + 1) * P], pr3[u % 4][:, c * P:(c + 1) * P], ident)
                        last.then_inc(PE3.done(f"pt{u}"), 1)
                    if 3 <= s < NU + 3:
                        u = s - 3
                        b = u // 2
                        pe.wait_ge(*AC3.after(f"pT_evac{u}", p))
                        if u >= 2:
                            pe.wait_ge(*VE3.after(f"ov_evac{u - 2}", p))
                        for c in range(2):
                            last = mm(bank[4 + u % 2][:, 0:DC], pT3[u % 2][:, c, :], cN[b // BT][:, b % BT, c, 0:DC], c == 0, c == 1)
                        last.then_inc(PE3.done(f"ov{u}"), 1)
                    if s >= 4:
                        u = s - 4
                        pe.wait_ge(*VE3.after(f"ov_evac{u}", p))
                        if u >= 2:
                            pe.wait_ge(*VE3.after(f"opT_evac{u - 2}", p))
                        for c in range(2):
                            last = nc.tensor.transpose(bank[6 + u % 2][:, c * P:(c + 1) * P], op3[u % 2][:, c * P:(c + 1) * P], ident)
                        last.then_inc(PE3.done(f"opT{u}"), 1)
                for j in range(2):
                    pe.wait_ge(*VE3.after(f"opT_evac{NU // 2 * (j + 1) - 1}", p))
                    pe.wait_ge(*AC3.after(f"exp{NU - 2 + j}", p))
                    for h in range(H1):
                        o = bank[j][:, h * HD1:(h + 1) * HD1]
                        mm(o, view(oT3[j][:, 0, h, :, :], "p b s -> p (b s)"), c_wv[:, 0, h * HD1:(h + 1) * HD1], True, False)
                        last = mm(o, view(oT3[j][0:DC2, 1, h, :, :], "p b s -> p (b s)"), c_wv[0:DC2, 1, h * HD1:(h + 1) * HD1], False, True)
                    last.then_inc(PE3.done(f"o{j}"), 1)
                for j in range(2):
                    pe.wait_ge(*AC3.after(f"o_evac{j}", p))
                    for c in range(4):
                        last = nc.tensor.transpose(bank[2 + j][:, c * P:(c + 1) * P], o3[j][:, c * P:(c + 1) * P], ident)
                    last.then_inc(PE3.done(f"ot{j}"), 1)
                for j in range(2):
                    pe.wait_ge(*AC3.after(f"ot_evac{j}", p))
                    for c in range(4):
                        last = mm(bank[4 + j][:, 0:D], o3T[j][:, c, :], c_wo[:, c, :], c == 0, c == 3)
                    last.then_inc(PE3.done(f"wo{j}"), 1)
            pe.wait_ge(weights4_in, 16 * 10)
            pe.wait_ge(*set4.sem_value("A"))
            pe.sem_inc(PE4.sem, PE4.round())
            ZC, XC, DTC = 0, DIN, 2 * DIN + 2 * NST
            with pe.Fori(0, NPAIR) as p:
                pe.wait_ge(*VE4.after("u", p))
                pe.wait_ge(*AC4.after("decay1", p - 1))
                for j in range(2):
                    for k in range(2):
                        last = nc.tensor.transpose(bank[0][:, k * PW + j * P:k * PW + (j + 1) * P], u4[:, j, k * P:(k + 1) * P], ident)
                last.then_inc(PE4.done("tr"), 1)
                pe.wait_ge(*AC4.after("uT", p))
                pe.wait_ge(*VE4.after("x1", p - 1))
                for j in range(2):
                    for k in range(2):
                        last = mm(bank[6][:, j * HM:(j + 1) * HM], uT4[:, k, j * P:(j + 1) * P], m_in[:, k, DTC:DTC + HM], k == 0, k == 1)
                last.then_inc(PE4.done("dt"), 1)
                pe.wait_ge(*AC4.after("yT_evac1", p - 1))
                for n in (2, 0, 1):
                    for c in range(2):
                        for k in range(2):
                            last = mm(bank[1 + n][:, c * PW:(c + 1) * PW], m_in[:, k, XC + (2 * n + c) * P:XC + (2 * n + c + 1) * P],
                                      uT4[:, k, :], k == 0, k == 1)
                    last.then_inc(PE4.done(f"xbc{n}"), 1)
                for j in range(2):
                    for k in range(2):
                        last = mm(bank[4 + j], uT4[:, k, j * P:(j + 1) * P], m_in[:, k, ZC:ZC + DIN], k == 0, k == 1)
                    last.then_inc(PE4.done(f"z{j}"), 1)
                pe.wait_ge(*VE4.after("dtA", p))
                for j in range(2):
                    last = mm(bank[6][:, (2 + j) * HM:(3 + j) * HM], K["tri"], dts["dtA"][:, j, :])
                last.then_inc(PE4.done("cum"), 1)

                def cum_rows(j):
                    for h in range(HM):
                        last = mm(bank[(3, 0)[h // 4]][:, (h % 4) * P:(h % 4 + 1) * P],
                                  dts["dtA"][:, j, h:h + 1].broadcast_to((P, P)), K["tri"])
                    last.then_inc(PE4.done(f"cumT{j}"), 1)

                pe.wait_ge(*AC4.after("tap3_5", p))
                cum_rows(0)
                pe.wait_ge(*VE4.after("silu2", p))
                for j in range(2):
                    mm(bank[7][:, j * P:(j + 1) * P], cv[:, 4, j * P:(j + 1) * P], cv[:, 5, j * P:(j + 1) * P]).then_inc(PE4.done(f"G{j}"), 1)
                pe.wait_ge(*VE4.after("silu1", p))
                for j in range(2):
                    for c in range(4):
                        last = nc.tensor.transpose(bank[1 + j][:, c * P:(c + 1) * P], cv[:, c, j * P:(j + 1) * P], ident)
                    last.then_inc(PE4.done(f"xs{j}"), 1)
                pe.wait_ge(*AC4.after("relu0_7", p))
                cum_rows(1)
                for j in range(2):
                    pe.wait_ge(*VE4.after(f"M{j}", p))
                    pe.wait_ge(*VE4.after(f"xdt{j}", p))
                    pe.wait_ge(*VE4.after(f"z_silu{j}", p))
                    for h in range(HM):
                        last = mm(bank[4 + j][:, h * HDM:(h + 1) * HDM], dec[j][:, h, :], xdt[j][:, h * HDM:(h + 1) * HDM])
                    last.then_inc(PE4.done(f"y{j}"), 1)
                for j in range(2):
                    pe.wait_ge(*VE4.after(f"yz{j}", p))
                    for c in range(4):
                        last = nc.tensor.transpose(bank[1 + j][:, c * P:(c + 1) * P], y4[j][:, c * P:(c + 1) * P], ident)
                    last.then_inc(PE4.done(f"yT{j}"), 1)
                for j in range(2):
                    pe.wait_ge(*AC4.after(f"yT_evac{j}", p))
                    for c in range(4):
                        last = mm(bank[6 + j][:, 0:D], yT4[j][:, c, :], m_out[:, c, :], c == 0, c == 3)
                    last.then_inc(PE4.done(f"out{j}"), 1)
            pe.wait_ge(*ints.sem_value("int2"))
            pe.sem_inc(PE5.sem, PE5.round())
            with pe.Fori(0, NPAIR) as p:
                pe.wait_ge(*VE5.after("x1", p - 1))
                for j in range(2):
                    pe.wait_ge(*VE5.after(f"ln_norm{j}", p))
                    for k in range(2):
                        last = nc.tensor.transpose(bank[6][:, k * PW + j * P:k * PW + (j + 1) * P], xn5[j][:, k * P:(k + 1) * P], ident)
                last.then_inc(PE5.done("tr"), 1)
                pe.wait_ge(*AC5.after("xnT", p))
                for n in range(3):
                    pe.wait_ge(*VE5.after(f"h{n}", p - 1))
                    for w, o, tag in ((f_g, 0, "g"), (f_u, 3, "u")):
                        for c in (2 * n, 2 * n + 1):
                            for k in range(2):
                                last = mm(bank[o + n][:, (c % 2) * PW:(c % 2 + 1) * PW], w[:, k, c * P:(c + 1) * P], xnT5[:, k, :], k == 0, k == 1)
                        last.then_inc(PE5.done(f"{tag}{n}"), 1)
                for j in range(2):
                    for c in range(6):
                        if c % 2 == 0:
                            pe.wait_ge(*VE5.after(f"h{c // 2}", p))
                        last = mm(bank[7 - j][:, 0:D], h5[:, c, j * P:(j + 1) * P], f_d[:, c, :], c == 0, c == 5)
                    last.then_inc(PE5.done(f"down{j}"), 1)

        return high[0], all_steps


SBUF_COLS = 53200


def layouts(a):
    T = lambda w: np.ascontiguousarray(np.asarray(w).T)
    ctx = a["ctx_768"]
    first = ctx[:, :2 * P, :].reshape(NT, BT, 2, P, DC)
    return {
        "consts": host_constants()[0],
        "x": a["x"].reshape(TOK, D),
        "ctx_T": np.ascontiguousarray(ctx.reshape(NT, BT, KEYS, DC).transpose(0, 3, 1, 2)),
        "ctx_N": np.ascontiguousarray(first.transpose(0, 3, 1, 2, 4)).reshape(NT, P, 2 * BT, DC),
        "ctx_last": np.ascontiguousarray(ctx[:, KEYS - 1, :]),
        "mask": a["mask_BxS2_bk0"],
        "wq": T(a["L0_xattn_Wq"]), "bq": T(a["L0_xattn_bq"].reshape(2, P)),
        "wk": np.concatenate([a["L0_xattn_Wk"], a["L0_xattn_bk"][:, None]], 1),
        "wv": np.concatenate([T(a["L0_xattn_Wv"]), a["L0_xattn_bv"][None, :]], 0),
        "wqkv": T(a["L0_attn_W_qkv"]), "wr": T(a["L0_ffn_w_router"]),
        "s_g": T(a["L0_ffn_w_gate"]), "s_u": T(a["L0_ffn_w_up"]), "s_d": T(a["L0_ffn_w_down"]),
        "c_wq": a["L1_xattn_W_q"], "c_wk": T(a["L1_xattn_W_k"]), "c_wv": a["L1_xattn_W_v"], "c_wo": a["L1_xattn_W_o"],
        "c_bo": a["L1_xattn_b_o"],
        "m_in": T(a["L1_attn_in_proj_w"]), "m_out": T(a["L1_attn_out_proj_w"]), "m_lnw": a["L1_attn_ln_w"],
        "m_lnb": a["L1_attn_ln_b"], "m_D": a["L1_attn_D"], "m_dtb": a["L1_attn_dt_bias"], "m_A": a["L1_attn_A_log"],
        "m_conv": a["L1_attn_conv_w"], "m_cb": T(a["L1_attn_conv_b"].reshape(NCH, P)), "m_nw": T(a["L1_attn_norm_w"].reshape(4, P)),
        "f_g": T(a["L1_ffn_w_gate"]), "f_u": T(a["L1_ffn_w_up"]), "f_d": T(a["L1_ffn_w_down"]),
        "e_gu": a["L0_ffn_gate_up_proj"], "e_dn": a["L0_ffn_down_proj"],
    }


def build(nc, arrays):
    I = {k: nc.dram_tensor("in_" + k, v.shape, mybir.dt.from_np(v.dtype), kind="ExternalInput").ap() for k, v in arrays.items()}
    out = nc.dram_tensor("out_x", (TOK, D), mybir.dt.float32, kind="ExternalOutput").ap()
    return perceiver_kernel(nc, I, out)


def kernel(**inputs):
    import concourse.bacc as bacc
    from concourse.bass_utils import run_bass_kernel_spmd

    arrays = layouts({k: np.asarray(v) for k, v in inputs.items()})
    nc = bacc.Bacc("TRN2", target_bir_lowering=False, num_devices=1)
    build(nc, arrays)
    r = run_bass_kernel_spmd(nc, [{"in_" + k: v for k, v in arrays.items()}], core_ids=[0])
    return r.results[0]["out_x"].reshape(B, S, D)
```

```python
import concourse.bass as bass
from concourse import mybir
from contextlib import ExitStack
import numpy as np

ORDER = {
    "setup_vector": """
        ones0 ones1 ones_n0 ones_l0 ones_n1 ones_l1 zero negmask""",
    "attn0_tensor": """
        trA q qk sc_0 sc_1 pt ov_0 ov_1 ot_0 ot_1 wv_0 wv_1""",
    "attn0_scalar": """
        xnT_A q_bias0 q_bias1 qk_evac0 qk_evac1 exp0 exp1 oT_evac0_0 oT_evac1_0 oT_evac0_1 oT_evac1_1""",
    "attn0_vector": """
        lnA_stats0 lnA_stats1 lnA_mean0 lnA_mean1 lnA_var lnA_norm0 lnA_norm1 row_max0 row_max1 pT_evac rsum
        ov_evac0 ov_evac1 x_attn0 x_attn1""",
    "attn0_gpsimd": """
        lnA_rstd""",
    "norm_tensor": """
        trB""",
    "norm_scalar": """
        xnT_B""",
    "norm_vector": """
        lnB_stats0 lnB_stats1 lnB_mean0 lnB_mean1 lnB_var lnB_norm0 lnB_norm1""",
    "norm_gpsimd": """
        lnB_rstd""",
    "linear_tensor": """
        qk_0 qk_1 v qt kv_0_0 kv_0_1 ks kv_1_0 kv_1_1 at trC""",
    "linear_scalar": """
        square0 square1 vblk0_0 vblk0_1 vblk0_2 vblk0_3 sp_exp0 sp_exp1 softplus0 softplus1 vblk1_0 vblk1_1 vblk1_2
        vblk1_3 qt_evac xnT_C""",
    "linear_vector": """
        ss0 ss1 ss_max rn_half rn_y0 rn_yy0 rn_syy0 rn_y1 rn_yy1 rn_syy1 rn_y2 rn_yy2 rn_syy2 rn_y3 unit0 unit1
        kv_evac0_0 kv_evac0_1 den_mul den rden kv_evac1_0 kv_evac1_1 at_norm x_lin lnC_stats0 lnC_stats1 lnC_mean0
        lnC_mean1 lnC_var lnC_norm0 lnC_norm1 xm0 xm1""",
    "linear_gpsimd": """
        lnC_rstd xnT_all""",
    "routing_vector": """
        logits top tops tops_down down expert onehot gate_1p gate rank_oh over7 rank novf q7 oend q obase e7 base_oh
        etab_sum base etab_min etab_n t1 etab past t2 t3 tile slot1 slot2 slot""",
    "shared_tensor": """
        gu0 gu1 gu2 lg gu3 rank count gu4 gu5 gu6 gu7 down0 down1 down2 down3 down4 down5 down6 down7""",
    "shared_scalar": """
        silu0 silu1 silu2 silu3 gate_exp xm0 xm1 xm2 xm3 xm4 xm5 xm6 xm7 silu4 silu5 silu6 silu7""",
    "shared_vector": """
        h0 h1 h2 h3 h4 h5 h6 h7 x0 x1 x2 x3 x4 x5 x6 x7""",
    "experts_tensor": """
        xt0 gu0 xt1 gu1 xt2 dn0 gu2 xt3 dn1 gu3 dn2 dn3""",
    "experts_scalar": """
        xT0 xT1 silu0 xT2 silu1 xT3 silu2 silu3""",
    "experts_vector": """
        h0 h1 y0 h2 y1 h3 y2 y3""",
    "overflow_tensor": """
        xt gu dn""",
    "overflow_scalar": """
        xT silu""",
    "overflow_vector": """
        h y""",
    "x_experts_vector": """
        x0 x1 x2 x3 x4 x5 x6 x7""",
    "attn1_tensor": """
        q0 q1 qk0 qk1 qk2 qk3 qk4 qk5 qk6 qk7 sc0 sc1 sc2 pt0 sc3 pt1 ov0 sc4 pt2 ov1 opT0 sc5 pt3 ov2 opT1 sc6 pt4
        ov3 opT2 sc7 pt5 ov4 opT3 sc8 pt6 ov5 opT4 sc9 pt7 ov6 opT5 sc10 pt8 ov7 opT6 sc11 pt9 ov8 opT7 sc12 pt10
        ov9 opT8 sc13 pt11 ov10 opT9 sc14 pt12 ov11 opT10 sc15 pt13 ov12 opT11 pt14 ov13 opT12 pt15 ov14 opT13 ov15
        opT14 opT15 o0 o1 wo0 wo1""",
    "attn1_scalar": """
        q_evac0 q_evac1 qk_evac0 qk_evac1 qk_evac2 qk_evac3 qk_evac4 qk_evac5 qk_evac6 qk_evac7 exp0 exp1 exp2
        pT_evac0 exp3 pT_evac1 exp4 pT_evac2 exp5 pT_evac3 exp6 pT_evac4 exp7 pT_evac5 exp8 pT_evac6 exp9 pT_evac7
        exp10 pT_evac8 exp11 pT_evac9 exp12 pT_evac10 exp13 pT_evac11 exp14 pT_evac12 exp15 pT_evac13 pT_evac14
        pT_evac15 o_evac0 o_evac1""",
    "attn1_vector": """
        qk_evac0 qk_evac1 qk_evac2 qk_evac3 qk_evac4 qk_evac5 qk_evac6 qk_evac7 row_max0 row_max1 rsum0 norm0
        row_max2 rsum1 norm1 row_max3 rsum2 norm2 ov_evac0 row_max4 rsum3 norm3 ov_evac1 opT_evac0 row_max5 rsum4
        norm4 ov_evac2 opT_evac1 row_max6 rsum5 norm5 ov_evac3 opT_evac2 row_max7 rsum6 norm6 ov_evac4 opT_evac3
        row_max8 rsum7 norm7 ov_evac5 opT_evac4 row_max9 rsum8 norm8 ov_evac6 opT_evac5 row_max10 rsum9 norm9
        ov_evac7 opT_evac6 row_max11 rsum10 norm10 ov_evac8 opT_evac7 row_max12 rsum11 norm11 ov_evac9 opT_evac8
        row_max13 rsum12 norm12 ov_evac10 opT_evac9 row_max14 rsum13 norm13 ov_evac11 opT_evac10 row_max15 rsum14
        norm14 ov_evac12 opT_evac11 rsum15 norm15 ov_evac13 opT_evac12 ov_evac14 opT_evac13 ov_evac15 opT_evac14
        opT_evac15 bias0 bias1 x0 x1""",
    "attn1_norm_vector": """
        ln_stats0 ln_stats1 ln_mean0 ln_mean1 ln_var ln_norm0 ln_norm1""",
    "scan_norm_vector": """
        ln1_stats0 ln1_stats1 ln1_mean0 ln1_mean1 ln1_var ln1_norm0 ln1_norm1 ln2_stats0 ln2_stats1 ln2_mean0
        ln2_mean1 ln2_var ln2_norm0 ln2_norm1 ln_w u""",
    "ffn_norm_vector": """
        ln_stats0 ln_stats1 ln_mean0 ln_mean1 ln_var ln_norm0 ln_norm1""",
    "attn1_norm_gpsimd": """
        ln_rstd""",
    "scan_norm_gpsimd": """
        ln1_rstd ln2_rstd""",
    "ffn_norm_gpsimd": """
        ln_rstd""",
    "attn1_transposes_tensor": """
        tr""",
    "ffn_transposes_tensor": """
        tr""",
    "attn1_transposes_scalar": """
        xnT""",
    "ffn_transposes_scalar": """
        xnT""",
    "attn1_setup_vector": """
        rows_one row_zero op_zero0 op_zero1""",
    "scan_tensor": """
        tr dt xbc2 xbc0 xbc1 cum cumT0 z0 z1 G0 G1 cumT1 xs0 xs1 y0 y1 yT0 yT1 out0 out1""",
    "scan_scalar": """
        uT dt_exp xp2 tap3_4 tap3_5 xp0 tap3_0 tap3_1 xp1 tap3_2 tap3_3 tanh2 relu0_0 relu0_1 relu0_2 relu0_3
        relu0_4 relu0_5 relu0_6 relu0_7 decay0 z_tanh0 z_tanh1 tanh0 tanh1 relu1_0 relu1_1 relu1_2 relu1_3 relu1_4
        relu1_5 relu1_6 relu1_7 xs_evac0 xs_evac1 decay1 square0 yT_evac0 square1 yT_evac1""",
    "scan_vector": """
        dt_raw dt_abs dt_pos dt_2e dt_r dt_s dt_s2 dt_p15 dt_p13 dt_p11 dt_p9 dt_p7 dt_p5 dt_p3 dt_p1 dt dtA tap0_4
        tap0_5 tap1_4 tap1_5 tap2_4 tap2_5 cum tap0_0 tap0_1 tap1_0 tap1_1 tap2_0 tap2_1 silu2 tap0_2 tap0_3 tap1_2
        tap1_3 tap2_2 tap2_3 gm0 gm1 silu0 silu1 M0 z_silu0 z_silu1 xdt0 xdt1 xr0 xr1 M1 ya0 yz0 ya1 yz1 mean_square
        x0 x1""",
    "scan_gpsimd": """
        xD0 xD1 rms""",
    "scan_setup_vector": """
        pad nw0 nw1 nw2 nw3 D A""",
    "scan_setup_scalar": """
        expA""",
    "ffn_tensor": """
        g0 u0 g1 u1 g2 u2 down""",
    "ffn_scalar": """
        silu0 silu1 silu2""",
    "ffn_vector": """
        h0 h1 h2 x""",
    "ffn_weights_float": """
        int0 int1 int2""",
}
ORDER = {k: v.split() for k, v in ORDER.items()}

P = 128
B, S, D = 32, 32, 256
TOK = B * S
NT = TOK // P
BT = P // S
KEYS, DC = 257, 192
DC2 = DC - P
NPAIR = NT // 2
PW = 2 * P
H0, HD0 = 16, 16
E, F0 = 16, 512
RING = 4
NOVF = (TOK - 1) // P
H1, HD1 = 8, 64
INNER = H1 * HD1
HM, HDM, NST = 8, 64, 128
DIN = HM * HDM
TAPS = 4
NCH = (DIN + 2 * NST) // P
F1 = 768
MASKED = -(2.0 ** 127)


class Steps:

    def __init__(self, name, sem):
        self.key, self.sem, self.n = name, sem, 0
        self.known = ORDER.get(name)
        self.names = list(self.known or [])

    def done(self, name):
        if self.known:
            assert self.names[self.n % len(self.names)] == name, (self.key, name, self.names[self.n % len(self.names)])
        else:
            self.names += [name] * (name not in self.names)
        self.n += 1
        return self.sem

    def after(self, name, rnd=0):
        if not self.known:
            return self.sem, 1
        return self.sem, (rnd + 1) * len(self.names) + (self.names.index(name) + 1)

    def sem_value(self, name):
        return self.sem, (self.names.index(name) + 1 if self.known else 1)

    def all(self, rounds=1):
        return self.sem, (rounds + 1) * max(len(self.names), 1)

    def round(self):
        return max(len(self.names), 1)


def host_constants():
    s = np.arange(P)
    same = (s[:, None] // S) == (s[None, :] // S)
    parts = {
        "ident": np.eye(P),
        "tri": same & (s[:, None] <= s[None, :]),
        "gmask": (same & (s[:, None] <= s[None, :])) / 16.0,
        "same": same,
        "before": s[:, None] < s[None, :],
        "hmask": ((s[:, None] // HD0) == (s[None, :] // HD0)) * HD0 ** -0.5,
        "ones": np.ones((P, P)),
        "inb": (s[:, None] // S) == np.arange(BT)[None, :],
        "iota": np.tile(np.arange(E), (P, 1)),
        "down": np.tile(E - np.arange(E), (P, 1)),
        "caps": np.tile(P * np.arange(1, NT), (P, 1)),
        "nth": np.tile(np.arange(NOVF), (P, 1)),
        "mhalf": np.full((P, 64), -0.5),
        "zeros": np.zeros((P, E)),
    }
    at, cols = {}, 0
    for k, v in parts.items():
        at[k] = (cols, v.shape[1])
        cols += v.shape[1]
    return np.concatenate([np.asarray(v, np.float32) for v in parts.values()], 1), at


def perceiver_kernel(nc, I, out):
    fp32, i32, u32, u8 = mybir.dt.float32, mybir.dt.int32, mybir.dt.uint32, mybir.dt.uint8
    ALU, ACT, AX = mybir.AluOpType, mybir.ActivationFunctionType, mybir.AxisListType.X
    _, CONST = host_constants()
    ctx = ExitStack()
    with ctx:
        big = ctx.enter_context(nc.sbuf_tensor("big", [P, SBUF_COLS], fp32))
        ps = ctx.enter_context(nc.psum_tensor("ps", [P, 8, 512], fp32))
        high = [0]

        def region(start):
            at = [start]

            def take(*dims):
                n = int(np.prod(dims))
                v = big[:, at[0]:at[0] + n]
                at[0] += n + (n & 1)
                high[0] = max(high[0], at[0])
                if len(dims) == 2:
                    v = v.rearrange("p (a b) -> p a b", b=dims[1])
                elif len(dims) == 3:
                    v = v.rearrange("p (a b c) -> p a b c", b=dims[1], c=dims[2])
                elif len(dims) == 4:
                    v = v.rearrange("p (a b c d) -> p a b c d", b=dims[1], c=dims[2], d=dims[3])
                return v
            return take, at

        keep, at = region(0)
        x = keep(NT, D)
        const = keep(CONST["zeros"][0] + CONST["zeros"][1])
        K = {k: const[:, a:a + n] for k, (a, n) in CONST.items()}
        ident = K["ident"]
        LN, LNX, LNB = ((keep(2, 6), keep(2, 2), keep(2), keep(2)) for _ in range(3))
        oneh, eidx = keep(NT, E), keep(NT)
        negmask, zrow = keep(KEYS), keep(D)
        etab = keep(NOVF + 1)
        mask8 = keep(66)
        cT1 = [keep(BT, KEYS) for _ in range(2)]
        cT2 = [keep(BT, KEYS) for _ in range(2)]
        cN = [keep(BT, 2, DC + 1) for _ in range(2)]
        cLq = [keep(DC + 1) for _ in range(2)]
        cLb = [keep(BT, DC) for _ in range(2)]
        w0 = at[0]
        wts, at = region(w0)
        wq, bq, wk, wv1, wv2 = wts(2, D), wts(2), wts(2, DC + 1), wts(D), wts(D)
        wqkv, wr = wts(2, 3 * D), wts(2, E)
        sg_w, su_w, sd_w = wts(2, F0), wts(2, F0), wts(4, D)
        w1 = at[0]
        ring_gu = [wts(2, 2 * F0) for _ in range(RING)]
        ring_dn = [wts(4, D) for _ in range(RING)]
        w2 = at[0]
        w4, at4 = region(w0)
        m_in, m_out = w4(2, 2 * DIN + 2 * NST + HM), w4(4, D)
        m_lnw, m_lnb, m_D, m_conv, m_cb = w4(D), w4(D), w4(HM), w4(NCH, TAPS), w4(NCH)
        m_nw, m_dtb, m_A = w4(4), w4(HM), w4(HM)
        assert at4[0] <= w1, (at4[0], w1)
        w5, at5 = region(w1)
        f_gi, f_ui, f_di = w5(2, F1), w5(2, F1), w5(6, D)
        f_g, f_u, f_d = w5(2, F1), w5(2, F1), w5(6, D)
        assert at5[0] <= w2, (at5[0], w2)
        w3, at = region(w2)
        c_wq, c_wk, c_wv, c_wo, c_bo = w3(2, INNER), w3(H1, DC), w3(2, INNER), w3(4, D), w3(D)
        work0 = at[0]
        a12, at = region(work0)
        xm, xnT_all = a12(NT, D), a12(2, TOK)
        lg, lg_top, gate = a12(NT, E), a12(NT), a12(NT)
        work1 = at[0]
        a1, at1 = region(work1)
        xnx = [a1(D) for _ in range(2)]
        xnT_x, xnT_a, qT, qpT = (a1(2, PW) for _ in range(4))
        pr = [a1(KEYS) for _ in range(2)]
        pT = a1(2, 2, P)
        op = [a1(DC + 1) for _ in range(2)]
        oT = [a1(2, P) for _ in range(2)]
        nmx, sm, ri = a1(2), a1(2), a1(2)
        assert at1[0] - work1 >= 4 * TOK
        xn = [a1(D) for _ in range(2)]
        xnT = a1(2, PW)
        ss, rn, rt = a1(2, 32), a1(2, 32), a1(2, 32)
        fqk2 = a1(2, 512)
        fqk = [fqk2[:, j, :] for j in range(2)]
        vblk = [a1(2, BT, P) for _ in range(2)]
        kvm = [a1(2, BT, P) for _ in range(2)]
        dtmp = a1(2, D)
        den = a1(32)
        qtT = a1(2, 2, P)

        a2, _ = region(work1)
        hs = a2(4, TOK)
        sgate = [c_wq[:, k, :] for k in range(2)]
        xg = [a2(D) for _ in range(RING)]
        xgT = [a2(2, P) for _ in range(2)]
        egate = [a2(4, P) for _ in range(2)]
        eh = [a2(4, P) for _ in range(2)]
        ey = [a2(D) for _ in range(RING)]
        r_oh, rank, cnt7, novf, oend, obase = a2(NT, E), a2(NT), a2(E, NT - 1), a2(E), a2(E), a2(E)
        r_q7, rq, r_bt, r_g, r_t, slot_f, slot_i = a2(NT, NT - 1), a2(NT), a2(NT), a2(NT), a2(NT), a2(NT), a2(NT)
        r_e7, etab_f = a2(NOVF, E), a2(NOVF + 1)
        yg = xm

        a3, at3 = region(work0)
        qp3 = a3(2, 2 * BT, H1 * S)
        assert NT * D == 2 * BT * H1 * S
        xn3 = [a3(D) for _ in range(2)]
        xnT3, q3 = a3(2, PW), a3(4, PW)
        pr3 = [a3(KEYS) for _ in range(4)]
        nmx3, sm3, rs3 = a3(4), a3(4), a3(4)
        pT3 = [a3(2, P) for _ in range(2)]
        op3 = [a3(2 * P) for _ in range(2)]
        oT3 = a3(2, 2, H1, P)
        o3T = a3(4, PW)
        t3 = [a3(D) for _ in range(2)]

        a4, at4w = region(work0)
        uT4 = a4(2, PW)
        xp = a4(NCH, 2 * BT, S + TAPS - 1)
        cv, th = a4(NCH, PW), a4(NCH, PW)
        xs4, xdt, xD = ([a4(DIN) for _ in range(2)] for _ in range(3))
        zt, zs, y4 = ([a4(DIN) for _ in range(2)] for _ in range(3))
        dec = [a4(HM, P) for _ in range(2)]
        gm4 = [a4(P) for _ in range(2)]
        yT4 = [a4(4, P) for _ in range(2)]
        dts = {n: a4(2, HM) for n in ("d", "a", "m", "e", "e2", "r", "s", "s2", "p", "dt", "dtA", "cum")}
        ssq, rms = a4(2), a4(2)
        assert at4w[0] >= at3[0]
        xn4, u4 = a4(2, D), a4(2, D)
        xn5 = [a4(D) for _ in range(2)]
        a5, _ = region(work0)
        xnT5, sg5, h5 = a5(2, PW), a5(6, PW), a5(6, PW)

        bank = [ps[:, n, :] for n in range(8)]

        def sem(name):
            return ctx.enter_context(nc.semaphore(name))

        all_steps = []

        def steps(name):
            all_steps.append(Steps(name, sem(name + "_done")))
            return all_steps[-1]

        weights1_in, weights2_in, weights3_in, weights4_in, weights5_in = (sem(f"weights{n}_in") for n in range(1, 6))
        const_in, x0_in, x_in, weights_q_in = (sem(n) for n in ("const_in", "x_first_pair_in", "x_rest_in", "query_weights_in"))
        ctx_in = [sem(f"ctx_in{j}") for j in range(2)]
        x_out = sem("x_out")
        setup = steps("setup_vector")
        PEX, ACX, VEX, GPX = (steps("attn0_" + e) for e in ("tensor", "scalar", "vector", "gpsimd"))
        PEB, ACB, VEB, GPB = (steps("norm_" + e) for e in ("tensor", "scalar", "vector", "gpsimd"))
        PEL, ACL, VEL, GPL = (steps("linear_" + e) for e in ("tensor", "scalar", "vector", "gpsimd"))

        def view(a, pat, **kw):
            return a.rearrange(pat, **kw)

        tiles_dram = nc.dram_tensor("expert_in", ((E + NOVF) * P, D), fp32, kind="Internal").ap()
        ytiles_dram = nc.dram_tensor("expert_out", ((E + NOVF) * P, D), fp32, kind="Internal").ap()
        mask_dram = nc.dram_tensor("mask_add", (B, KEYS), fp32, kind="Internal").ap()
        zero_in, mask_out, scattered, weights_sh = (sem(n) for n in ("zero_in", "mask_out", "scattered", "shared_weights_in"))
        gathered0, gathered = sem("gathered_first_pair"), sem("gathered_rest")
        gu_in = [sem(f"gate_up_in{r}") for r in range(RING)]
        dn_in = [sem(f"down_in{r}") for r in range(RING)]
        xg_in = [sem(f"expert_tokens_in{r}") for r in range(RING)]
        y_out, ovf_in, ovf_out = sem("expert_out_stored"), sem("overflow_in"), sem("overflow_out")
        RT, SHP, SHA, SHV = steps("routing_vector"), steps("shared_tensor"), steps("shared_scalar"), steps("shared_vector")
        PE2, AC2, VE2 = (steps("experts_" + e) for e in ("tensor", "scalar", "vector"))
        PEO, ACO, VEO = (steps("overflow_" + e) for e in ("tensor", "scalar", "vector"))
        XE = steps("x_experts_vector")
        NR = E // RING
        PE3, AC3, VE3 = (steps("attn1_" + e) for e in ("tensor", "scalar", "vector"))
        VN3, VN4, VN5 = (steps(a + "_norm_vector") for a in ("attn1", "scan", "ffn"))
        GN3, GN4, GN5 = (steps(a + "_norm_gpsimd") for a in ("attn1", "scan", "ffn"))
        PT3, PT5 = (steps(a + "_transposes_tensor") for a in ("attn1", "ffn"))
        AT3, AT5 = (steps(a + "_transposes_scalar") for a in ("attn1", "ffn"))
        set3 = steps("attn1_setup_vector")
        PE4, AC4, VE4, GP4 = (steps("scan_" + e) for e in ("tensor", "scalar", "vector", "gpsimd"))
        set4, set4a = steps("scan_setup_vector"), steps("scan_setup_scalar")
        PE5, AC5, VE5 = (steps("ffn_" + e) for e in ("tensor", "scalar", "vector"))
        ints = steps("ffn_weights_float")
        wk_zero = sem("attn1_zero_done")
        NU = 2 * BT * 2
        CTX3 = 16 * 5

        passed = sem("waits_passed")

        def wait_alone(eng, semaphore, value):
            eng.wait_ge(semaphore, value)
            eng.sem_inc(passed, 1)

        def norm_stats(dve, V, tag, p, src, eps, scratch=LN):
            st, mv, ve, _ = scratch
            for j in range(2):
                nc.vector.bn_stats(st[:, j, :], src(j)).then_inc(V.done(f"{tag}_stats{j}"), 1)
            for j in range(2):
                wait_alone(dve, *V.after(f"{tag}_stats{j}", p))
                nc.vector.bn_aggr(mv[:, j, :], st[:, j, :]).then_inc(V.done(f"{tag}_mean{j}"), 1)
            dve.wait_ge(*V.after(f"{tag}_mean1", p))
            nc.vector.tensor_scalar_add(ve, mv[:, :, 1], eps).then_inc(V.done(f"{tag}_var"), 1)

        def norm_apply(dve, V, G, tag, p, src, dst, scratch=LN):
            _, mv, _, rstd = scratch
            dve.wait_ge(*G.after(f"{tag}_rstd", p))
            for j in range(2):
                nc.vector.tensor_scalar(dst(j), src(j), mv[:, j, 0:1], rstd[:, j:j + 1], ALU.subtract,
                                        ALU.mult).then_inc(V.done(f"{tag}_norm{j}"), 1)

        def layer_norm_vector(dve, V, G, tag, p, src, dst, eps):
            norm_stats(dve, V, tag, p, src, eps)
            norm_apply(dve, V, G, tag, p, src, dst)

        def layer_norm_gpsimd(pool, V, G, tag, p, scratch=LN):
            pool.wait_ge(*V.after(f"{tag}_var", p))
            nc.gpsimd.tensor_tensor(scratch[3], scratch[2], K["mhalf"][:, 0:2], ALU.pow).then_inc(G.done(f"{tag}_rstd"), 1)

        def load_expert(sp, r, e):
            if isinstance(e, int):
                gu, dn = I["e_gu"][e], I["e_dn"][e]
                sp.dma_start(ring_gu[r], gu.rearrange("(k p) n -> p k n", p=P)).then_inc(gu_in[r], 16)
                sp.dma_start(ring_dn[r], dn.rearrange("(k p) n -> p k n", p=P)).then_inc(dn_in[r], 16)
            else:
                sp.dma_start(ring_gu[r], I["e_gu"][bass.ds(e, 1), :, :].rearrange("a (k p) n -> p (a k) n", p=P)).then_inc(gu_in[r], 16)
                sp.dma_start(ring_dn[r], I["e_dn"][bass.ds(e, 1), :, :].rearrange("a (k p) n -> p (a k) n", p=P)).then_inc(dn_in[r], 16)

        def load_tokens(sp, r, it):
            sp.wait_ge(scattered, 16 * NT)
            sp.dma_start(xg[r], tiles_dram[bass.ds(it * (RING * P) + r * P, P), :]).then_inc(xg_in[r], 16)

        def load_context3(sp, j, t):
            load_context(sp, j, t)
            sp.dma_start(cT2[j][DC2 + 1:DC2 + 2], mask_dram[bass.ds(t * BT, BT), :].unsqueeze(0)).then_inc(ctx_in[j], 16)
            sp.dma_start(view(cLb[j], "p a b -> p (a b)"),
                         I["ctx_last"].rearrange("(t b) d -> t (b d)", b=BT)[bass.ds(t, 1), :].partition_broadcast(P)).then_inc(ctx_in[j], 16)

        def load_context(sp, j, t):
            sp.dma_start(cT1[j], I["ctx_T"][t, 0:P, :, :]).then_inc(ctx_in[j], 16)
            sp.dma_start(cT2[j][0:DC2], I["ctx_T"][t, P:DC, :, :]).then_inc(ctx_in[j], 16)
            sp.dma_start(cN[j].rearrange("p b c d -> p (b c) d")[:, :, 0:DC], I["ctx_N"][t]).then_inc(ctx_in[j], 16)

        SC, OV, OT, WV, KV = (0, 3), (2, 0), (3, 1), (2, 0), ((5, 6), (4, 5))
        CTX1 = 16 * (3 + BT)

        block = ctx.enter_context(nc.Block())

        @block.sync
        def _(sp):
            def load_context1(p):
                for j in range(2):
                    t = p * 2 + j
                    load_context(sp, j, t)
                    for b in range(BT):
                        sp.dma_start(cLq[j][S * b:S * b + S, 0:DC],
                                     I["ctx_last"][bass.ds(t * BT + b, 1), :].partition_broadcast(S)).then_inc(ctx_in[j], 16)

            x_tiles = I["x"].rearrange("(t p) d -> p t d", p=P)
            sp.dma_start(x[:, 0:2, :], x_tiles[:, 0:2, :]).then_inc(x0_in, 16)
            sp.dma_start(const, I["consts"]).then_inc(const_in, 16)
            sp.dma_start(bq, I["bq"]).then_inc(weights_q_in, 16)
            for dst, src in ((wq, I["wq"]), (wk, I["wk"])):
                sp.dma_start(dst, src.rearrange("(k p) n -> p k n", p=P)).then_inc(weights_q_in, 16)
            load_context1(0)
            sp.dma_start(wv1, I["wv"][0:P, :]).then_inc(weights1_in, 16)
            sp.dma_start(wv2[0:DC2 + 1, :], I["wv"][P:DC + 1, :]).then_inc(weights1_in, 16)
            for dst, src in ((wqkv, I["wqkv"]), (wr, I["wr"])):
                sp.dma_start(dst, src.rearrange("(k p) n -> p k n", p=P)).then_inc(weights1_in, 16)
            sp.dma_start(x[:, 2:, :], x_tiles[:, 2:, :]).then_inc(x_in, 16)
            sp.dma_start(mask8[0:B, 0:65].bitcast(u8)[:, 0:KEYS], I["mask"]).then_inc(weights1_in, 16)
            for dst, src in ((sg_w, I["s_g"]), (su_w, I["s_u"]), (sd_w, I["s_d"])):
                sp.dma_start(dst, src.rearrange("(k p) n -> p k n", p=P)).then_inc(weights_sh, 16)
            with sp.Fori(1, NPAIR) as p:
                for j in range(2):
                    wait_alone(sp, *PEX.after(f"ov_{j}", p - 1))
                    wait_alone(sp, *VEX.after(f"ov_evac{j}", p - 1))
                load_context1(p)
            for r in range(RING):
                load_expert(sp, r, r)
            sp.wait_ge(*setup.sem_value("zero"))
            sp.dma_start(tiles_dram.rearrange("(n p) d -> p n d", p=P), zrow.unsqueeze(1).broadcast_to((P, E + NOVF, D)))\
                .then_inc(zero_in, 16)
            sp.dma_start(ytiles_dram[E * P:, :].rearrange("(n p) d -> p n d", p=P), zrow.unsqueeze(1).broadcast_to((P, NOVF, D)))\
                .then_inc(zero_in, 16)
            sp.wait_ge(*setup.sem_value("negmask"))
            sp.dma_start(mask_dram, negmask[0:B, :]).then_inc(mask_out, 16)
            sp.wait_ge(*PEX.all(NPAIR))
            sp.wait_ge(*VEX.all(NPAIR))
            sp.wait_ge(mask_out, 16)
            for j in range(2):
                load_context3(sp, j, j)
            sp.dma_start(c_wo, I["c_wo"].rearrange("(k p) n -> p k n", p=P)).then_inc(weights3_in, 16)
            sp.wait_ge(wk_zero, 1)
            for hp in range(2):
                sp.dma_start(view(c_wk, "p (g two) d -> p g two d", two=2)[hp * HD1:(hp + 1) * HD1, :, hp, :],
                             I["c_wk"].rearrange("(g two e) d -> e g two d", two=2, e=HD1)[:, :, hp, :]).then_inc(weights3_in, 16)
            sp.dma_start(c_wv[:, 0, :], I["c_wv"][0:P, :]).then_inc(weights3_in, 16)
            sp.dma_start(c_wv[0:DC2, 1, :], I["c_wv"][P:DC, :]).then_inc(weights3_in, 16)
            sp.dma_start(c_bo, I["c_bo"].partition_broadcast(P)).then_inc(weights3_in, 16)
            sp.wait_ge(*SHV.sem_value("h7"))
            sp.dma_start(c_wq, I["c_wq"].rearrange("(k p) n -> p k n", p=P)).then_inc(weights3_in, 16)
            for r in range(RING):
                load_tokens(sp, r, 0)
            with sp.Fori(1, NR) as it:
                for r in range(RING):
                    sp.wait_ge(*PE2.after(f"dn{r}", it - 1))
                    load_expert(sp, r, it * RING + r)
                    load_tokens(sp, r, it)
            sp.wait_ge(*RT.sem_value("etab"))
            n_over = sp.value_load(etab.bitcast(i32)[0:1, NOVF:NOVF + 1], min_val=0, max_val=NOVF)
            with sp.If(n_over > 0):
                sp.wait_ge(*PE2.all(NR))
                with sp.Fori(0, NOVF) as i:
                    sp.wait_ge(*PEO.after("dn", i - 1))
                    e = sp.value_load(etab.bitcast(i32)[0:1, bass.ds(i, 1)], min_val=0, max_val=E - 1)
                    sp.dma_start(ring_gu[0], I["e_gu"][bass.ds(e, 1), :, :].rearrange("a (k p) n -> p (a k) n", p=P)).then_inc(ovf_in, 16)
                    sp.dma_start(ring_dn[0], I["e_dn"][bass.ds(e, 1), :, :].rearrange("a (k p) n -> p (a k) n", p=P)).then_inc(ovf_in, 16)
                    sp.dma_start(xg[0], tiles_dram[bass.ds(i * P + E * P, P), :]).then_inc(ovf_in, 16)
            sp.wait_ge(*XE.sem_value("x7"))
            sp.dma_start(m_in, I["m_in"].rearrange("(k p) n -> p k n", p=P)).then_inc(weights4_in, 16)
            sp.dma_start(m_out, I["m_out"].rearrange("(k p) n -> p k n", p=P)).then_inc(weights4_in, 16)
            for dst, src in ((m_lnw, "m_lnw"), (m_lnb, "m_lnb"), (m_D, "m_D"), (m_dtb, "m_dtb"), (m_A, "m_A")):
                sp.dma_start(dst, I[src].partition_broadcast(P)).then_inc(weights4_in, 16)
            sp.dma_start(m_conv, I["m_conv"].rearrange("(c p) t -> p c t", p=P)).then_inc(weights4_in, 16)
            sp.dma_start(m_cb, I["m_cb"]).then_inc(weights4_in, 16)
            sp.dma_start(m_nw, I["m_nw"]).then_inc(weights4_in, 16)
            for dst, src in ((f_gi, "f_g"), (f_ui, "f_u"), (f_di, "f_d")):
                sp.dma_start(dst.bitcast(i32), I[src].rearrange("(k p) n -> p k n", p=P)).then_inc(weights5_in, 16)
            with sp.Fori(1, NPAIR) as p:
                for j in range(2):
                    u = NU // 2 * (j + 1) - 1
                    wait_alone(sp, *PE3.after(f"ov{u}", p - 1))
                    wait_alone(sp, *VE3.after(f"ov_evac{u}", p - 1))
                    load_context3(sp, j, p * 2 + j)
            with sp.Fori(0, NPAIR) as p:
                sp.wait_ge(*VE5.after("x", p))
                sp.dma_start(out.rearrange("(t p) d -> p t d", p=P)[:, bass.ds(p * 2, 2), :], x[:, bass.ds(p * 2, 2), :]).then_inc(x_out, 16)
            sp.wait_ge(x_out, 16 * NPAIR)

        @block.gpsimd
        def _(pool):
            nc.gpsimd.memset(view(c_wk, "p a b -> p (a b)"), 0.0).then_inc(wk_zero, 1)
            pool.sem_inc(GPX.sem, GPX.round())
            pool.sem_inc(GPL.sem, GPL.round())
            pool.sem_inc(GPB.sem, GPB.round())

            def linear_gpsimd(p, nxt):
                if nxt is not None:
                    layer_norm_gpsimd(pool, VEX, GPX, "lnA", nxt, LNX)
                if nxt is not None:
                    layer_norm_gpsimd(pool, VEB, GPB, "lnB", nxt, LNB)
                layer_norm_gpsimd(pool, VEL, GPL, "lnC", p)
                pool.wait_ge(*ACL.after("xnT_C", p))
                nc.gpsimd.tensor_copy(xnT_all[:, :, bass.ds(p * PW, PW)], xnT).then_inc(GPL.done("xnT_all"), 1)

            pool.wait_ge(const_in, 16)
            layer_norm_gpsimd(pool, VEX, GPX, "lnA", 0, LNX)
            layer_norm_gpsimd(pool, VEB, GPB, "lnB", 0, LNB)
            with pool.Fori(0, NPAIR - 1) as p:
                linear_gpsimd(p, p + 1)
            linear_gpsimd(NPAIR - 1, None)
            pool.wait_ge(zero_in, 32)
            pool.wait_ge(*RT.sem_value("slot"))
            pool.wait_ge(*SHA.sem_value(f"xm{NT - 1}"))
            for t in range(NT):
                pool.indirect_dma_start(out=tiles_dram, out_offset=bass.IndirectOffsetOnAxis(slot_i[:, t:t + 1].bitcast(i32), 0),
                                        in_=xm[:, t, :], in_offset=None).then_inc(scattered, 16)
            with pool.Fori(0, NR) as it:
                for r in range(RING):
                    pool.wait_ge(*VE2.after(f"y{r}", it))
                    pool.dma_start(ytiles_dram[bass.ds(it * (RING * P) + r * P, P), :], ey[r]).then_inc(y_out, 16)
            pool.wait_ge(y_out, 16 * E)
            n_over = pool.value_load(etab.bitcast(i32)[0:1, NOVF:NOVF + 1], min_val=0, max_val=NOVF)
            with pool.If(n_over > 0):
                with pool.Fori(0, NOVF) as i:
                    pool.wait_ge(*VEO.after("y", i))
                    pool.dma_start(ytiles_dram[bass.ds(i * P + E * P, P), :], ey[0]).then_inc(ovf_out, 16)
                pool.wait_ge(ovf_out, 16 * NOVF)
            pool.wait_ge(scattered, 16 * NT)
            for t in range(NT):
                pool.indirect_dma_start(out=yg[:, t, :], out_offset=None, in_=ytiles_dram,
                                        in_offset=bass.IndirectOffsetOnAxis(slot_i[:, t:t + 1].bitcast(i32), 0))\
                    .then_inc(gathered0 if t < 2 else gathered, 16)
            pool.sem_inc(GN3.sem, GN3.round())
            with pool.Fori(0, NPAIR) as p:
                layer_norm_gpsimd(pool, VN3, GN3, "ln", p)
            pool.wait_ge(weights5_in, 48)
            for n, (dst, src) in enumerate(((f_g, f_gi), (f_u, f_ui), (f_d, f_di))):
                nc.gpsimd.tensor_copy(dst, src.bitcast(i32)).then_inc(ints.done(f"int{n}"), 1)
            pool.sem_inc(GP4.sem, GP4.round())
            pool.sem_inc(GN4.sem, GN4.round())
            pool.sem_inc(GN5.sem, GN5.round())

            def scan_gpsimd(p, nxt):
                for j in range(2):
                    pool.wait_ge(*AC4.after(f"xs_evac{j}", p))
                    nc.gpsimd.tensor_tensor(view(xD[j], "p (h e) -> p h e", h=HM), view(xs4[j], "p (h e) -> p h e", h=HM),
                                            m_D.unsqueeze(2).broadcast_to((P, HM, HDM)), ALU.mult).then_inc(GP4.done(f"xD{j}"), 1)
                if nxt is not None:
                    layer_norm_gpsimd(pool, VN4, GN4, "ln1", nxt)
                    layer_norm_gpsimd(pool, VN4, GN4, "ln2", nxt)
                else:
                    layer_norm_gpsimd(pool, VN5, GN5, "ln", 0)
                pool.wait_ge(*VE4.after("mean_square", p))
                nc.gpsimd.tensor_tensor(rms, ssq, K["mhalf"][:, 0:2], ALU.pow).then_inc(GP4.done("rms"), 1)

            layer_norm_gpsimd(pool, VN4, GN4, "ln1", 0)
            layer_norm_gpsimd(pool, VN4, GN4, "ln2", 0)
            pool.wait_ge(*set4.sem_value("D"))
            with pool.Fori(0, NPAIR - 1) as p:
                scan_gpsimd(p, p + 1)
            scan_gpsimd(NPAIR - 1, None)
            with pool.Fori(1, NPAIR) as p:
                layer_norm_gpsimd(pool, VN5, GN5, "ln", p)

        @block.scalar
        def _(act):
            act.sem_inc(ACX.sem, ACX.round())
            act.sem_inc(ACL.sem, ACL.round())
            act.sem_inc(ACB.sem, ACB.round())
            act.wait_ge(const_in, 16)
            act.wait_ge(weights_q_in, 16 * 3)

            def xnT_evac(PEn, ACn, dst, bk, tag, pe_step, p):
                act.wait_ge(*PEn.after(pe_step, p))
                nc.scalar.copy(view(dst, "p a b -> p (a b)"), bk).then_inc(ACn.done(tag), 1)

            def queries(p):
                act.wait_ge(*PEX.after("q", p))
                for k in range(2):
                    nc.scalar.activation(qT[:, k, :], bank[1][:, k * PW:(k + 1) * PW], ACT.Identity,
                                         bias=bq[:, k:k + 1]).then_inc(ACX.done(f"q_bias{k}"), 1)

            def queries_keys(p):
                act.wait_ge(*PEX.after("qk", p))
                nc.scalar.mul(qpT[:, 0, :], bank[2][:, 0:PW], D ** -0.5).then_inc(ACX.done("qk_evac0"), 1)
                nc.scalar.mul(qpT[0:DC2 + 1, 1, :], bank[2][0:DC2 + 1, PW:2 * PW], D ** -0.5)\
                    .then_inc(ACX.done("qk_evac1"), 1)

            def probabilities(p):
                for j in range(2):
                    act.wait_ge(*VEX.after(f"row_max{j}", p))
                    nc.scalar.activation(pr[j], bank[SC[j]][:, 0:KEYS], ACT.Exp, bias=nmx[:, j:j + 1],
                                         accum_out=sm[:, j:j + 1]).then_inc(ACX.done(f"exp{j}"), 1)

            def context_sums(p):
                for j in range(2):
                    act.wait_ge(*PEX.after(f"ot_{j}", p))
                    nc.scalar.copy(oT[j][:, 0, :], bank[OT[j]][:, 0:P]).then_inc(ACX.done(f"oT_evac0_{j}"), 1)
                    nc.scalar.copy(oT[j][0:DC2 + 1, 1, :], bank[OT[j]][0:DC2 + 1, P:2 * P])\
                        .then_inc(ACX.done(f"oT_evac1_{j}"), 1)

            def shared_silu(s):
                act.wait_ge(*SHP.sem_value(f"gu{s}"))
                if s >= 2:
                    act.wait_ge(*SHV.sem_value(f"h{s - 2}"))
                nc.scalar.activation(sgate[s % 2], bank[2 * (s % 2)], ACT.Silu).then_inc(SHA.done(f"silu{s}"), 1)

            def linear_scalar(p, nxt):
                for j in range(2):
                    act.wait_ge(*PEL.after(f"qk_{j}", p))
                    nc.scalar.activation(fqk[j], bank[5 + j], ACT.Square)\
                        .then_inc(ACL.done(f"square{j}"), 1)
                if nxt is not None:
                    xnT_evac(PEX, ACX, xnT_a, bank[0], "xnT_A", "trA", nxt)
                act.wait_ge(*PEL.after("v", p))

                def value_blocks(j):
                    for b in range(BT):
                        nc.scalar.activation(vblk[j][:, :, b, :], view(bank[7][:, j * D:(j + 1) * D], "p (a b) -> p a b", b=P),
                                             ACT.Copy, scale=K["inb"][:, b:b + 1]).then_inc(ACL.done(f"vblk{j}_{b}"), 1)

                value_blocks(0)
                if nxt is not None:
                    queries(nxt)
                else:
                    shared_silu(0)
                for j in range(2):
                    act.wait_ge(*VEL.after(f"unit{j}", p))
                    nc.scalar.activation(fqk[j], fqk[j], ACT.Exp).then_inc(ACL.done(f"sp_exp{j}"), 1)
                if nxt is not None:
                    queries_keys(nxt)
                for j in range(2):
                    act.wait_ge(*ACL.after(f"sp_exp{j}", p))
                    nc.scalar.activation(fqk[j], fqk[j], ACT.Ln, bias=K["ones"][:, 0:1]).then_inc(ACL.done(f"softplus{j}"), 1)
                value_blocks(1)
                if nxt is not None:
                    probabilities(nxt)
                act.wait_ge(*PEL.after("qt", p))
                nc.scalar.copy(view(qtT, "p a b c -> p (a b c)"), bank[4]).then_inc(ACL.done("qt_evac"), 1)
                if nxt is not None:
                    context_sums(nxt)
                if nxt is not None:
                    xnT_evac(PEB, ACB, xnT_x, bank[6], "xnT_B", "trB", nxt)
                if nxt is None:
                    shared_silu(1)
                act.wait_ge(*GPL.after("xnT_all", p - 1))
                xnT_evac(PEL, ACL, xnT, bank[4], "xnT_C", "trC", p)

            xnT_evac(PEX, ACX, xnT_a, bank[0], "xnT_A", "trA", 0)
            queries(0)
            queries_keys(0)
            probabilities(0)
            context_sums(0)
            xnT_evac(PEB, ACB, xnT_x, bank[6], "xnT_B", "trB", 0)
            with act.Fori(0, NPAIR - 1) as p:
                linear_scalar(p, p + 1)
            linear_scalar(NPAIR - 1, None)
            shared_silu(2)
            shared_silu(3)
            act.wait_ge(*RT.sem_value("top"))
            nc.scalar.activation(gate, lg_top, ACT.Exp, scale=-1.0).then_inc(SHA.done("gate_exp"), 1)
            act.wait_ge(*RT.sem_value("gate"))
            for t in range(NT):
                nc.scalar.activation(xm[:, t, :], xm[:, t, :], ACT.Copy, scale=gate[:, t:t + 1]).then_inc(SHA.done(f"xm{t}"), 1)
            for s in range(4, 8):
                shared_silu(s)
            act.sem_inc(AC2.sem, AC2.round())

            def expert_tokens(PEx, ACx, s, i, h):
                act.wait_ge(*PEx.after("xt" + s, i))
                nc.scalar.copy(view(xgT[h], "p a b -> p (a b)"), bank[6 + h][:, 0:D]).then_inc(ACx.done("xT" + s), 1)

            def expert_silu(PEx, ACx, s, i, h):
                act.wait_ge(*PEx.after("gu" + s, i))
                nc.scalar.activation(view(egate[h], "p a b -> p (a b)"), bank[2 * h], ACT.Silu).then_inc(ACx.done("silu" + s), 1)

            with act.Fori(0, NR) as it:
                expert_tokens(PE2, AC2, "0", it, 0)
                for r in range(RING):
                    if r + 1 < RING:
                        expert_tokens(PE2, AC2, str(r + 1), it, (r + 1) % 2)
                    act.wait_ge(*(VE2.after(f"h{r + 2}", it - 1) if r < 2 else VE2.after(f"h{r - 2}", it)))
                    expert_silu(PE2, AC2, str(r), it, r % 2)
            n_over = act.value_load(etab.bitcast(i32)[0:1, NOVF:NOVF + 1], min_val=0, max_val=NOVF)
            with act.If(n_over > 0):
                act.sem_inc(ACO.sem, ACO.round())
                act.wait_ge(*VE2.all(NR))
                with act.Fori(0, NOVF) as i:
                    expert_tokens(PEO, ACO, "", i, 0)
                    expert_silu(PEO, ACO, "", i, 0)
                act.wait_ge(*VEO.all(NOVF))
            act.sem_inc(AC3.sem, AC3.round())
            act.sem_inc(AT3.sem, AT3.round())

            def attn1_scalar(p, nxt):
                for n in range(2):
                    act.wait_ge(*PE3.after(f"q{n}", p))
                    nc.scalar.copy(view(q3[:, 2 * n:2 * n + 2, :], "p a b -> p (a b)"), bank[2 + n]).then_inc(AC3.done(f"q_evac{n}"), 1)
                for h in range(H1):
                    act.wait_ge(*PE3.after(f"qk{h}", p))
                    nc.scalar.mul(qp3[:, 0, :, h * S:(h + 1) * S], view(bank[4 + h % 4][:, 0:PW], "p (b s) -> p b s", s=S),
                                  HD1 ** -0.5).then_inc(AC3.done(f"qk_evac{h}"), 1)
                for s in range(NU + 2):
                    if s < NU:
                        act.wait_ge(*VE3.after(f"row_max{s}", p))
                        if s >= 4:
                            act.wait_ge(*VE3.after(f"ov_evac{s - 4}", p))
                        nc.scalar.activation(pr3[s % 4], bank[s % 2][:, 0:KEYS], ACT.Exp, bias=nmx3[:, s % 4:s % 4 + 1],
                                             accum_out=sm3[:, s % 4:s % 4 + 1]).then_inc(AC3.done(f"exp{s}"), 1)
                    if s >= 2:
                        act.wait_ge(*PE3.after(f"pt{s - 2}", p))
                        nc.scalar.copy(view(pT3[s % 2], "p a b -> p (a b)"), bank[2 + s % 2][:, 0:2 * P])\
                            .then_inc(AC3.done(f"pT_evac{s - 2}"), 1)
                for n in range(2):
                    act.wait_ge(*PE3.after(f"o{n}", p))
                    nc.scalar.copy(view(o3T[:, 2 * n:2 * n + 2, :], "p a b -> p (a b)"), bank[n]).then_inc(AC3.done(f"o_evac{n}"), 1)
                if nxt is not None:
                    xnT_evac(PT3, AT3, xnT3, bank[0], "xnT", "tr", nxt)

            xnT_evac(PT3, AT3, xnT3, bank[0], "xnT", "tr", 0)
            with act.Fori(0, NPAIR - 1) as p:
                attn1_scalar(p, p + 1)
            attn1_scalar(NPAIR - 1, None)
            act.wait_ge(weights4_in, 16 * 10)
            nc.scalar.activation(m_A, m_A, ACT.Exp).then_inc(set4a.done("expA"), 1)
            act.sem_inc(AC4.sem, AC4.round())
            with act.Fori(0, NPAIR) as p:
                act.wait_ge(*PE4.after("tr", p))
                nc.scalar.copy(view(uT4, "p a b -> p (a b)"), bank[0]).then_inc(AC4.done("uT"), 1)
                act.wait_ge(*VE4.after("dt_abs", p))
                nc.scalar.activation(dts["e"], dts["a"], ACT.Exp, scale=-1.0).then_inc(AC4.done("dt_exp"), 1)
                for n in (2, 0, 1):
                    act.wait_ge(*PE4.after(f"xbc{n}", p))
                    nc.scalar.copy(xp[:, 2 * n:2 * n + 2, :, TAPS - 1:TAPS - 1 + S],
                                   view(bank[1 + n], "p (c b s) -> p c b s", c=2, s=S)).then_inc(AC4.done(f"xp{n}"), 1)
                    for c in range(2):
                        nc.scalar.activation(cv[:, 2 * n + c, :], bank[1 + n][:, c * PW:(c + 1) * PW], ACT.Identity,
                                             bias=m_cb[:, 2 * n + c:2 * n + c + 1], scale=m_conv[:, 2 * n + c, TAPS - 1:TAPS])\
                            .then_inc(AC4.done(f"tap3_{2 * n + c}"), 1)
                def tanh(n):
                    act.wait_ge(*VE4.after(f"tap2_{2 * n + 1}", p))
                    nc.scalar.activation(th[:, 2 * n:2 * n + 2, :], cv[:, 2 * n:2 * n + 2, :], ACT.Tanh, scale=0.5)\
                        .then_inc(AC4.done(f"tanh{n}"), 1)

                tanh(2)
                for j in range(2):
                    if j == 1:
                        for i in range(2):
                            act.wait_ge(*PE4.after(f"z{i}", p))
                            nc.scalar.activation(zt[i], bank[4 + i], ACT.Tanh, scale=0.5).then_inc(AC4.done(f"z_tanh{i}"), 1)
                        tanh(0)
                        tanh(1)
                    act.wait_ge(*VE4.after("cum", p))
                    act.wait_ge(*PE4.after(f"cumT{j}", p))
                    for h in range(HM):
                        nc.scalar.activation(dec[j][:, h, :], bank[(3, 0)[h // 4]][:, (h % 4) * P:(h % 4 + 1) * P], ACT.Relu,
                                             scale=-1.0, bias=dts["cum"][:, j, h:h + 1]).then_inc(AC4.done(f"relu{j}_{h}"), 1)
                    if j == 1:
                        for i in range(2):
                            act.wait_ge(*PE4.after(f"xs{i}", p))
                            nc.scalar.copy(xs4[i], bank[1 + i]).then_inc(AC4.done(f"xs_evac{i}"), 1)
                    act.wait_ge(*AC4.after(f"relu{j}_7", p))
                    nc.scalar.activation(dec[j], dec[j], ACT.Exp, scale=-1.0).then_inc(AC4.done(f"decay{j}"), 1)
                for j in range(2):
                    act.wait_ge(*VE4.after(f"yz{j}", p))
                    nc.scalar.activation(zt[j], y4[j], ACT.Square, accum_out=ssq[:, j:j + 1]).then_inc(AC4.done(f"square{j}"), 1)
                    act.wait_ge(*PE4.after(f"yT{j}", p))
                    nc.scalar.copy(view(yT4[j], "p a b -> p (a b)"), bank[1 + j]).then_inc(AC4.done(f"yT_evac{j}"), 1)
            act.sem_inc(AC5.sem, AC5.round())
            act.sem_inc(AT5.sem, AT5.round())

            def ffn_scalar(p, nxt):
                for n in range(3):
                    act.wait_ge(*PE5.after(f"g{n}", p))
                    nc.scalar.activation(sg5[:, 2 * n:2 * n + 2, :], view(bank[n], "p (c t) -> p c t", c=2), ACT.Silu, scale=1.0 / 127.0)\
                        .then_inc(AC5.done(f"silu{n}"), 1)
                if nxt is not None:
                    xnT_evac(PT5, AT5, xnT5, bank[6], "xnT", "tr", nxt)

            xnT_evac(PT5, AT5, xnT5, bank[6], "xnT", "tr", 0)
            with act.Fori(0, NPAIR - 1) as p:
                ffn_scalar(p, p + 1)
            ffn_scalar(NPAIR - 1, None)

        @block.vector
        def _(dve):
            nc.vector.memset(view(cT2[0], "p a b -> p (a b)")[DC2:DC2 + 1, :], 1.0).then_inc(setup.done("ones0"), 1)
            nc.vector.memset(view(cT2[1], "p a b -> p (a b)")[DC2:DC2 + 1, :], 1.0).then_inc(setup.done("ones1"), 1)
            for j in range(2):
                nc.vector.memset(cN[j][:, :, :, DC:DC + 1], 1.0).then_inc(setup.done(f"ones_n{j}"), 1)
                nc.vector.memset(cLq[j][:, DC:DC + 1], 1.0).then_inc(setup.done(f"ones_l{j}"), 1)
            nc.vector.memset(zrow, 0.0).then_inc(setup.done("zero"), 1)
            dve.sem_inc(VEX.sem, VEX.round())
            dve.sem_inc(VEL.sem, VEL.round())
            dve.sem_inc(VEB.sem, VEB.round())
            dve.wait_ge(x0_in, 16)
            dve.wait_ge(*setup.sem_value("ones_l1"))

            def tiles_of(p):
                return lambda j: x[:, p * 2 + j, :]

            def stats_attn(p):
                norm_stats(dve, VEX, "lnA", p, tiles_of(p), 1e-5, LNX)

            def apply_attn(p):
                wait_alone(dve, *PEB.after("trB", p - 1))
                norm_apply(dve, VEX, GPX, "lnA", p, tiles_of(p), lambda j: xnx[j], LNX)

            def row_maxima(p):
                for j in range(2):
                    dve.wait_ge(*PEX.after(f"sc_{j}", p))
                    nc.vector.reduce_max(nmx[:, j:j + 1], bank[SC[j]][:, 0:KEYS], AX, negate=True)\
                        .then_inc(VEX.done(f"row_max{j}"), 1)

            def probabilities_T(p):
                dve.wait_ge(*PEX.after("pt", p))
                nc.vector.tensor_copy(view(pT, "p a b c -> p (a b c)"), bank[1]).then_inc(VEX.done("pT_evac"), 1)
                dve.wait_ge(*ACX.after("exp1", p))
                nc.vector.reciprocal(ri, sm).then_inc(VEX.done("rsum"), 1)

            def last_key(p):
                for j in range(2):
                    dve.wait_ge(*PEX.after(f"ov_{j}", p))
                    dve.wait_ge(ctx_in[j], (p + 1) * CTX1)
                    nc.vector.scalar_tensor_tensor(op[j], cLq[j], pr[j][:, KEYS - 1:KEYS], bank[OV[j]][:, 0:DC + 1],
                                                   ALU.mult, ALU.add).then_inc(VEX.done(f"ov_evac{j}"), 1)

            def add_attn(p):
                for j in range(2):
                    dve.wait_ge(*PEX.after(f"wv_{j}", p))
                    nc.vector.scalar_tensor_tensor(x[:, p * 2 + j, :], bank[WV[j]][:, 0:D], ri[:, j:j + 1], x[:, p * 2 + j, :],
                                                   ALU.mult, ALU.add).then_inc(VEX.done(f"x_attn{j}"), 1)

            def stats_linear(p):
                wait_alone(dve, *VEX.after("x_attn1", p))
                norm_stats(dve, VEB, "lnB", p, tiles_of(p), 1e-5, LNB)

            def apply_linear(p):
                wait_alone(dve, *PEX.after("trA", p))
                norm_apply(dve, VEB, GPB, "lnB", p, tiles_of(p), lambda j: xnx[j], LNB)

            def shared_hidden(s):
                n, c = s // 4, s % 4
                dve.wait_ge(*SHA.sem_value(f"silu{s}"))
                nc.vector.tensor_tensor(hs[:, c, n * 512:(n + 1) * 512], sgate[s % 2], bank[2 * (s % 2) + 1], ALU.mult)\
                    .then_inc(SHV.done(f"h{s}"), 1)

            def linear_vector(p, nxt):
                xt = tiles_of(p)
                if nxt is not None:
                    stats_attn(nxt)
                    apply_attn(nxt)
                for j in range(2):
                    dve.wait_ge(*ACL.after(f"square{j}", p))
                    nc.vector.reduce_sum(ss[:, j, :], view(fqk[j], "p (a b) -> p a b", b=16), AX).then_inc(VEL.done(f"ss{j}"), 1)
                dve.wait_ge(*VEL.after("ss1", p))
                nc.vector.tensor_scalar_max(ss, ss, 1e-24).then_inc(VEL.done("ss_max"), 1)
                dve.wait_ge(*VEL.after("ss_max", p))
                nc.vector.tensor_scalar(rt.bitcast(i32), ss.bitcast(i32), 1, None, ALU.logical_shift_right)\
                    .then_inc(VEL.done("rn_half"), 1)
                dve.wait_ge(*VEL.after("rn_half", p))
                nc.vector.tensor_scalar(rn.bitcast(i32), rt.bitcast(i32), -1.0, float(0x5f3759df), ALU.mult, ALU.add)\
                    .then_inc(VEL.done("rn_y0"), 1)
                for n in range(3):
                    dve.wait_ge(*VEL.after(f"rn_y{n}", p))
                    nc.vector.scalar_tensor_tensor(rt, rn, -0.5, rn, ALU.mult, ALU.mult).then_inc(VEL.done(f"rn_yy{n}"), 1)
                    dve.wait_ge(*VEL.after(f"rn_yy{n}", p))
                    nc.vector.tensor_tensor(rt, rt, ss, ALU.mult).then_inc(VEL.done(f"rn_syy{n}"), 1)
                    dve.wait_ge(*VEL.after(f"rn_syy{n}", p))
                    nc.vector.scalar_tensor_tensor(rn, rt, 1.5, rn, ALU.add, ALU.mult).then_inc(VEL.done(f"rn_y{n + 1}"), 1)
                dve.wait_ge(*VEL.after("rn_y3", p))
                for j in range(2):
                    nc.vector.tensor_tensor(view(fqk[j], "p (a b) -> p a b", b=16), view(bank[5 + j], "p (a b) -> p a b", b=16),
                                            rn[:, j, :].unsqueeze(2).broadcast_to((P, 32, 16)), ALU.mult)\
                        .then_inc(VEL.done(f"unit{j}"), 1)
                if nxt is None:
                    shared_hidden(0)
                else:
                    row_maxima(nxt)
                for j in range(2):
                    if j == 1:
                        dve.wait_ge(*PEL.after("ks", p))
                        nc.vector.scalar_tensor_tensor(dtmp, view(bank[7], "p (a b) -> p a b", b=D), 1e-6, fqk2[:, :, 0:D], ALU.add,
                                                       ALU.mult).then_inc(VEL.done("den_mul"), 1)
                        dve.wait_ge(*VEL.after("den_mul", p))
                        nc.vector.reduce_sum(den, view(dtmp, "p a b -> p (a b)").rearrange("p (a b) -> p a b", b=16), AX)\
                            .then_inc(VEL.done("den"), 1)
                        dve.wait_ge(*VEL.after("den", p))
                        nc.vector.reciprocal(den, den).then_inc(VEL.done("rden"), 1)
                        if nxt is not None:
                            probabilities_T(nxt)
                    for hf in range(2):
                        dve.wait_ge(*PEL.after(f"kv_{j}_{hf}", p))
                        nc.vector.tensor_tensor(kvm[j][:, hf, :, :], view(bank[KV[j][hf]], "p (a b) -> p a b", b=P),
                                                K["hmask"].unsqueeze(1).broadcast_to((P, BT, P)), ALU.mult)\
                            .then_inc(VEL.done(f"kv_evac{j}_{hf}"), 1)
                    if nxt is not None and j == 1:
                        last_key(nxt)
                if nxt is None:
                    shared_hidden(1)
                dve.wait_ge(*VEL.after("rden", p))
                dve.wait_ge(*PEL.after("at", p))
                heads = (P, 32, 16)
                nc.vector.tensor_tensor(view(dtmp, "p a b -> p (a b)").rearrange("p (a b) -> p a b", b=16),
                                        view(bank[6], "p (a b) -> p a b", b=16), den.unsqueeze(2).broadcast_to(heads),
                                        ALU.mult).then_inc(VEL.done("at_norm"), 1)
                dve.wait_ge(*VEL.after("at_norm", p))
                xpair = x[:, bass.ds(p * 2, 2), :]
                nc.vector.tensor_tensor(xpair, xpair, dtmp, ALU.add).then_inc(VEL.done("x_lin"), 1)
                if nxt is not None:
                    add_attn(nxt)
                    stats_linear(nxt)
                wait_alone(dve, *VEL.after("x_lin", p))
                norm_stats(dve, VEL, "lnC", p, xt, 1e-5)
                if nxt is not None:
                    apply_linear(nxt)
                wait_alone(dve, *PEL.after("trC", p - 1))
                norm_apply(dve, VEL, GPL, "lnC", p, xt, lambda j: xn[j])
                for j in range(2):
                    dve.wait_ge(*VEL.after(f"lnC_norm{j}", p))
                    nc.vector.tensor_scalar_mul(xm[:, p * 2 + j, :], xn[j], 1.0).then_inc(VEL.done(f"xm{j}"), 1)

            stats_attn(0)
            apply_attn(0)
            row_maxima(0)
            probabilities_T(0)
            last_key(0)
            add_attn(0)
            stats_linear(0)
            apply_linear(0)
            dve.wait_ge(weights1_in, 16 * 5)
            nc.vector.tensor_scalar(negmask[0:B, :], mask8[0:B, 0:65].bitcast(u8)[:, 0:KEYS], 1.0, -MASKED, ALU.subtract,
                                    ALU.mult).then_inc(setup.done("negmask"), 1)
            dve.wait_ge(x_in, 16)
            dve.wait_ge(const_in, 16)
            with dve.Fori(0, NPAIR - 1) as p:
                linear_vector(p, p + 1)
            linear_vector(NPAIR - 1, None)
            shared_hidden(2)
            all_t = (P, NT, E)
            dve.wait_ge(*SHP.sem_value("lg"))
            nc.vector.tensor_copy(view(lg, "p a b -> p (a b)"), bank[5][:, 0:NT * E]).then_inc(RT.done("logits"), 1)
            dve.wait_ge(*RT.sem_value("logits"))
            nc.vector.reduce_max(lg_top, lg, AX).then_inc(RT.done("top"), 1)
            dve.wait_ge(*RT.sem_value("top"))
            nc.vector.tensor_tensor(lg, lg, lg_top.unsqueeze(2).broadcast_to(all_t), ALU.is_ge).then_inc(RT.done("tops"), 1)
            dve.wait_ge(*RT.sem_value("tops"))
            nc.vector.tensor_tensor(lg, lg, K["down"].unsqueeze(1).broadcast_to(all_t), ALU.mult).then_inc(RT.done("tops_down"), 1)
            dve.wait_ge(*RT.sem_value("tops_down"))
            nc.vector.reduce_max(eidx, lg, AX).then_inc(RT.done("down"), 1)
            dve.wait_ge(*RT.sem_value("down"))
            nc.vector.tensor_scalar(eidx, eidx, -1.0, float(E), ALU.mult, ALU.add).then_inc(RT.done("expert"), 1)
            dve.wait_ge(*RT.sem_value("expert"))
            nc.vector.tensor_tensor(oneh, K["iota"].unsqueeze(1).broadcast_to(all_t), eidx.unsqueeze(2).broadcast_to(all_t),
                                    ALU.is_equal).then_inc(RT.done("onehot"), 1)
            shared_hidden(3)
            dve.wait_ge(*SHA.sem_value("gate_exp"))
            nc.vector.tensor_scalar_add(gate, gate, 1.0).then_inc(RT.done("gate_1p"), 1)
            dve.wait_ge(*RT.sem_value("gate_1p"))
            nc.vector.reciprocal(gate, gate).then_inc(RT.done("gate"), 1)
            def flat3(a):
                return view(a, "p a b -> p (a b)")

            dve.wait_ge(*SHP.sem_value("rank"))
            nc.vector.tensor_tensor(flat3(r_oh), bank[6][:, 0:NT * E], flat3(oneh), ALU.mult).then_inc(RT.done("rank_oh"), 1)
            dve.wait_ge(*SHP.sem_value("count"))
            nc.vector.tensor_tensor(cnt7, bank[7][:, 0:E].unsqueeze(2).broadcast_to((P, E, NT - 1)),
                                    K["caps"].unsqueeze(1).broadcast_to((P, E, NT - 1)), ALU.is_gt).then_inc(RT.done("over7"), 1)
            dve.wait_ge(*RT.sem_value("rank_oh"))
            nc.vector.reduce_sum(rank, r_oh, AX).then_inc(RT.done("rank"), 1)
            dve.wait_ge(*RT.sem_value("over7"))
            nc.vector.reduce_sum(novf, cnt7, AX).then_inc(RT.done("novf"), 1)
            dve.wait_ge(*RT.sem_value("rank"))
            nc.vector.tensor_tensor(r_q7, rank.unsqueeze(2).broadcast_to((P, NT, NT - 1)),
                                    K["caps"].unsqueeze(1).broadcast_to((P, NT, NT - 1)), ALU.is_ge).then_inc(RT.done("q7"), 1)
            dve.wait_ge(*RT.sem_value("novf"))
            nc.vector.tensor_tensor_scan(oend, K["ones"][:, 0:E], novf, 0.0, ALU.mult, ALU.add).then_inc(RT.done("oend"), 1)
            dve.wait_ge(*RT.sem_value("q7"))
            nc.vector.reduce_sum(rq, r_q7, AX).then_inc(RT.done("q"), 1)
            dve.wait_ge(*RT.sem_value("oend"))
            nc.vector.tensor_tensor(obase, oend, novf, ALU.subtract).then_inc(RT.done("obase"), 1)
            nc.vector.tensor_tensor(r_e7, oend.unsqueeze(1).broadcast_to((P, NOVF, E)),
                                    K["nth"].unsqueeze(2).broadcast_to((P, NOVF, E)), ALU.is_le).then_inc(RT.done("e7"), 1)
            dve.wait_ge(*RT.sem_value("obase"))
            nc.vector.tensor_tensor(r_oh, oneh, obase.unsqueeze(1).broadcast_to((P, NT, E)), ALU.mult).then_inc(RT.done("base_oh"), 1)
            dve.wait_ge(*RT.sem_value("e7"))
            nc.vector.reduce_sum(etab_f[:, 0:NOVF], r_e7, AX).then_inc(RT.done("etab_sum"), 1)
            dve.wait_ge(*RT.sem_value("base_oh"))
            nc.vector.reduce_sum(r_bt, r_oh, AX).then_inc(RT.done("base"), 1)
            dve.wait_ge(*RT.sem_value("etab_sum"))
            nc.vector.tensor_scalar_min(etab_f[:, 0:NOVF], etab_f[:, 0:NOVF], E - 1.0).then_inc(RT.done("etab_min"), 1)
            nc.vector.tensor_copy(etab_f[:, NOVF:NOVF + 1], oend[:, E - 1:E]).then_inc(RT.done("etab_n"), 1)
            dve.wait_ge(*RT.sem_value("base"))
            nc.vector.tensor_tensor(r_t, r_bt, rq, ALU.add).then_inc(RT.done("t1"), 1)
            dve.wait_ge(*RT.sem_value("etab_n"))
            nc.vector.tensor_copy(etab.bitcast(i32), etab_f).then_inc(RT.done("etab"), 1)
            nc.vector.tensor_scalar_min(r_g, rq, 1.0).then_inc(RT.done("past"), 1)
            dve.wait_ge(*RT.sem_value("t1"))
            nc.vector.scalar_tensor_tensor(r_t, r_t, E - 1.0, eidx, ALU.add, ALU.subtract).then_inc(RT.done("t2"), 1)
            dve.wait_ge(*RT.sem_value("t2"))
            nc.vector.tensor_tensor(r_t, r_t, r_g, ALU.mult).then_inc(RT.done("t3"), 1)
            dve.wait_ge(*RT.sem_value("t3"))
            nc.vector.tensor_tensor(r_t, r_t, eidx, ALU.add).then_inc(RT.done("tile"), 1)
            dve.wait_ge(*RT.sem_value("tile"))
            nc.vector.scalar_tensor_tensor(slot_f, r_t, float(P), rank, ALU.mult, ALU.add).then_inc(RT.done("slot1"), 1)
            dve.wait_ge(*RT.sem_value("slot1"))
            nc.vector.scalar_tensor_tensor(slot_f, rq, -float(P), slot_f, ALU.mult, ALU.add).then_inc(RT.done("slot2"), 1)
            dve.wait_ge(*RT.sem_value("slot2"))
            nc.vector.tensor_copy(slot_i.bitcast(i32), slot_f).then_inc(RT.done("slot"), 1)
            for s in range(4, 8):
                shared_hidden(s)

            def add_shared(t):
                dve.wait_ge(*SHP.sem_value(f"down{t}"))
                nc.vector.tensor_tensor(x[:, t, :], x[:, t, :], bank[4 + t % 2][:, 0:D], ALU.add).then_inc(SHV.done(f"x{t}"), 1)

            for t in range(2):
                add_shared(t)
            dve.wait_ge(*SHV.sem_value("h7"))
            nc.vector.memset(qp3[DC2:DC2 + 2, 1, :, :], 1.0).then_inc(set3.done("rows_one"), 1)
            dve.wait_ge(*set3.sem_value("rows_one"))
            nc.vector.memset(qp3[DC2:DC2 + 1, 1, :, :], 0.0).then_inc(set3.done("row_zero"), 1)
            dve.sem_inc(VE2.sem, VE2.round())

            def expert_hidden(ACx, VEx, s, i, h):
                dve.wait_ge(*ACx.after("silu" + s, i))
                nc.vector.tensor_tensor(flat3(eh[h]), flat3(egate[h]), bank[2 * h + 1], ALU.mult).then_inc(VEx.done("h" + s), 1)

            def expert_output(PEx, VEx, s, i, h, y):
                dve.wait_ge(*PEx.after("dn" + s, i))
                nc.vector.tensor_copy(y, bank[4 + h][:, 0:D]).then_inc(VEx.done("y" + s), 1)

            with dve.Fori(0, NR) as it:
                expert_hidden(AC2, VE2, "0", it, 0)
                for r in range(RING):
                    if r + 1 < RING:
                        expert_hidden(AC2, VE2, str(r + 1), it, (r + 1) % 2)
                    if r == 0:
                        dve.wait_ge(y_out, it * (16 * RING))
                    expert_output(PE2, VE2, str(r), it, r % 2, ey[r])
            n_over = dve.value_load(etab.bitcast(i32)[0:1, NOVF:NOVF + 1], min_val=0, max_val=NOVF)
            with dve.If(n_over > 0):
                dve.sem_inc(VEO.sem, VEO.round())
                dve.wait_ge(y_out, 16 * E)
                with dve.Fori(0, NOVF) as i:
                    dve.wait_ge(ovf_out, i * 16)
                    expert_hidden(ACO, VEO, "", i, 0)
                    expert_output(PEO, VEO, "", i, 0, ey[0])
            for t in range(2, NT):
                add_shared(t)
            dve.wait_ge(y_out, 16 * E)
            for j in range(2):
                nc.vector.memset(op3[j], 0.0).then_inc(set3.done(f"op_zero{j}"), 1)

            def add_experts(tiles):
                for t in tiles:
                    dve.wait_ge(*SHV.sem_value(f"x{t}"))
                    nc.vector.tensor_tensor(x[:, t, :], x[:, t, :], yg[:, t, :], ALU.add).then_inc(XE.done(f"x{t}"), 1)

            dve.wait_ge(gathered0, 16 * 2)
            add_experts(range(2))
            wait_alone(dve, *XE.sem_value("x1"))
            dve.wait_ge(*set3.sem_value("row_zero"))
            dve.wait_ge(weights3_in, 16 * 7)
            dve.sem_inc(VE3.sem, VE3.round())
            dve.sem_inc(VN3.sem, VN3.round())

            def stats_attn1(p):
                norm_stats(dve, VN3, "ln", p, tiles_of(p), 1e-5)

            def apply_attn1(p):
                dve.wait_ge(*PT3.after("tr", p - 1))
                norm_apply(dve, VN3, GN3, "ln", p, tiles_of(p), lambda j: xn3[j])

            dve.sem_inc(VE4.sem, VE4.round())
            dve.sem_inc(VN4.sem, VN4.round())

            def norm1_stats(p):
                norm_stats(dve, VN4, "ln1", p, tiles_of(p), 1e-5)

            def norm1_apply(p):
                norm_apply(dve, VN4, GN4, "ln1", p, tiles_of(p), lambda j: xn4[:, j, :])
                wait_alone(dve, *VN4.after("ln1_norm1", p))
                norm_stats(dve, VN4, "ln2", p, lambda j: xn4[:, j, :], 1e-5)

            def norm2_apply(p):
                dve.wait_ge(*PE4.after("tr", p - 1))
                norm_apply(dve, VN4, GN4, "ln2", p, lambda j: xn4[:, j, :], lambda j: u4[:, j, :])
                dve.wait_ge(*VN4.after("ln2_norm1", p))
                nc.vector.tensor_tensor(u4, u4, m_lnw.unsqueeze(1).broadcast_to((P, 2, D)), ALU.mult).then_inc(VN4.done("ln_w"), 1)
                dve.wait_ge(*VN4.after("ln_w", p))
                nc.vector.tensor_tensor(u4, u4, m_lnb.unsqueeze(1).broadcast_to((P, 2, D)), ALU.add).then_inc(VN4.done("u"), 1)

            def attn1_vector(p, nxt):
                for h in range(H1):
                    dve.wait_ge(*AC3.after(f"qk_evac{h}", p))
                    nc.vector.tensor_scalar_mul(qp3[0:DC2, 1, :, h * S:(h + 1) * S],
                                                view(bank[4 + h % 4][0:DC2, PW:2 * PW], "p (b s) -> p b s", s=S),
                                                HD1 ** -0.5).then_inc(VE3.done(f"qk_evac{h}"), 1)
                for s in range(NU + 4):
                    if nxt is not None:
                        if s == NU // 2:
                            stats_attn1(nxt)
                        if s == NU // 2 + 2:
                            apply_attn1(nxt)
                    else:
                        if s == NU // 2:
                            norm1_stats(0)
                        if s == NU // 2 + 2:
                            norm1_apply(0)
                        if s == NU // 2 + 5:
                            dve.wait_ge(weights4_in, 16 * 10)
                            norm2_apply(0)
                    if s < NU:
                        dve.wait_ge(*PE3.after(f"sc{s}", p))
                        nc.vector.reduce_max(nmx3[:, s % 4:s % 4 + 1], bank[s % 2][:, 0:KEYS], AX, negate=True)\
                            .then_inc(VE3.done(f"row_max{s}"), 1)
                    if 1 <= s <= NU:
                        u = s - 1
                        dve.wait_ge(*AC3.after(f"exp{u}", p))
                        nc.vector.reciprocal(rs3[:, u % 4:u % 4 + 1], sm3[:, u % 4:u % 4 + 1]).then_inc(VE3.done(f"rsum{u}"), 1)
                        dve.wait_ge(*VE3.after(f"rsum{u}", p))
                        nc.vector.tensor_scalar_mul(pr3[u % 4], pr3[u % 4], rs3[:, u % 4:u % 4 + 1]).then_inc(VE3.done(f"norm{u}"), 1)
                    if 3 <= s < NU + 3:
                        u = s - 3
                        b = u // 2
                        if u == 0 or u == NU // 2:
                            dve.wait_ge(ctx_in[b // BT], (p + 1) * CTX3 + NPAIR * CTX1)
                        dve.wait_ge(*PE3.after(f"ov{u}", p))
                        nc.vector.scalar_tensor_tensor(op3[u % 2][:, 0:DC], cLb[b // BT][:, b % BT, :], pr3[u % 4][:, KEYS - 1:KEYS],
                                                       bank[4 + u % 2][:, 0:DC], ALU.mult, ALU.add).then_inc(VE3.done(f"ov_evac{u}"), 1)
                    if s >= 4:
                        u = s - 4
                        b, g = u // 2, u % 2
                        dve.wait_ge(*PE3.after(f"opT{u}", p))
                        if u == 0:
                            dve.wait_ge(*PE3.after("o1", p - 1))
                        nc.vector.tensor_copy(oT3[:, b // BT, :, 4 * g:4 * g + 4, b % BT * S:(b % BT + 1) * S],
                                              view(bank[6 + u % 2][:, 0:2 * P], "p (c h s) -> p c h s", c=2, s=S))\
                            .then_inc(VE3.done(f"opT_evac{u}"), 1)
                for j in range(2):
                    dve.wait_ge(*PE3.after(f"wo{j}", p))
                    nc.vector.tensor_tensor(t3[j], bank[4 + j][:, 0:D], c_bo, ALU.add).then_inc(VE3.done(f"bias{j}"), 1)
                for j in range(2):
                    dve.wait_ge(*VE3.after(f"bias{j}", p))
                    nc.vector.tensor_tensor(x[:, p * 2 + j, :], x[:, p * 2 + j, :], t3[j], ALU.add).then_inc(VE3.done(f"x{j}"), 1)
                dve.wait_ge(*VE3.after("x1", p))

            stats_attn1(0)
            apply_attn1(0)
            dve.wait_ge(gathered, 16 * (NT - 2))
            add_experts(range(2, NT))
            dve.wait_ge(*XE.sem_value("x7"))
            with dve.Fori(0, NPAIR - 1) as p:
                attn1_vector(p, p + 1)
            attn1_vector(NPAIR - 1, None)
            dve.wait_ge(weights4_in, 16 * 10)
            nc.vector.memset(xp[:, :, :, 0:TAPS - 1], 0.0).then_inc(set4.done("pad"), 1)
            for c in range(4):
                nc.vector.tensor_scalar_mul(m_out[:, c, :], m_out[:, c, :], m_nw[:, c:c + 1]).then_inc(set4.done(f"nw{c}"), 1)
            nc.vector.tensor_scalar_mul(m_D, m_D, 0.25).then_inc(set4.done("D"), 1)
            dve.wait_ge(*set4a.sem_value("expA"))
            nc.vector.tensor_scalar_mul(m_A, m_A, -1.0).then_inc(set4.done("A"), 1)
            dve.wait_ge(*set4.sem_value("A"))
            dve.sem_inc(VE5.sem, VE5.round())
            dve.sem_inc(VN5.sem, VN5.round())

            def norm_ffn(p):
                wait_alone(dve, *PT5.after("tr", p - 1))
                layer_norm_vector(dve, VN5, GN5, "ln", p, tiles_of(p), lambda j: xn5[j], 1e-5)

            def scan_vector(p, nxt):
                dve.wait_ge(*PE4.after("dt", p))
                nc.vector.tensor_tensor(dts["d"], view(bank[6][:, 0:2 * HM], "p (a b) -> p a b", b=HM),
                                        m_dtb.unsqueeze(1).broadcast_to((P, 2, HM)), ALU.add).then_inc(VE4.done("dt_raw"), 1)
                dve.wait_ge(*VE4.after("dt_raw", p))
                nc.vector.scalar_tensor_tensor(dts["a"], dts["d"], -1.0, dts["d"], ALU.mult, ALU.max).then_inc(VE4.done("dt_abs"), 1)
                nc.vector.tensor_scalar_max(dts["m"], dts["d"], 0.0).then_inc(VE4.done("dt_pos"), 1)
                def taps(n):
                    for k in range(TAPS - 1):
                        for c in (2 * n, 2 * n + 1):
                            if k:
                                dve.wait_ge(*VE4.after(f"tap{k - 1}_{c}", p))
                            else:
                                dve.wait_ge(*AC4.after(f"tap3_{2 * n + 1}", p))
                            nc.vector.scalar_tensor_tensor(view(cv[:, c, :], "p (b s) -> p b s", s=S), xp[:, c, :, k:k + S],
                                                           m_conv[:, c, k:k + 1], view(cv[:, c, :], "p (b s) -> p b s", s=S),
                                                           ALU.mult, ALU.add).then_inc(VE4.done(f"tap{k}_{c}"), 1)

                def silu(n):
                    dve.wait_ge(*AC4.after(f"tanh{n}", p))
                    nc.vector.scalar_tensor_tensor(cv[:, 2 * n:2 * n + 2, :], th[:, 2 * n:2 * n + 2, :], 1.0, cv[:, 2 * n:2 * n + 2, :],
                                                   ALU.add, ALU.mult).then_inc(VE4.done(f"silu{n}"), 1)

                dve.wait_ge(*AC4.after("dt_exp", p))
                nc.vector.tensor_scalar_add(dts["e2"], dts["e"], 2.0).then_inc(VE4.done("dt_2e"), 1)
                dve.wait_ge(*VE4.after("dt_2e", p))
                nc.vector.reciprocal(dts["r"], dts["e2"]).then_inc(VE4.done("dt_r"), 1)
                dve.wait_ge(*VE4.after("dt_r", p))
                nc.vector.tensor_tensor(dts["s"], dts["e"], dts["r"], ALU.mult).then_inc(VE4.done("dt_s"), 1)
                dve.wait_ge(*VE4.after("dt_s", p))
                nc.vector.tensor_tensor(dts["s2"], dts["s"], dts["s"], ALU.mult).then_inc(VE4.done("dt_s2"), 1)
                dve.wait_ge(*VE4.after("dt_s2", p))
                nc.vector.tensor_scalar_mul(dts["p"], dts["s2"], 1.0 / 15.0).then_inc(VE4.done("dt_p15"), 1)
                for i in (13, 11, 9, 7, 5, 3):
                    dve.wait_ge(*VE4.after(f"dt_p{i + 2}", p))
                    nc.vector.scalar_tensor_tensor(dts["p"], dts["p"], 1.0 / i, dts["s2"], ALU.add, ALU.mult)\
                        .then_inc(VE4.done(f"dt_p{i}"), 1)
                dve.wait_ge(*VE4.after("dt_p3", p))
                nc.vector.scalar_tensor_tensor(dts["p"], dts["p"], 1.0, dts["s"], ALU.add, ALU.mult)\
                    .then_inc(VE4.done("dt_p1"), 1)
                dve.wait_ge(*VE4.after("dt_p1", p))
                nc.vector.scalar_tensor_tensor(dts["dt"], dts["p"], 2.0, dts["m"], ALU.mult, ALU.add)\
                    .then_inc(VE4.done("dt"), 1)
                dve.wait_ge(*VE4.after("dt", p))
                nc.vector.tensor_tensor(dts["dtA"], dts["dt"], m_A.unsqueeze(1).broadcast_to((P, 2, HM)), ALU.mult)\
                    .then_inc(VE4.done("dtA"), 1)
                taps(2)
                dve.wait_ge(*PE4.after("cum", p))
                nc.vector.tensor_copy(dts["cum"], view(bank[6][:, 2 * HM:4 * HM], "p (a b) -> p a b", b=HM)).then_inc(VE4.done("cum"), 1)
                taps(0)
                silu(2)
                taps(1)
                for j in range(2):
                    dve.wait_ge(*PE4.after("G1", p))
                    nc.vector.tensor_tensor(gm4[j], bank[7][:, j * P:(j + 1) * P], K["gmask"], ALU.mult).then_inc(VE4.done(f"gm{j}"), 1)

                def z_silu(j):
                    dve.wait_ge(*AC4.after(f"z_tanh{j}", p))
                    nc.vector.scalar_tensor_tensor(zs[j], zt[j], 1.0, bank[4 + j], ALU.add, ALU.mult).then_inc(VE4.done(f"z_silu{j}"), 1)

                def decayed_scores(j):
                    dve.wait_ge(*AC4.after(f"decay{j}", p))
                    dve.wait_ge(*VE4.after(f"gm{j}", p))
                    nc.vector.tensor_tensor(dec[j], dec[j], gm4[j].unsqueeze(1).broadcast_to((P, HM, P)), ALU.mult)\
                        .then_inc(VE4.done(f"M{j}"), 1)

                def gated_output(j):
                    dve.wait_ge(*PE4.after(f"y{j}", p))
                    dve.wait_ge(*GP4.after(f"xD{j}", p))
                    nc.vector.tensor_tensor(y4[j], bank[4 + j], xD[j], ALU.add).then_inc(VE4.done(f"ya{j}"), 1)
                    dve.wait_ge(*VE4.after(f"ya{j}", p))
                    nc.vector.tensor_tensor(y4[j], y4[j], zs[j], ALU.mult).then_inc(VE4.done(f"yz{j}"), 1)

                silu(0)
                silu(1)
                decayed_scores(0)
                z_silu(0)
                z_silu(1)
                for j in range(2):
                    dve.wait_ge(*AC4.after(f"xs_evac{j}", p))
                    nc.vector.tensor_tensor(view(xdt[j], "p (h e) -> p h e", h=HM), view(xs4[j], "p (h e) -> p h e", h=HM),
                                            dts["dt"][:, j, :].unsqueeze(2).broadcast_to((P, HM, HDM)), ALU.mult)\
                        .then_inc(VE4.done(f"xdt{j}"), 1)
                for j in range(2):
                    nc.vector.tensor_tensor(x[:, p * 2 + j, :], x[:, p * 2 + j, :], xn4[:, j, :], ALU.add).then_inc(VE4.done(f"xr{j}"), 1)
                decayed_scores(1)
                if nxt is not None:
                    norm1_stats(nxt)
                gated_output(0)
                if nxt is not None:
                    norm1_apply(nxt)
                else:
                    norm_ffn(0)
                gated_output(1)
                dve.wait_ge(*AC4.after("square1", p))
                nc.vector.tensor_scalar(ssq, ssq, 1.0 / DIN, 1e-5, ALU.mult, ALU.add).then_inc(VE4.done("mean_square"), 1)
                if nxt is not None:
                    norm2_apply(nxt)
                dve.wait_ge(*GP4.after("rms", p))
                for j in range(2):
                    dve.wait_ge(*PE4.after(f"out{j}", p))
                    nc.vector.scalar_tensor_tensor(x[:, p * 2 + j, :], bank[6 + j][:, 0:D], rms[:, j:j + 1], x[:, p * 2 + j, :],
                                                   ALU.mult, ALU.add).then_inc(VE4.done(f"x{j}"), 1)
                dve.wait_ge(*VE4.after("x1", p))

            with dve.Fori(0, NPAIR - 1) as p:
                scan_vector(p, p + 1)
            scan_vector(NPAIR - 1, None)
            def ffn_vector(p, nxt):
                if nxt is not None:
                    norm_ffn(nxt)
                for n in range(3):
                    dve.wait_ge(*AC5.after(f"silu{n}", p))
                    dve.wait_ge(*PE5.after(f"u{n}", p))
                    nc.vector.tensor_tensor(h5[:, 2 * n:2 * n + 2, :], sg5[:, 2 * n:2 * n + 2, :], view(bank[3 + n], "p (c t) -> p c t", c=2),
                                            ALU.mult).then_inc(VE5.done(f"h{n}"), 1)
                dve.wait_ge(*PE5.after("down", p))
                xpair = x[:, bass.ds(p * 2, 2), :]
                nc.vector.scalar_tensor_tensor(xpair, view(bank[7], "p (a b) -> p a b", b=D), 1.0 / 127.0 ** 2, xpair,
                                               ALU.mult, ALU.add).then_inc(VE5.done("x"), 1)

            with dve.Fori(0, NPAIR - 1) as p:
                ffn_vector(p, p + 1)
            ffn_vector(NPAIR - 1, None)

        @block.tensor
        def _(pe):
            def mm(o, l, r, first=True, last=True):
                return nc.tensor.matmul(o, l, r, start=first, stop=last)

            pe.sem_inc(PEX.sem, PEX.round())
            pe.sem_inc(PEL.sem, PEL.round())
            pe.sem_inc(PEB.sem, PEB.round())
            pe.wait_ge(const_in, 16)
            pe.wait_ge(weights_q_in, 16 * 3)

            def transpose_norm(V, PEn, bk, rows, tag, ln, p):
                for j in range(2):
                    pe.wait_ge(*V.after(f"{ln}_norm{j}", p))
                    for k in range(2):
                        last = nc.tensor.transpose(bk[:, k * PW + j * P:k * PW + (j + 1) * P], rows[j][:, k * P:(k + 1) * P], ident)
                last.then_inc(PEn.done(tag), 1)

            def project_queries(p):
                pe.wait_ge(*ACX.after("xnT_A", p))
                for o in range(2):
                    for k in range(2):
                        last = mm(bank[1][:, o * PW:(o + 1) * PW], wq[:, k, o * P:(o + 1) * P], xnT_a[:, k, :], k == 0, k == 1)
                last.then_inc(PEX.done("q"), 1)

            def scores(p):
                pe.wait_ge(*ACX.after("q_bias1", p))
                for o, m in ((0, P), (1, DC2 + 1)):
                    for k in range(2):
                        last = mm(bank[2][0:m, o * PW:(o + 1) * PW], wk[:, k, o * P:o * P + m], qT[:, k, :], k == 0, k == 1)
                last.then_inc(PEX.done("qk"), 1)
                pe.wait_ge(*ACX.after("qk_evac1", p))
                pe.wait_ge(*setup.sem_value("ones_l1"))
                for j in range(2):
                    pe.wait_ge(ctx_in[j], (p + 1) * CTX1)
                    for b in range(BT):
                        mm(bank[SC[j]][S * b:S * b + S, 0:KEYS], qpT[:, 0, j * P + S * b:j * P + S * b + S],
                           cT1[j][:, b, :], True, False)
                    for b in range(BT):
                        last = mm(bank[SC[j]][S * b:S * b + S, 0:KEYS], qpT[0:DC2 + 1, 1, j * P + S * b:j * P + S * b + S],
                                  cT2[j][0:DC2 + 1, b, :], False, True)
                    last.then_inc(PEX.done(f"sc_{j}"), 1)

            def transpose_probabilities(p):
                for j in range(2):
                    pe.wait_ge(*ACX.after(f"exp{j}", p))
                    for c in range(2):
                        last = nc.tensor.transpose(bank[1][:, (j * 2 + c) * P:(j * 2 + c + 1) * P], pr[j][:, c * P:(c + 1) * P], ident)
                last.then_inc(PEX.done("pt"), 1)

            def context_sums(p):
                pe.wait_ge(*VEX.after("pT_evac", p))
                for j in range(2):
                    for c in range(2):
                        for b in range(BT):
                            last = mm(bank[OV[j]][S * b:S * b + S, 0:DC + 1], pT[:, j, c, S * b:S * b + S],
                                      cN[j][:, b, c, :], c == 0, c == 1)
                    last.then_inc(PEX.done(f"ov_{j}"), 1)

            def transpose_sums(p):
                for j in range(2):
                    pe.wait_ge(*VEX.after(f"ov_evac{j}", p))
                    nc.tensor.transpose(bank[OT[j]][:, 0:P], op[j][:, 0:P], ident)
                    last = nc.tensor.transpose(bank[OT[j]][0:DC2 + 1, P:2 * P], op[j][:, P:DC + 1], ident)
                    last.then_inc(PEX.done(f"ot_{j}"), 1)

            def project_values(p):
                pe.wait_ge(weights1_in, 16 * 5)
                for j in range(2):
                    pe.wait_ge(*ACX.after(f"oT_evac1_{j}", p))
                    mm(bank[WV[j]][:, 0:D], oT[j][:, 0, :], wv1, True, False)
                    mm(bank[WV[j]][:, 0:D], oT[j][0:DC2 + 1, 1, :], wv2[0:DC2 + 1, :], False, True)\
                        .then_inc(PEX.done(f"wv_{j}"), 1)

            def router_logits(tiles):
                for t in tiles:
                    for k in range(2):
                        last = mm(bank[5][:, t * E:(t + 1) * E], xnT_all[:, k, t * P:(t + 1) * P], wr[:, k, :], k == 0, k == 1)
                return last

            def shared_up(s):
                n, c = s // 4, s % 4
                if s >= 2:
                    pe.wait_ge(*SHV.sem_value(f"h{s - 2}"))
                for w, o in ((sg_w, 0), (su_w, 1)):
                    for k in range(2):
                        last = mm(bank[2 * (s % 2) + o], w[:, k, c * P:(c + 1) * P], xnT_all[:, k, n * 512:(n + 1) * 512], k == 0, k == 1)
                last.then_inc(SHP.done(f"gu{s}"), 1)

            def linear_tensor(p, nxt):
                pe.wait_ge(*ACB.after("xnT_B", p))
                for j in range(2):
                    for k in range(2):
                        last = mm(bank[5 + j], xnT_x[:, k, j * P:(j + 1) * P], wqkv[:, k, 0:2 * D], k == 0, k == 1)
                    last.then_inc(PEL.done(f"qk_{j}"), 1)
                if nxt is not None:
                    transpose_norm(VEX, PEX, bank[0], xnx, "trA", "lnA", nxt)
                for j in range(2):
                    for k in range(2):
                        last = mm(bank[7][:, j * D:(j + 1) * D], xnT_x[:, k, j * P:(j + 1) * P], wqkv[:, k, 2 * D:3 * D], k == 0, k == 1)
                last.then_inc(PEL.done("v"), 1)
                if nxt is None:
                    pe.wait_ge(weights_sh, 48)
                    pe.wait_ge(*GPL.after("xnT_all", NPAIR // 2 - 1))
                    shared_up(0)
                    shared_up(1)
                else:
                    project_queries(nxt)
                    scores(nxt)
                pe.wait_ge(*VEL.after("unit1", p))
                for j in range(2):
                    pe.wait_ge(*ACL.after(f"softplus{j}", p))
                    for hf in range(2):
                        last = nc.tensor.transpose(bank[4][:, (2 * j + hf) * P:(2 * j + hf + 1) * P], fqk[j][:, hf * P:(hf + 1) * P], ident)
                last.then_inc(PEL.done("qt"), 1)
                for j in range(2):
                    for hf in range(2):
                        if j == 1:
                            pe.wait_ge(*(ACL.after("qt_evac", p) if hf == 0 else VEL.after("kv_evac0_0", p)))
                        mm(bank[KV[j][hf]], fqk[j][:, D + hf * P:D + (hf + 1) * P],
                           view(vblk[j][:, hf, :, :], "p a b -> p (a b)")).then_inc(PEL.done(f"kv_{j}_{hf}"), 1)
                    if j == 0:
                        pe.wait_ge(*ACL.after(f"vblk1_{BT - 1}", p))
                        for i in range(2):
                            last = mm(bank[7][:, i * D:(i + 1) * D], K["same"], fqk[i][:, D:2 * D])
                        last.then_inc(PEL.done("ks"), 1)
                        if nxt is not None:
                            transpose_probabilities(nxt)
                if nxt is not None:
                    context_sums(nxt)
                for j in range(2):
                    pe.wait_ge(*VEL.after(f"kv_evac{j}_1", p))
                    for hf in range(2):
                        for b in range(BT):
                            last = mm(bank[6][S * b:S * b + S, j * D + hf * P:j * D + (hf + 1) * P], qtT[:, j, hf, S * b:S * b + S],
                                      kvm[j][:, hf, b, :])
                last.then_inc(PEL.done("at"), 1)
                if nxt is not None:
                    transpose_sums(nxt)
                if nxt is not None:
                    project_values(nxt)
                if nxt is not None:
                    transpose_norm(VEB, PEB, bank[6], xnx, "trB", "lnB", nxt)
                else:
                    pe.wait_ge(*GPL.after("xnT_all", p - 1))
                    router_logits(range(NT - 2))
                transpose_norm(VEL, PEL, bank[4], xn, "trC", "lnC", p)

            transpose_norm(VEX, PEX, bank[0], xnx, "trA", "lnA", 0)
            project_queries(0)
            scores(0)
            transpose_probabilities(0)
            context_sums(0)
            transpose_sums(0)
            project_values(0)
            transpose_norm(VEB, PEB, bank[6], xnx, "trB", "lnB", 0)
            with pe.Fori(0, NPAIR - 1) as p:
                linear_tensor(p, p + 1)
            linear_tensor(NPAIR - 1, None)
            def shared_down(t):
                if t >= 2:
                    pe.wait_ge(*SHV.sem_value(f"x{t - 2}"))
                for c in range(4):
                    last = mm(bank[4 + t % 2][:, 0:D], hs[:, c, t * P:(t + 1) * P], sd_w[:, c, :], c == 0, c == 3)
                last.then_inc(SHP.done(f"down{t}"), 1)

            shared_up(2)
            pe.wait_ge(*GPL.all(NPAIR))
            pe.wait_ge(*VEX.all(NPAIR))
            pe.wait_ge(*VEL.all(NPAIR))
            router_logits(range(NT - 2, NT)).then_inc(SHP.done("lg"), 1)
            shared_up(3)
            pe.wait_ge(*RT.sem_value("onehot"))
            oneh_all = view(oneh, "p a b -> p (a b)")
            mm(bank[6][:, 0:NT * E], K["before"], oneh_all, True, False)
            for t in range(1, NT):
                last = mm(bank[6][:, t * E:NT * E], K["ones"], oneh_all[:, 0:(NT - t) * E], False, t == NT - 1)
            last.then_inc(SHP.done("rank"), 1)
            for t in range(NT):
                last = mm(bank[7][:, 0:E], K["ones"], oneh[:, t, :], t == 0, t == NT - 1)
            last.then_inc(SHP.done("count"), 1)
            for s in range(4, 8):
                shared_up(s)
            for t in range(2):
                shared_down(t)
            pe.wait_ge(*SHV.sem_value("x1"))
            pe.sem_inc(PE2.sem, PE2.round())
            pe.wait_ge(*SHV.sem_value("h7"))

            def expert_transpose(PEx, s, h, r):
                for k in range(2):
                    last = nc.tensor.transpose(bank[6 + h][:, k * P:(k + 1) * P], xg[r][:, k * P:(k + 1) * P], ident)
                last.then_inc(PEx.done("xt" + s), 1)

            def expert_up(PEx, ACx, s, i, h, r):
                pe.wait_ge(*ACx.after("xT" + s, i))
                for o in range(2):
                    for c in range(4):
                        for k in range(2):
                            last = mm(bank[2 * h + o][:, c * P:(c + 1) * P], ring_gu[r][:, k, o * F0 + c * P:o * F0 + (c + 1) * P],
                                      xgT[h][:, k, :], k == 0, k == 1)
                last.then_inc(PEx.done("gu" + s), 1)

            def expert_down(PEx, VEx, s, i, h, r):
                pe.wait_ge(*VEx.after("h" + s, i))
                for c in range(4):
                    last = mm(bank[4 + h][:, 0:D], eh[h][:, c, :], ring_dn[r][:, c, :], c == 0, c == 3)
                last.then_inc(PEx.done("dn" + s), 1)

            with pe.Fori(0, NR) as it:
                pe.wait_ge(xg_in[0], it * 16 + 16)
                expert_transpose(PE2, "0", 0, 0)
                for r in range(RING):
                    pe.wait_ge(gu_in[r], it * 16 + 16)
                    expert_up(PE2, AC2, str(r), it, r % 2, r)
                    if r + 1 < RING:
                        pe.wait_ge(xg_in[r + 1], it * 16 + 16)
                        expert_transpose(PE2, str(r + 1), (r + 1) % 2, r + 1)
                    if r >= 1:
                        q = r - 1
                        pe.wait_ge(dn_in[q], it * 16 + 16)
                        pe.wait_ge(*VE2.after(f"y{q - 2}", it) if q >= 2 else VE2.after(f"y{q + 2}", it - 1))
                        expert_down(PE2, VE2, str(q), it, q % 2, q)
                q = RING - 1
                pe.wait_ge(dn_in[q], it * 16 + 16)
                pe.wait_ge(*VE2.after(f"y{q - 2}", it))
                expert_down(PE2, VE2, str(q), it, q % 2, q)
            n_over = pe.value_load(etab.bitcast(i32)[0:1, NOVF:NOVF + 1], min_val=0, max_val=NOVF)
            with pe.If(n_over > 0):
                pe.sem_inc(PEO.sem, PEO.round())
                pe.wait_ge(*VE2.all(NR))
                with pe.Fori(0, NOVF) as i:
                    pe.wait_ge(ovf_in, i * 48 + 48)
                    pe.wait_ge(*VEO.after("y", i - 1))
                    expert_transpose(PEO, "", 0, 0)
                    expert_up(PEO, ACO, "", i, 0, 0)
                    expert_down(PEO, VEO, "", i, 0, 0)
                pe.wait_ge(*VEO.all(NOVF))
            pe.wait_ge(*VE2.all(NR))
            for t in range(2, NT):
                shared_down(t)
            pe.wait_ge(weights3_in, 16 * 7)
            pe.sem_inc(PE3.sem, PE3.round())
            pe.sem_inc(PT3.sem, PT3.round())
            pe.sem_inc(PT5.sem, PT5.round())
            pe.sem_inc(PE4.sem, PE4.round())
            pe.sem_inc(PE5.sem, PE5.round())
            pe.wait_ge(*set3.sem_value("row_zero"))
            def attn1_tensor(p, nxt):
                pe.wait_ge(*AT3.after("xnT", p))
                for n in range(2):
                    for o in range(2 * n, 2 * n + 2):
                        for k in range(2):
                            last = mm(bank[2 + n][:, (o % 2) * PW:(o % 2 + 1) * PW], c_wq[:, k, o * P:(o + 1) * P], xnT3[:, k, :], k == 0, k == 1)
                    last.then_inc(PE3.done(f"q{n}"), 1)
                for h in range(H1):
                    pe.wait_ge(*AC3.after(f"q_evac{h // 4}", p))
                    if h == 0:
                        pe.wait_ge(*XE.sem_value("x7"))
                    if h >= 4:
                        pe.wait_ge(*VE3.after(f"qk_evac{h - 4}", p))
                    elif h < 2:
                        pe.wait_ge(*VE3.after(f"bias{h}", p - 1))
                    else:
                        pe.wait_ge(*VE3.after(f"opT_evac{NU - 4 + h}", p - 1))
                    mm(bank[4 + h % 4][:, 0:PW], c_wk[:, h, 0:P], q3[:, h // 2, :])
                    mm(bank[4 + h % 4][0:DC2, PW:2 * PW], c_wk[:, h, P:DC], q3[:, h // 2, :]).then_inc(PE3.done(f"qk{h}"), 1)
                pe.wait_ge(*AC3.after("o_evac1", p - 1))
                pe.wait_ge(*VE3.after("qk_evac7", p))
                for s in range(NU + 4):
                    if s < NU:
                        b, g = s // 2, s % 2
                        j = b // BT
                        if s % (NU // 2) == 0:
                            pe.wait_ge(ctx_in[j], (p + 1) * CTX3 + NPAIR * CTX1)
                        if s >= 2:
                            pe.wait_ge(*AC3.after(f"exp{s - 2}", p))
                        mm(bank[s % 2][:, 0:KEYS], qp3[:, 0, b, g * P:(g + 1) * P], cT1[j][:, b % BT, :], True, False)
                        mm(bank[s % 2][:, 0:KEYS], qp3[0:DC2 + 2, 1, b, g * P:(g + 1) * P], cT2[j][0:DC2 + 2, b % BT, :], False, True)\
                            .then_inc(PE3.done(f"sc{s}"), 1)
                    if 2 <= s < NU + 2:
                        u = s - 2
                        pe.wait_ge(*VE3.after(f"norm{u}", p))
                        if u >= 2:
                            pe.wait_ge(*AC3.after(f"pT_evac{u - 2}", p))
                        for c in range(2):
                            last = nc.tensor.transpose(bank[2 + u % 2][:, c * P:(c + 1) * P], pr3[u % 4][:, c * P:(c + 1) * P], ident)
                        last.then_inc(PE3.done(f"pt{u}"), 1)
                    if 3 <= s < NU + 3:
                        u = s - 3
                        b = u // 2
                        pe.wait_ge(*AC3.after(f"pT_evac{u}", p))
                        if u >= 2:
                            pe.wait_ge(*VE3.after(f"ov_evac{u - 2}", p))
                        for c in range(2):
                            last = mm(bank[4 + u % 2][:, 0:DC], pT3[u % 2][:, c, :], cN[b // BT][:, b % BT, c, 0:DC], c == 0, c == 1)
                        last.then_inc(PE3.done(f"ov{u}"), 1)
                    if s >= 4:
                        u = s - 4
                        pe.wait_ge(*VE3.after(f"ov_evac{u}", p))
                        if u >= 2:
                            pe.wait_ge(*VE3.after(f"opT_evac{u - 2}", p))
                        for c in range(2):
                            last = nc.tensor.transpose(bank[6 + u % 2][:, c * P:(c + 1) * P], op3[u % 2][:, c * P:(c + 1) * P], ident)
                        last.then_inc(PE3.done(f"opT{u}"), 1)
                pe.wait_ge(*VE3.after(f"opT_evac{NU - 1}", p))
                pe.wait_ge(*AC3.after(f"exp{NU - 1}", p))
                for c in range(4):
                    for k, rows in ((0, P), (1, DC2)):
                        for e in range(2):
                            h = 2 * c + e
                            last = mm(bank[c // 2][e * HD1:(e + 1) * HD1, (c % 2) * PW:(c % 2 + 1) * PW],
                                      c_wv[0:rows, k, h * HD1:(h + 1) * HD1], oT3[0:rows, :, k, h, :], k == 0, k == 1)
                    if c % 2:
                        last.then_inc(PE3.done(f"o{c // 2}"), 1)
                pe.wait_ge(*AC3.after("o_evac0", p))
                if nxt is not None:
                    transpose_norm(VN3, PT3, bank[0], xn3, "tr", "ln", nxt)
                pe.wait_ge(*AC3.after("o_evac1", p))
                for j in range(2):
                    for c in range(4):
                        last = mm(bank[4 + j][:, 0:D], o3T[:, c, j * P:(j + 1) * P], c_wo[:, c, :], c == 0, c == 3)
                    last.then_inc(PE3.done(f"wo{j}"), 1)

            transpose_norm(VN3, PT3, bank[0], xn3, "tr", "ln", 0)
            with pe.Fori(0, NPAIR - 1) as p:
                attn1_tensor(p, p + 1)
            attn1_tensor(NPAIR - 1, None)
            pe.wait_ge(weights4_in, 16 * 10)
            pe.wait_ge(*set4.sem_value("A"))
            ZC, XC, DTC = 0, DIN, 2 * DIN + 2 * NST
            with pe.Fori(0, NPAIR) as p:
                pe.wait_ge(*VN4.after("u", p))
                pe.wait_ge(*AC4.after("decay1", p - 1))
                for j in range(2):
                    for k in range(2):
                        last = nc.tensor.transpose(bank[0][:, k * PW + j * P:k * PW + (j + 1) * P], u4[:, j, k * P:(k + 1) * P], ident)
                last.then_inc(PE4.done("tr"), 1)
                pe.wait_ge(*AC4.after("uT", p))
                pe.wait_ge(*VE4.after("x1", p - 1))
                for j in range(2):
                    for k in range(2):
                        last = mm(bank[6][:, j * HM:(j + 1) * HM], uT4[:, k, j * P:(j + 1) * P], m_in[:, k, DTC:DTC + HM], k == 0, k == 1)
                last.then_inc(PE4.done("dt"), 1)
                pe.wait_ge(*AC4.after("yT_evac1", p - 1))
                for n in (2, 0, 1):
                    for c in range(2):
                        for k in range(2):
                            last = mm(bank[1 + n][:, c * PW:(c + 1) * PW], m_in[:, k, XC + (2 * n + c) * P:XC + (2 * n + c + 1) * P],
                                      uT4[:, k, :], k == 0, k == 1)
                    last.then_inc(PE4.done(f"xbc{n}"), 1)
                pe.wait_ge(*VE4.after("dtA", p))
                for j in range(2):
                    last = mm(bank[6][:, (2 + j) * HM:(3 + j) * HM], K["tri"], dts["dtA"][:, j, :])
                last.then_inc(PE4.done("cum"), 1)

                def cum_rows(j):
                    for h in range(HM):
                        last = mm(bank[(3, 0)[h // 4]][:, (h % 4) * P:(h % 4 + 1) * P],
                                  dts["dtA"][:, j, h:h + 1].broadcast_to((P, P)), K["tri"])
                    last.then_inc(PE4.done(f"cumT{j}"), 1)

                pe.wait_ge(*AC4.after("tap3_5", p))
                cum_rows(0)
                for j in range(2):
                    for k in range(2):
                        last = mm(bank[4 + j], uT4[:, k, j * P:(j + 1) * P], m_in[:, k, ZC:ZC + DIN], k == 0, k == 1)
                    last.then_inc(PE4.done(f"z{j}"), 1)
                pe.wait_ge(*VE4.after("silu2", p))
                for j in range(2):
                    mm(bank[7][:, j * P:(j + 1) * P], cv[:, 4, j * P:(j + 1) * P], cv[:, 5, j * P:(j + 1) * P]).then_inc(PE4.done(f"G{j}"), 1)
                pe.wait_ge(*AC4.after("relu0_7", p))
                cum_rows(1)
                pe.wait_ge(*VE4.after("silu1", p))
                for j in range(2):
                    for c in range(4):
                        last = nc.tensor.transpose(bank[1 + j][:, c * P:(c + 1) * P], cv[:, c, j * P:(j + 1) * P], ident)
                    last.then_inc(PE4.done(f"xs{j}"), 1)
                for j in range(2):
                    pe.wait_ge(*VE4.after(f"M{j}", p))
                    pe.wait_ge(*VE4.after(f"xdt{j}", p))
                    pe.wait_ge(*VE4.after(f"z_silu{j}", p))
                    for h in range(HM):
                        last = mm(bank[4 + j][:, h * HDM:(h + 1) * HDM], dec[j][:, h, :], xdt[j][:, h * HDM:(h + 1) * HDM])
                    last.then_inc(PE4.done(f"y{j}"), 1)
                for j in range(2):
                    pe.wait_ge(*VE4.after(f"yz{j}", p))
                    for c in range(4):
                        last = nc.tensor.transpose(bank[1 + j][:, c * P:(c + 1) * P], y4[j][:, c * P:(c + 1) * P], ident)
                    last.then_inc(PE4.done(f"yT{j}"), 1)
                for j in range(2):
                    pe.wait_ge(*AC4.after(f"yT_evac{j}", p))
                    for c in range(4):
                        last = mm(bank[6 + j][:, 0:D], yT4[j][:, c, :], m_out[:, c, :], c == 0, c == 3)
                    last.then_inc(PE4.done(f"out{j}"), 1)
            pe.wait_ge(*VE4.all(NPAIR))
            pe.wait_ge(*ints.sem_value("int2"))
            def ffn_tensor(p, nxt):
                pe.wait_ge(*AT5.after("xnT", p))
                for n in range(3):
                    pe.wait_ge(*VE5.after(f"h{n}", p - 1))
                    for w, o, tag in ((f_g, 0, "g"), (f_u, 3, "u")):
                        for c in (2 * n, 2 * n + 1):
                            for k in range(2):
                                last = mm(bank[o + n][:, (c % 2) * PW:(c % 2 + 1) * PW], w[:, k, c * P:(c + 1) * P], xnT5[:, k, :], k == 0, k == 1)
                        last.then_inc(PE5.done(f"{tag}{n}"), 1)
                if nxt is not None:
                    transpose_norm(VN5, PT5, bank[6], xn5, "tr", "ln", nxt)
                pe.wait_ge(*VE5.after("x", p - 1))
                for j in range(2):
                    for c in range(6):
                        if c % 2 == 0:
                            pe.wait_ge(*VE5.after(f"h{c // 2}", p))
                        last = mm(bank[7][:, j * D:(j + 1) * D], h5[:, c, j * P:(j + 1) * P], f_d[:, c, :], c == 0, c == 5)
                last.then_inc(PE5.done("down"), 1)

            transpose_norm(VN5, PT5, bank[6], xn5, "tr", "ln", 0)
            with pe.Fori(0, NPAIR - 1) as p:
                ffn_tensor(p, p + 1)
            ffn_tensor(NPAIR - 1, None)

        return high[0], all_steps


SBUF_COLS = 53200


def layouts(a):
    T = lambda w: np.ascontiguousarray(np.asarray(w).T)
    ctx = a["ctx_768"]
    first = ctx[:, :2 * P, :].reshape(NT, BT, 2, P, DC)
    return {
        "consts": host_constants()[0],
        "x": a["x"].reshape(TOK, D),
        "ctx_T": np.ascontiguousarray(ctx.reshape(NT, BT, KEYS, DC).transpose(0, 3, 1, 2)),
        "ctx_N": np.ascontiguousarray(first.transpose(0, 3, 1, 2, 4)).reshape(NT, P, 2 * BT, DC),
        "ctx_last": np.ascontiguousarray(ctx[:, KEYS - 1, :]),
        "mask": a["mask_BxS2_bk0"],
        "wq": T(a["L0_xattn_Wq"]), "bq": T(a["L0_xattn_bq"].reshape(2, P)),
        "wk": np.concatenate([a["L0_xattn_Wk"], a["L0_xattn_bk"][:, None]], 1),
        "wv": np.concatenate([T(a["L0_xattn_Wv"]), a["L0_xattn_bv"][None, :]], 0),
        "wqkv": T(a["L0_attn_W_qkv"]), "wr": T(a["L0_ffn_w_router"]),
        "s_g": T(a["L0_ffn_w_gate"]), "s_u": T(a["L0_ffn_w_up"]), "s_d": T(a["L0_ffn_w_down"]),
        "c_wq": a["L1_xattn_W_q"], "c_wk": T(a["L1_xattn_W_k"]), "c_wv": a["L1_xattn_W_v"], "c_wo": a["L1_xattn_W_o"],
        "c_bo": a["L1_xattn_b_o"],
        "m_in": T(a["L1_attn_in_proj_w"]), "m_out": T(a["L1_attn_out_proj_w"]), "m_lnw": a["L1_attn_ln_w"],
        "m_lnb": a["L1_attn_ln_b"], "m_D": a["L1_attn_D"], "m_dtb": a["L1_attn_dt_bias"], "m_A": a["L1_attn_A_log"],
        "m_conv": a["L1_attn_conv_w"], "m_cb": T(a["L1_attn_conv_b"].reshape(NCH, P)), "m_nw": T(a["L1_attn_norm_w"].reshape(4, P)),
        "f_g": T(a["L1_ffn_w_gate"]), "f_u": T(a["L1_ffn_w_up"]), "f_d": T(a["L1_ffn_w_down"]),
        "e_gu": a["L0_ffn_gate_up_proj"], "e_dn": a["L0_ffn_down_proj"],
    }


def build(nc, arrays):
    I = {k: nc.dram_tensor("in_" + k, v.shape, mybir.dt.from_np(v.dtype), kind="ExternalInput").ap() for k, v in arrays.items()}
    out = nc.dram_tensor("out_x", (TOK, D), mybir.dt.float32, kind="ExternalOutput").ap()
    return perceiver_kernel(nc, I, out)


def kernel(**inputs):
    import concourse.bacc as bacc
    from concourse.bass_utils import run_bass_kernel_spmd

    arrays = layouts({k: np.asarray(v) for k, v in inputs.items()})
    nc = bacc.Bacc("TRN2", target_bir_lowering=False, num_devices=1)
    build(nc, arrays)
    r = run_bass_kernel_spmd(nc, [{"in_" + k: v for k, v in arrays.items()}], core_ids=[0])
    return r.results[0]["out_x"].reshape(B, S, D)
```
